# Optimizing a Trainium2 kernel written in Bass

```python
import numpy as np
import jax
import jax.numpy as jnp

def _softmax(x, axis=-1):
    return jax.nn.softmax(x, axis=axis)

def _gelu(x):
    return jax.nn.gelu(x, approximate=True)

def _silu(x):
    return jax.nn.silu(x)

def _sigmoid(x):
    return jax.nn.sigmoid(x)

def _layernorm(x, axis=-1, eps=1e-05):
    m = jnp.mean(x, axis=axis, keepdims=True)
    v = jnp.var(x, axis=axis, keepdims=True)
    return (x - m) / jnp.sqrt(v + eps)

def _scatter_add(tgt, idx, src, axis=0):
    return tgt.at[idx].add(src)

def _segment_sum(src, seg, n):
    return jax.ops.segment_sum(src, seg, n)
kernel_name = 'mk_prb_d2_jaxref_r8_63f836'

def setup_inputs(seed: int=0):
    np.random.seed(seed)
    _w = jnp.asarray

    def _L0_attn_setup():
        import jax, jax.numpy as jnp
        import numpy as np
        N_HEAD = 16
        EPS = 1e-06

        def _rotate_half(x):
            d = x.shape[-1] // 2
            return jnp.concatenate((-x[..., d:], x[..., :d]), axis=-1)

        def _rms_norm(x, w, eps=EPS):
            d = x.shape[-1]
            rms = jnp.linalg.norm(x, axis=-1, keepdims=True) * d ** (-0.5)
            return w * (x / (rms + eps))
        key = jax.random.key(seed)
        ks = jax.random.split(key, 3)
        B, T, C = (4, 256, 128)
        x = jax.random.normal(ks[0], (B, T, C), dtype=jnp.float32)
        W_kqv = jax.random.normal(ks[1], (3 * C, C), dtype=jnp.float32) * C ** (-0.5)
        W_proj = jax.random.normal(ks[2], (C, C), dtype=jnp.float32) * C ** (-0.5)
        D = C // N_HEAD
        q_norm_w = jnp.ones((D,), dtype=jnp.float32)
        k_norm_w = jnp.ones((D,), dtype=jnp.float32)
        return {'x': x, 'W_kqv': W_kqv, 'W_proj': W_proj, 'q_norm_w': q_norm_w, 'k_norm_w': k_norm_w}
    _L0_attn_in = _L0_attn_setup()

    def _L0_ffn_setup():
        import jax, jax.numpy as jnp
        import numpy as np
        B, S, D, FF, E, L = (8, 256, 128, 512, 16, 4)

        def _unipool_layer(xt, router, W1, W2):
            logits = xt @ router
            probs = jax.nn.softmax(logits, axis=-1)
            w = jnp.max(probs, axis=-1)
            idx = jnp.argmax(probs, axis=-1)

            def body(acc, params):
                w1, w2, i = params
                h = jax.nn.silu(xt @ w1) @ w2
                sel = jnp.where(idx == i, w, 0.0)
                return (acc + sel[:, None] * h, None)
            out, _ = jax.lax.scan(body, jnp.zeros_like(xt), (W1, W2, jnp.arange(W1.shape[0])))
            return out
        key = jax.random.key(seed)
        k0, k1, k2, k3 = jax.random.split(key, 4)
        x = jax.random.normal(k0, (B, S, D), dtype=jnp.float32)
        routers = jax.random.normal(k1, (L, D, E), dtype=jnp.float32) * 0.02
        W1 = jax.random.normal(k2, (E, D, FF), dtype=jnp.float32) * 0.02
        W2 = jax.random.normal(k3, (E, FF, D), dtype=jnp.float32) * 0.02
        return {'x': x, 'routers': routers, 'W1': W1, 'W2': W2}
    _L0_ffn_in = _L0_ffn_setup()

    def _L1_attn_setup():
        import jax, jax.numpy as jnp
        import numpy as np
        import math
        D = 128
        H = 16
        HEAD_D = D // H
        T = 256
        B = 4
        key = jax.random.key(seed)
        k1, k2, k3 = jax.random.split(key, 3)
        x = jax.random.normal(k1, (B, T, D), dtype=jnp.float32)
        w_attn = jax.random.normal(k2, (D, D + 2 * HEAD_D), dtype=jnp.float32) * (1.0 / math.sqrt(D))
        w_proj = jax.random.normal(k3, (D, D), dtype=jnp.float32) * (1.0 / math.sqrt(D))
        return {'x': x, 'w_attn': w_attn, 'w_proj': w_proj}
    _L1_attn_in = _L1_attn_setup()

    def _L1_ffn_setup():
        import jax, jax.numpy as jnp
        import numpy as np
        DIM = 128
        HEADS = 16
        HD = DIM // HEADS
        M = 32
        E = 4
        K = 2
        HID = 256
        MID = 256
        LB = 0.01
        EPS = 1.1920929e-07

        def _rms(x, w):
            return x * jax.lax.rsqrt(jnp.mean(x * x, axis=-1, keepdims=True) + EPS) * w

        def _gelu(x):
            return jax.nn.gelu(x, approximate=False)
        key = jax.random.key(seed)
        ks = jax.random.split(key, 20)
        d = DIM
        w = lambda k, s: jax.random.normal(k, s, jnp.float32) * 0.02
        return {'x': jax.random.normal(ks[0], (4, 128, d), jnp.float32), 'n1_w': jnp.ones((d,), jnp.float32), 'n2_w': jnp.ones((d,), jnp.float32), 'wq': w(ks[1], (d, d)), 'wk': w(ks[2], (d, d)), 'wv': w(ks[3], (d, d)), 'wo': w(ks[4], (d, d)), 'qn_w': jnp.ones((HD,), jnp.float32), 'kn_w': jnp.ones((HD,), jnp.float32), 'gate_w': w(ks[5], (E, d)), 'e0_up': w(ks[6], (HID, d)), 'e0_down': w(ks[7], (d, HID)), 'e1_w1': w(ks[8], (HID, d)), 'e1_w2': w(ks[9], (HID, d)), 'e1_down': w(ks[10], (d, HID)), 'e2_l1': w(ks[11], (MID, d)), 'e2_l2': w(ks[12], (HID, MID)), 'e2_l3': w(ks[13], (MID, HID)), 'e2_l4': w(ks[14], (d, MID)), 'e3_down': w(ks[15], (d, d)), 'e3_up': w(ks[16], (HID, d)), 'e3_out': w(ks[17], (d, HID))}
    _L1_ffn_in = _L1_ffn_setup()
    _d = {'L0_attn_x': _L0_attn_in['x'], 'L0_attn_W_kqv': _L0_attn_in['W_kqv'], 'L0_attn_W_proj': _L0_attn_in['W_proj'], 'L0_attn_q_norm_w': _L0_attn_in['q_norm_w'], 'L0_attn_k_norm_w': _L0_attn_in['k_norm_w'], 'L0_ffn_routers': _L0_ffn_in['routers'], 'L0_ffn_W1': _L0_ffn_in['W1'], 'L0_ffn_W2': _L0_ffn_in['W2'], 'L1_attn_w_attn': _L1_attn_in['w_attn'], 'L1_attn_w_proj': _L1_attn_in['w_proj'], 'L1_ffn_n1_w': _L1_ffn_in['n1_w'], 'L1_ffn_n2_w': _L1_ffn_in['n2_w'], 'L1_ffn_wq': _L1_ffn_in['wq'], 'L1_ffn_wk': _L1_ffn_in['wk'], 'L1_ffn_wv': _L1_ffn_in['wv'], 'L1_ffn_wo': _L1_ffn_in['wo'], 'L1_ffn_qn_w': _L1_ffn_in['qn_w'], 'L1_ffn_kn_w': _L1_ffn_in['kn_w'], 'L1_ffn_gate_w': _L1_ffn_in['gate_w'], 'L1_ffn_e0_up': _L1_ffn_in['e0_up'], 'L1_ffn_e0_down': _L1_ffn_in['e0_down'], 'L1_ffn_e1_w1': _L1_ffn_in['e1_w1'], 'L1_ffn_e1_w2': _L1_ffn_in['e1_w2'], 'L1_ffn_e1_down': _L1_ffn_in['e1_down'], 'L1_ffn_e2_l1': _L1_ffn_in['e2_l1'], 'L1_ffn_e2_l2': _L1_ffn_in['e2_l2'], 'L1_ffn_e2_l3': _L1_ffn_in['e2_l3'], 'L1_ffn_e2_l4': _L1_ffn_in['e2_l4'], 'L1_ffn_e3_down': _L1_ffn_in['e3_down'], 'L1_ffn_e3_up': _L1_ffn_in['e3_up'], 'L1_ffn_e3_out': _L1_ffn_in['e3_out']}
    _x0 = _d['L0_attn_x']
    _d['L0_attn_x'] = jax.random.normal(jax.random.fold_in(jax.random.key(seed), 1), (1, 2048, 128), dtype=_x0.dtype)
    del _x0
    return _d

def reference(L0_attn_x, L0_attn_W_kqv, L0_attn_W_proj, L0_attn_q_norm_w, L0_attn_k_norm_w, L0_ffn_routers, L0_ffn_W1, L0_ffn_W2, L1_attn_w_attn, L1_attn_w_proj, L1_ffn_n1_w, L1_ffn_n2_w, L1_ffn_wq, L1_ffn_wk, L1_ffn_wv, L1_ffn_wo, L1_ffn_qn_w, L1_ffn_kn_w, L1_ffn_gate_w, L1_ffn_e0_up, L1_ffn_e0_down, L1_ffn_e1_w1, L1_ffn_e1_w2, L1_ffn_e1_down, L1_ffn_e2_l1, L1_ffn_e2_l2, L1_ffn_e2_l3, L1_ffn_e2_l4, L1_ffn_e3_down, L1_ffn_e3_up, L1_ffn_e3_out):

    def _L0_attn_ref(x, W_kqv, W_proj, q_norm_w, k_norm_w):
        import jax, jax.numpy as jnp
        import numpy as np
        N_HEAD = 16
        EPS = 1e-06

        def _rotate_half(x):
            d = x.shape[-1] // 2
            return jnp.concatenate((-x[..., d:], x[..., :d]), axis=-1)

        def _rms_norm(x, w, eps=EPS):
            d = x.shape[-1]
            rms = jnp.linalg.norm(x, axis=-1, keepdims=True) * d ** (-0.5)
            return w * (x / (rms + eps))
        B, T, C = x.shape
        H = N_HEAD
        D = C // H
        kqv = x @ W_kqv.T
        k, q, v = jnp.split(kqv, 3, axis=2)

        def to_heads(t):
            return t.reshape(B, T, H, D).transpose(0, 2, 1, 3)
        k, q, v = (to_heads(k), to_heads(q), to_heads(v))
        inv_freq = 1.0 / 10000.0 ** (jnp.arange(0, D, 2, dtype=jnp.float32) / D)
        t_pos = jnp.arange(T, dtype=jnp.float32)
        freqs = t_pos[:, None] * inv_freq[None, :]
        freqs = jnp.concatenate((freqs, freqs), axis=-1)
        cos = jnp.cos(freqs)[None, None]
        sin = jnp.sin(freqs)[None, None]
        q = q * cos + _rotate_half(q) * sin
        k = k * cos + _rotate_half(k) * sin
        q = _rms_norm(q, q_norm_w)
        k = _rms_norm(k, k_norm_w)
        scores = jnp.einsum('bhtd,bhsd->bhts', q, k) / jnp.sqrt(jnp.float32(D))
        causal = jnp.triu(jnp.ones((T, T), dtype=bool), k=1)
        scores = jnp.where(causal[None, None], -jnp.inf, scores)
        att = jax.nn.softmax(scores, axis=-1)
        y = jnp.einsum('bhts,bhsd->bhtd', att, v)
        y = y.transpose(0, 2, 1, 3).reshape(B, T, C)
        return y @ W_proj.T

    def _L0_ffn_ref(x, routers, W1, W2):
        import jax, jax.numpy as jnp
        import numpy as np
        B, S, D, FF, E, L = (8, 256, 128, 512, 16, 4)

        def _unipool_layer(xt, router, W1, W2):
            logits = xt @ router
            probs = jax.nn.softmax(logits, axis=-1)
            w = jnp.max(probs, axis=-1)
            idx = jnp.argmax(probs, axis=-1)

            def body(acc, params):
                w1, w2, i = params
                h = jax.nn.silu(xt @ w1) @ w2
                sel = jnp.where(idx == i, w, 0.0)
                return (acc + sel[:, None] * h, None)
            out, _ = jax.lax.scan(body, jnp.zeros_like(xt), (W1, W2, jnp.arange(W1.shape[0])))
            return out
        b, s, d = x.shape
        xt = x.reshape(-1, d)

        def step(carry, router):
            return (_unipool_layer(carry, router, W1, W2), None)
        xt, _ = jax.lax.scan(step, xt, routers)
        return xt.reshape(b, s, d)

    def _L1_attn_ref(x, w_attn, w_proj):
        import jax, jax.numpy as jnp
        import numpy as np
        import math
        D = 128
        H = 16
        HEAD_D = D // H
        T = 256
        B = 4
        Bv, Tv, _ = x.shape
        qkv = x @ w_attn
        q = qkv[..., :D].reshape(Bv, Tv, H, HEAD_D).transpose(0, 2, 1, 3)
        k = qkv[..., D:D + HEAD_D]
        v = qkv[..., D + HEAD_D:]
        scale = 1.0 / math.sqrt(HEAD_D)
        att = jnp.einsum('bhqd,bkd->bhqk', q, k) * scale
        causal = jnp.tril(jnp.ones((Tv, Tv), dtype=bool))
        att = jnp.where(causal[None, None, :, :], att, -jnp.inf)
        att = jax.nn.softmax(att, axis=-1)
        y = jnp.einsum('bhqk,bkd->bhqd', att, v)
        y = y.transpose(0, 2, 1, 3).reshape(Bv, Tv, D)
        return y @ w_proj

    def _L1_ffn_ref(x, n1_w, n2_w, wq, wk, wv, wo, qn_w, kn_w, gate_w, e0_up, e0_down, e1_w1, e1_w2, e1_down, e2_l1, e2_l2, e2_l3, e2_l4, e3_down, e3_up, e3_out):
        import jax, jax.numpy as jnp
        import numpy as np
        DIM = 128
        HEADS = 16
        HD = DIM // HEADS
        M = 32
        E = 4
        K = 2
        HID = 256
        MID = 256
        LB = 0.01
        EPS = 1.1920929e-07

        def _rms(x, w):
            return x * jax.lax.rsqrt(jnp.mean(x * x, axis=-1, keepdims=True) + EPS) * w

        def _gelu(x):
            return jax.nn.gelu(x, approximate=False)
        B, T, C = x.shape
        h = _rms(x, n1_w)
        heads = lambda w_: (h @ w_.T).reshape(B, T, HEADS, HD).transpose(0, 2, 1, 3)
        q = _rms(heads(wq), qn_w)
        k = _rms(heads(wk), kn_w)
        v = heads(wv)
        scores = jnp.einsum('bhqd,bhkd->bhqk', q, k) * HD ** (-0.5)
        causal = jnp.tril(jnp.ones((T, T), bool))
        scores = jnp.where(causal[None, None], scores, -jnp.inf)
        attn = jax.nn.softmax(scores, axis=-1)
        ao = jnp.einsum('bhqk,bhkd->bhqd', attn, v).transpose(0, 2, 1, 3).reshape(B, T, C) @ wo.T
        ao = ao.at[:, :, :M].set(0.0)
        x = x + ao
        xf = _rms(x, n2_w).reshape(-1, C)
        N = xf.shape[0]
        logits = jnp.nan_to_num(xf @ gate_w.T)
        probs = jax.nn.softmax(logits, axis=-1)
        topv, topi = jax.lax.top_k(probs, K)
        topv = topv / (topv.sum(-1, keepdims=True) + 1e-08)
        wts = jnp.zeros((N, E), x.dtype).at[jnp.arange(N)[:, None], topi].add(topv)
        o0 = _gelu(xf @ e0_up.T) @ e0_down.T
        o1 = jax.nn.silu(xf @ e1_w1.T) * (xf @ e1_w2.T) @ e1_down.T
        o2 = _gelu(_gelu(_gelu(xf @ e2_l1.T) @ e2_l2.T) @ e2_l3.T) @ e2_l4.T
        o3 = _gelu(_gelu(xf @ e3_down.T) @ e3_up.T) @ e3_out.T
        moe = wts[:, 0:1] * o0 + wts[:, 1:2] * o1 + wts[:, 2:3] * o2 + wts[:, 3:4] * o3
        moe = moe.reshape(B, T, C).at[:, :, :M].set(0.0)
        return x + moe
    x = L0_attn_x
    xn = _layernorm(x, axis=-1)
    x = x + _L0_attn_ref(xn, L0_attn_W_kqv, L0_attn_W_proj, L0_attn_q_norm_w, L0_attn_k_norm_w) + _L0_ffn_ref(xn, L0_ffn_routers, L0_ffn_W1, L0_ffn_W2)
    xn = _layernorm(x, axis=-1)
    x = x + _L1_attn_ref(xn, L1_attn_w_attn, L1_attn_w_proj) + _L1_ffn_ref(xn, L1_ffn_n1_w, L1_ffn_n2_w, L1_ffn_wq, L1_ffn_wk, L1_ffn_wv, L1_ffn_wo, L1_ffn_qn_w, L1_ffn_kn_w, L1_ffn_gate_w, L1_ffn_e0_up, L1_ffn_e0_down, L1_ffn_e1_w1, L1_ffn_e1_w2, L1_ffn_e1_down, L1_ffn_e2_l1, L1_ffn_e2_l2, L1_ffn_e2_l3, L1_ffn_e2_l4, L1_ffn_e3_down, L1_ffn_e3_up, L1_ffn_e3_out)
    return x

_drawn_inputs = setup_inputs


def setup_inputs(seed=0):
    import zlib

    import numpy as np

    out = dict(_drawn_inputs(seed))
    spreads = {'L0_attn_q_norm_w': (1.0, 0.6),
     'L0_attn_k_norm_w': (1.0, 0.6),
     'L1_ffn_n1_w': (1.0, 0.6),
     'L1_ffn_n2_w': (1.0, 0.6),
     'L1_ffn_qn_w': (1.0, 0.6),
     'L1_ffn_kn_w': (1.0, 0.6)}
    factors = {'L0_ffn_routers': 8.0,
     'L0_ffn_W1': 8.0,
     'L0_ffn_W2': 8.0,
     'L1_ffn_wq': 8.0,
     'L1_ffn_wk': 8.0,
     'L1_ffn_wv': 8.0,
     'L1_ffn_wo': 8.0,
     'L1_ffn_gate_w': 8.0,
     'L1_ffn_e0_up': 59.281,
     'L1_ffn_e0_down': 51.198,
     'L1_ffn_e1_w1': 22.879,
     'L1_ffn_e1_w2': 8.0,
     'L1_ffn_e1_down': 8.0,
     'L1_ffn_e2_l1': 21.361,
     'L1_ffn_e2_l2': 8.0,
     'L1_ffn_e2_l3': 8.0,
     'L1_ffn_e2_l4': 8.0,
     'L1_ffn_e3_down': 35.517,
     'L1_ffn_e3_up': 34.657,
     'L1_ffn_e3_out': 27.999,
     'L0_attn_W_kqv': 8.0,
     'L0_attn_W_proj': 8.0,
     'L1_attn_w_attn': 8.0,
     'L1_attn_w_proj': 8.0}
    for name, (base, spread) in spreads.items():
        noise = np.random.default_rng([zlib.crc32(name.encode()), seed]).standard_normal(out[name].shape)
        drawn = base * np.exp(spread * noise) if base else spread * noise
        out[name] = jnp.asarray(drawn.astype(out[name].dtype))
    for name, factor in factors.items():
        out[name] = (out[name] * factor).astype(out[name].dtype)
    return out
```

```python
from contextlib import ExitStack

import numpy as np
import concourse.bass as bass
from concourse import mybir

F32 = mybir.dt.float32
BF16 = mybir.dt.bfloat16
I32 = mybir.dt.int32
ALU = mybir.AluOpType
ACT = mybir.ActivationFunctionType
AX = mybir.AxisListType

P = 128
T = 2048
NT = T // P
C = 128
H = 16
D = C // H
HG = 4
GL = H // HG
NCH = T // 512
E0, FF, LAYERS = 16, 512, 4
KF = FF // P
NS = (T - E0) // P + E0
E1, HID = 4, 256
OPR = 64
MROW = 6 * D
MASKED = -1.0e30

STEPS = [(c, j) for c in range(NCH) for j in range(4 * c + 4)]
COMBOS = [(t, kc) for t in range(NT) for kc in range(t // 4 + 1)]
NSTEP = len(STEPS)
CHUNK_END = [STEPS.index((c, 4 * c + 3)) for c in range(NCH)]
TURN_AT = {0: (1, "K"), 1: (1, "Q"), 7: (2, "K"), 8: (2, "Q"), 17: (3, "K"), 18: (3, "Q")}
TURN_NEXT_AT = {33: (0, "K"), 34: (0, "Q")}
MAX_AT = {CHUNK_END[c] + 1: c for c in range(NCH - 1)}
MAX_LAST_AT, OUT_LAST_AT = 1, 2
OUT_AT = {CHUNK_END[c] + 2: c for c in range(NCH - 1)}

CONSTS = dict(ident=128, mask_kq=128, mask_qk=128, before=128, ones=128, cos=NT * D, sin=NT * D,
              upto=E0 * E0, iota=E0, tiles=NS)


def const_at():
    at, out = 0, {}
    for name, n in CONSTS.items():
        out[name] = (at, at + n)
        at += n
    return out, at


def need(eng, sem, value):
    if isinstance(value, int) and value <= 0:
        return
    eng.wait_ge(sem, value)


class Steps:

    def __init__(self, eng, sem, passed=None):
        self.eng, self.sem, self.n, self.loop, self.passed = eng, sem, 0, 0, passed

    def __call__(self, ins):
        ins.then_inc(self.sem, 1)
        self.n += 1

    def sync(self):
        need(self.eng, self.sem, self.n + self.loop)
        if self.passed is not None and not isinstance(self.loop, int):
            self.eng.sem_inc(self.passed, 1)


def build(nc, a, out):
    cat, ncon = const_at()
    with ExitStack() as ctx:
        def sb(name, shape, dt=F32):
            return ctx.enter_context(nc.sbuf_tensor(name, shape, dt))

        def ps(name, shape):
            return ctx.enter_context(nc.psum_tensor(name, shape, F32))

        def sem(name):
            return ctx.enter_context(nc.semaphore(name))

        consts = sb("consts", [P, ncon])
        con = {k: consts[:, lo:hi] for k, (lo, hi) in cat.items()}
        ident = con["ident"]
        cos = con["cos"].rearrange("p (t d) -> p t d", d=D)
        sin = con["sin"].rearrange("p (t d) -> p t d", d=D)
        upto = con["upto"].rearrange("p (a b) -> p a b", b=E0)
        bcon = sb("bcon", [P, 5 * 128], BF16)
        identb, mask_kq, mask_qk, beforeb, onesb = (bcon[:, 128 * i:128 * i + 128] for i in range(5))
        x = sb("x", [P, NT, C])
        xn = sb("xn", [P, NT, C])
        xT = sb("xT", [P, T])
        kqv = sb("kqv", [P, 3, NT, 2 * GL, HG * D])
        y = sb("y", [P, NT, 2 * GL, HG * D])
        scratch = y[:, :, :, :].rearrange("p t g c -> p (t g c)")
        w_kqv = sb("w_kqv", [P, 3 * C])
        w_proj = sb("w_proj", [P, C])
        w_mqa = sb("w_mqa", [P, C + 2 * D])
        w_qkv1 = sb("w_qkv1", [P, 3 * C])
        w_mproj = sb("w_mproj", [P, C])
        w_o = sb("w_o", [P, C])
        w_gate = sb("w_gate", [P, E1])
        routers = sb("routers", [P, LAYERS * E0])
        hnorm = sb("hnorm", [P, 4, D])
        cnorm = sb("cnorm", [P, 2, C])
        stats = sb("stats", [P, NT, 6])
        mv = sb("mv", [P, NT, 2])
        rstd = sb("rstd", [P, NT])
        ss = sb("ss", [P, NT, H])

        big = sb("big", [P, 25600])
        w1 = big[:, 0:E0 * FF]
        w2 = big[:, E0 * FF:2 * E0 * FF]
        at = [0]

        def part(nwords):
            lo = at[0]
            at[0] += nwords
            return big[:, lo:at[0]]

        qtok = part(NT * HG * OPR // 2).bitcast(BF16).rearrange("p (t h r) -> p t h r", h=HG, r=OPR)
        ktok = part(NT * HG * OPR // 2).bitcast(BF16).rearrange("p (t h r) -> p t h r", h=HG, r=OPR)
        moe_w = big[:, 0:27 * P]
        qT = [part(T).bitcast(BF16).rearrange("p (a t) -> p a t", a=2) for _ in range(2)]
        kT = [part(2 * T).bitcast(BF16).rearrange("p (h t) -> p h t", h=HG) for _ in range(2)]
        kst = [part(512).bitcast(BF16).rearrange("p (a t) -> p a t", a=2) for _ in range(2)]
        vpad = [part(NT * HG * 32).rearrange("p (t h d) -> p t h d", h=HG, d=32) for _ in range(2)]
        probs = [[w.rearrange("p (a t) -> p a t", a=2) for w in (part(1024), xT[:, 1024 * i:1024 * i + 1024])]
                 for i in range(2)]
        oT = [part(512) for _ in range(2)]
        rest = part(NT * HG * D).rearrange("p (t h d) -> p t h d", h=HG, d=D)
        mT = [part(256).bitcast(BF16) for _ in range(2)]
        hidden = [big[:, 27 * P + 1024 * i:27 * P + 1024 * i + 1024].rearrange("p (k t) -> p k t", k=2)
                  for i in range(6)]
        mpart = sb("mpart", [P, 2, 4, HG, NCH])
        negm = sb("negm", [P, 2, 4, HG])
        mtok = sb("mtok", [P, 2, 4, HG, 2], BF16)
        rec = sb("rec", [P, 2, 4, HG])

        rt = big[:, 2 * E0 * FF + C:2 * E0 * FF + C + 6 * NT * E0].rearrange("p (i n) -> p i n", i=6)
        ohb = sb("ohb", [P, NT, E0], BF16)
        wtop = sb("wtop", [P, NT])
        small = sb("small", [P, 4, NT])
        slot = sb("slot", [P, NT], I32)
        cnt_i = sb("cnt_i", [P, 2, E0], I32)
        ntile = sb("ntile", [P, 3, E0])
        owner_f = sb("owner_f", [P, NS])
        owner = sb("owner", [P, NS], I32)
        xs = scratch[:, 0:4 * C].rearrange("p (b c) -> p b c", c=C)
        yo = scratch[:, 4 * C:8 * C].rearrange("p (b c) -> p b c", c=C)
        xsT = scratch[:, 8 * C:10 * C].rearrange("p (b c) -> p b c", c=P)
        hs = scratch[:, 10 * C:18 * C].rearrange("p (b c) -> p b c", c=FF)
        hT = scratch[:, 18 * C:26 * C].rearrange("p (b c) -> p b c", c=FF)
        zeros = big[:, 2 * E0 * FF:2 * E0 * FF + C]
        xs_dram = nc.dram_tensor("xs_dram", [NS * P, C], F32, kind="Internal").ap()
        ys_dram = nc.dram_tensor("ys_dram", [NS * P, C], F32, kind="Internal").ap()

        st = [ps("st0", [P, 2, 512]), ps("st1", [P, 2, 512])]
        oacc = ps("oacc", [P, 512])
        sq = [ps("sq0", [P, 512]), ps("sq1", [P, 512])]
        misc = ps("misc", [P, 512])
        banks = [st[0][:, 0, :], st[0][:, 1, :], st[1][:, 0, :], st[1][:, 1, :]]

        consts_in = sem("consts_in")
        x_in = sem("x_in")
        w_in = sem("w_in")
        experts_in = sem("experts_in")
        moe_in = sem("moe_in")
        out_done = sem("out_done")
        dve_step = sem("dve_step")
        pool_step, pool_passed = sem("pool_step"), sem("pool_passed")
        consts_cast = sem("consts_cast")
        slots_zeroed = sem("slots_zeroed")
        var_ready, sd_ready = sem("var_ready"), sem("sd_ready")
        cur_ready = sem("cur_ready")
        DENSE = {"xT0": 4, "kqv0": NT, "yT0": 4, "proj0": 4, "xT1": 4, "mqa": NT, "hT1": 4, "qkv1": NT,
                 "yTa": 4, "proja": 4, "yTb": 4, "projb": 4, "xfT": 4, "gate": 1}
        done = {k: sem(f"{k}_done") for k in DENSE}
        freed = {k: sem(f"{k}_read") for k in DENSE}
        norm_sq, norm_sd = sem("norm_sq"), sem("norm_sd")
        kqv_ready = sem("kqv_ready")
        xn_ready = sem("xn_ready")
        curT_done, curT_read = sem("curT_done"), sem("curT_read")
        logits_done, exp_ready = sem("logits_done"), sem("exp_ready")
        dif_ready, onehot_ready, rank_done = sem("dif_ready"), sem("onehot_ready"), sem("rank_done")
        slot_ready, owner_ready = sem("slot_ready"), sem("owner_ready")
        scattered, gathered = sem("scattered"), sem("gathered")
        xs_loaded = [sem(f"xs_loaded{i}") for i in range(4)]
        ys_stored = [sem(f"ys_stored{i}") for i in range(4)]
        xsT_done, xsT_read = sem("xsT_done"), sem("xsT_read")
        up_done, silu_done = sem("up_done"), sem("silu_done")
        hT_done, hT_read = sem("hT_done"), sem("hT_read")
        down_done, down_read = sem("down_done"), sem("down_read")
        pads_zeroed = sem("pads_zeroed")
        qk_packed, v_packed = sem("qk_packed"), sem("v_packed")
        turned, turn_read = sem("turned"), sem("turn_read")
        k_loaded = [sem(f"k_loaded{c}") for c in range(NCH)]
        m_loaded = [sem(f"m_loaded{c}") for c in range(NCH)]
        sq_done, max_done = sem("sq_done"), sem("max_done")
        negm_ready, mT_done, mT_read = sem("negm_ready"), sem("mT_done"), sem("mT_read")
        st_done, exp_done, pv_done = sem("st_done"), sem("exp_done"), sem("pv_done")
        o_read, oT_done, y_done = sem("o_read"), sem("oT_done"), sem("y_done")
        wts_ready, gate_exp, gate_dif = sem("wts_ready"), sem("gate_exp"), sem("gate_dif")
        moe_done, moe_read = sem("moe_done"), sem("moe_read")
        mix_done, mix_read, gated = sem("mix_done"), sem("mix_read"), sem("gated")

        block = ctx.enter_context(nc.Block())

        def tok(tile):
            return slice(tile * P, tile * P + P)

        def group(i, slot_):
            if isinstance(slot_, int):
                return kqv[:, i, :, slot_, :].rearrange("p t (h d) -> p t h d", d=D)
            return kqv[:, i, :, bass.ds(slot_, 1), :].rearrange("p t a (h d) -> p t (a h) d", d=D)

        def bodies(eng, emit, first, last, slot0, steps=None, per_pair=0):
            emit(eng, None, None, first, first + 1, 0, slot0)
            emit(eng, None, first, first + 1, first + 2, first % 2, slot0)
            g = first + 1
            pairs = (last - 1 - g) // 2
            if pairs > 1:
                with eng.Fori(0, pairs) as i:
                    if steps is not None:
                        base, steps.loop = steps.n, i * per_pair
                    for b in range(2):
                        n = g + b + i * 2
                        emit(eng, n - 1, n, n + 1, n + 2, (g + b) % 2, slot0)
                if steps is not None:
                    assert steps.n - base == per_pair, steps.n - base
                    steps.n, steps.loop = base + per_pair * pairs, 0
                g += 2 * pairs
            while g <= last:
                emit(eng, g - 1, g, g + 1 if g < last else None, g + 2 if g + 1 < last else None, g % 2, slot0)
                g += 1
            emit(eng, last, None, None, None, 0, slot0)

        L0 = (0, GL - 1, 0)
        L1 = (GL, 3 * GL - 1, GL)

        def sp_attention(sp, gp, ga, gb, gt, par, slot0):
            if gb is None and ga is None:
                return
            pb = None if gb is None else nxt(ga, par, gb)
            if ga is None:
                keys_to(sp, gb, pb, 0)
            for s in range(NSTEP):
                if gb is not None:
                    if s in TURN_AT and TURN_AT[s][1] == "K":
                        keys_to(sp, gb, pb, TURN_AT[s][0])
                    if s in MAX_AT:
                        max_to(sp, gb, pb, MAX_AT[s])
                if ga is not None and s == MAX_LAST_AT:
                    max_to(sp, ga, par, NCH - 1)
                if gt is not None and s in TURN_NEXT_AT and TURN_NEXT_AT[s][1] == "K":
                    keys_to(sp, gt, 1 - pb, 0)

        def nxt(ga, par, gb):
            return gb % 2 if ga is None else 1 - par

        def keys_to(sp, g, par, c):
            sp.wait_ge(turn_read, 8 * g + 2 * c + 1)
            cols = slice(512 * c, 512 * c + 512)
            for b in range(2):
                rows = slice(64 * b, 64 * b + 64)
                sp.dma_start(kT[par][rows, b:HG:2, cols], kst[c % 2][rows, :, :]).then_inc(k_loaded[c], 16)

        def max_to(sp, g, par, c):
            sp.wait_ge(mT_read, 4 * g + c + 1)
            for h in range(HG):
                row = 64 * (h % 2) + MROW
                sp.dma_start(qT[par][row:row + 2, h // 2, 512 * c:512 * c + 512],
                             mT[c % 2][2 * h:2 * h + 2, :]).then_inc(m_loaded[c], 16)

        def tiles_in_ring(b):
            return len(range(b, NS, 4))

        @block.sync
        def _(sp):
            sp.dma_start(x[:, :, :], a["x"]).then_inc(x_in, 16)
            sp.dma_start(consts[:, :], a["consts"]).then_inc(consts_in, 16)
            for dst, name in ((w_kqv, "w_kqv"), (w_proj, "w_proj"), (w_mqa, "w_mqa"), (w_qkv1, "w_qkv1"),
                              (w_mproj, "w_mproj"), (w_o, "w_o"), (w_gate, "w_gate"), (routers, "routers")):
                sp.dma_start(dst[:, :], a[name]).then_inc(w_in, 16)
            for i, name in enumerate(("hq0", "hk0", "hq1", "hk1")):
                sp.dma_start(hnorm[:, i, :], a[name].to_broadcast([P, D])).then_inc(w_in, 16)
            for i, name in enumerate(("n1", "n2")):
                sp.dma_start(cnorm[:, i, :], a[name].to_broadcast([P, C])).then_inc(w_in, 16)
            for q in range(4):
                n = E0 * FF // 4
                sp.dma_start(w1[:, n * q:n * q + n], a["w1"][:, n * q:n * q + n]).then_inc(experts_in, 16)
                sp.dma_start(w2[:, n * q:n * q + n], a["w2"][:, n * q:n * q + n]).then_inc(experts_in, 16)
            with sp.Fori(0, LAYERS) as l:
                sp.wait_ge(scattered, 256 * (l + 1))
                for i in range(NS + 4):
                    if i < NS:
                        b = i % 4
                        if i >= 4:
                            sp.wait_ge(xsT_done, NS * l + (i - 3))
                        sp.dma_start(xs[:, b, :], xs_dram[tok(i), :]).then_inc(xs_loaded[b], 16)
                    if i >= 4:
                        sp.wait_ge(down_read, NS * l + (i - 3))
                        sp.dma_start(ys_dram[tok(i - 4), :], yo[:, (i - 4) % 4, :])\
                          .then_inc(ys_stored[(i - 4) % 4], 16)
            bodies(sp, sp_attention, *L0)
            bodies(sp, sp_attention, *L1)
            sp.wait_ge(turned, 8 * 3 * GL)
            sp.dma_start(moe_w, a["moe_w"]).then_inc(moe_in, 16)
            sp.wait_ge(mix_read, NT)
            sp.dma_start(out, x[:, :, :]).then_inc(out_done, 16)
            sp.wait_ge(out_done, 16)

        def pack(pool, steps, g, slot_, which):
            src = group(1 if which == "Q" else 0, slot_)
            dst = qtok if which == "Q" else ktok
            places = ((0, 1, 3), (2, 4), (5,)) if which == "Q" else ((0, 2, 5), (1, 4), (3,))
            left = src
            for i, cols in enumerate(places):
                for col in cols:
                    steps(pool.tensor_copy(dst[:, :, :, D * col:D * col + D], left))
                if i < 2:
                    r = rest
                    steps.sync()
                    steps(pool.tensor_tensor(r, left, dst[:, :, :, D * cols[0]:D * cols[0] + D], ALU.subtract))
                    steps.sync()
                    left = r

        def pool_qk(pool, steps, g, slot_):
            need(pool, turned, 8 * g)
            steps.sync()
            pack(pool, steps, g, slot_, "K")
            steps.sync()
            pack(pool, steps, g, slot_, "Q")
            steps.sync()
            pool.nop().then_inc(qk_packed, 1)

        def pool_v(pool, steps, g, par, slot_):
            if not isinstance(g, int) or g >= 2:
                pool.wait_ge(pv_done, NSTEP * (g - 1))
                pool.sem_inc(pool_passed, 1)
            pool.tensor_copy(vpad[par][:, :, :, 0:D], group(2, slot_)).then_inc(v_packed, 1)

        PACK_STEPS = 2 * 8

        @block.gpsimd
        def _(pool):
            steps = Steps(pool, pool_step, passed=pool_passed)
            steps(pool.memset(zeros, 0.0))
            steps.sync()
            pool.dma_start(xs_dram.rearrange("(s p) c -> p s c", p=P),
                           zeros.unsqueeze(1).to_broadcast([P, NS, C])).then_inc(slots_zeroed, 16)
            pool.wait_ge(slots_zeroed, 16)
            with pool.Fori(0, LAYERS) as l:
                pool.wait_ge(slot_ready, l + 1)
                pool.sem_inc(pool_passed, 1)
                for t in range(NT):
                    pool.indirect_dma_start(xs_dram, bass.IndirectOffsetOnAxis(ap=slot[:, t:t + 1], axis=0),
                                            xn[:, t, :], None).then_inc(scattered, 16)
                pool.wait_ge(scattered, 256 * (l + 1))
                for b in range(4):
                    pool.wait_ge(ys_stored[b], 16 * tiles_in_ring(b) * (l + 1))
                pool.sem_inc(pool_passed, 1)
                for t in range(NT):
                    pool.indirect_dma_start(xn[:, t, :], None, ys_dram,
                                            bass.IndirectOffsetOnAxis(ap=slot[:, t:t + 1], axis=0))\
                        .then_inc(gathered, 16)
            pool.wait_ge(cur_ready, NT * (LAYERS + 1))
            steps(pool.memset(qtok[:, :, :, MROW:OPR], 0.0))
            steps(pool.memset(ktok[:, :, :, MROW:MROW + 2], 1.0))
            steps(pool.memset(ktok[:, :, :, MROW + 2:OPR], 0.0))
            for par in range(2):
                for b in range(2):
                    steps.sync()
                    steps(pool.memset(kT[par][64 * (1 - b):64 * (1 - b) + 64, b:HG:2, :], 0.0))
                steps.sync()
                steps(pool.memset(vpad[par][:, :, :, D:D + 1], 1.0))
                steps(pool.memset(vpad[par][:, :, :, D + 1:32], 0.0))
            steps.sync()
            pool.nop().then_inc(pads_zeroed, 1)

            def emit(eng, gp, ga, gb, gt, par, slot0):
                if ga is None and gb is not None:
                    pool_qk(eng, steps, gb, gb - slot0)
                if gb is not None:
                    pool_v(eng, steps, gb, nxt(ga, par, gb), gb - slot0)
                if gt is not None:
                    pool_qk(eng, steps, gt, gt - slot0)

            pool.wait_ge(kqv_ready, 1)
            bodies(pool, emit, *L0, steps, 2 * PACK_STEPS)
            pool.wait_ge(kqv_ready, 2)
            bodies(pool, emit, *L1, steps, 2 * PACK_STEPS)

        def attn_pe(pe, gp, ga, gb, gt, par, slot0):
            pb = nxt(ga, par, gb) if gb is not None else None
            prev = []

            def take_misc(next_reader):
                for s_, v in prev:
                    need(pe, s_, v)
                prev[:] = [next_reader]

            def turn(g, c, kind):
                n = 8 * g + 2 * c + (kind == "Q")
                take_misc((turn_read, n + 1))
                need(pe, qk_packed, g + 1)
                view = misc[:, :].bitcast(BF16).rearrange("p (a t) -> p a t", a=2)
                src = ktok if kind == "K" else qtok
                for a_ in range(2):
                    for t in range(4):
                        m = pe.transpose(view[:, a_, tok(t)],
                                         src[:, 4 * c + t, 2 * a_:2 * a_ + 2, :].rearrange("p h r -> p (h r)"),
                                         identb)
                m.then_inc(turned, 1)

            def turn_max(g, c):
                take_misc((mT_read, 4 * g + c + 1))
                pe.wait_ge(negm_ready, 4 * g + c + 1)
                view = misc[0:2 * HG, :].bitcast(BF16)
                for t in range(4):
                    m = pe.transpose(view[:, tok(t)], mtok[:, c % 2, t, :, :].rearrange("p h e -> p (h e)"),
                                     identb)
                m.then_inc(mT_done, 1)

            def turn_out(g, c):
                take_misc((y_done, 4 * g + c + 1))
                pe.wait_ge(o_read, 4 * g + c + 1)
                for t in range(4):
                    m = pe.transpose(misc[:, tok(t)], oT[c % 2][:, tok(t)], ident)
                m.then_inc(oT_done, 1)

            def scores_t(g, gpar, s, a_):
                c, j = STEPS[s]
                off = 128 * max(0, j - 4 * c)
                if j == 0:
                    pe.wait_ge(m_loaded[c], 64 * (g + 1))
                need(pe, exp_done, 2 * NSTEP * g + (2 * (s - 1) + a_ + 1))
                for b in range(2):
                    o = st[a_][:, b, :]
                    m = pe.matmul(o[:, off:512], kT[gpar][:, 2 * a_ + b, tok(j)],
                                  qT[gpar][:, a_, 512 * c + off:512 * c + 512], start=True, stop=j < 4 * c)
                    if j >= 4 * c:
                        m = pe.matmul(o[:, off:off + 128], identb, mask_kq, start=False, stop=True)
                m.then_inc(st_done, 1)

            def scores(g, gpar, s, h):
                t, kc = COMBOS[s]
                c = t // 4
                if t % 4 == 0 and kc == 0 and h == 0:
                    pe.wait_ge(turn_read, 8 * g + 2 * c + 2)
                    pe.wait_ge(k_loaded[c], 32 * (g + 1))
                n = min(512, (t + 1) * P - 512 * kc)
                need(pe, max_done, HG * NSTEP * g + (HG * s + h - 1))
                o = sq[h % 2]
                m = pe.matmul(o[:, 0:n], qT[gpar][:, h // 2, tok(t)],
                              kT[gpar][:, h, 512 * kc:512 * kc + n], start=True, stop=kc < c)
                if kc == c:
                    m = pe.matmul(o[:, n - 128:n], identb, mask_qk, start=False, stop=True)
                m.then_inc(sq_done, 1)

            def weigh(g, gpar, s):
                c, j = STEPS[s]
                off = 128 * max(0, j - 4 * c)
                pe.wait_ge(exp_done, 2 * NSTEP * g + (2 * s + 2))
                if s == 0:
                    pe.wait_ge(v_packed, g + 1)
                if j == 0:
                    need(pe, o_read, 4 * g + c)
                for h in range(HG):
                    m = pe.matmul(oacc[32 * h:32 * h + 32, off:512], vpad[gpar][:, j, h, :],
                                  probs[s % 2][h // 2][:, h % 2, off:512], start=(j == 0), stop=(j == 4 * c + 3),
                                  tile_position=(0, 32 * h))
                m.then_inc(pv_done, 1)

            if ga is None and gb is None:
                prev[:] = [(y_done, 4 * gp + 3)]
                turn_out(gp, NCH - 1)
                return
            if ga is None:
                turn(gb, 0, "K")
                turn(gb, 0, "Q")
            elif gb is None:
                prev[:] = [(y_done, 4 * gp + 3)]
            else:
                prev[:] = [(turn_read, 8 * gb + 2)]
            for s in range(NSTEP):
                units = iter(range(HG))
                if gb is not None:
                    scores(gb, pb, s, next(units))
                for a_ in range(2):
                    if ga is not None and s + 1 < NSTEP:
                        scores_t(ga, par, s + 1, a_)
                    elif ga is not None and gb is not None:
                        scores_t(gb, pb, 0, a_)
                    if gb is not None:
                        scores(gb, pb, s, next(units))
                if ga is not None:
                    weigh(ga, par, s)
                if gb is not None:
                    scores(gb, pb, s, next(units))
                if gb is not None and s in TURN_AT:
                    turn(gb, *TURN_AT[s])
                if gb is not None and s in MAX_AT:
                    turn_max(gb, MAX_AT[s])
                if ga is not None and s == MAX_LAST_AT:
                    turn_max(ga, NCH - 1)
                if ga is not None and s in OUT_AT:
                    turn_out(ga, OUT_AT[s])
                if gp is not None and s == OUT_LAST_AT:
                    turn_out(gp, NCH - 1)
                if gt is not None and s in TURN_NEXT_AT:
                    turn(gt, *TURN_NEXT_AT[s])
            if ga is None:
                for a_ in range(2):
                    scores_t(gb, pb, 0, a_)

        def dense(pe, name, emit, before=None):
            if before is not None:
                pe.wait_ge(freed[before], DENSE[before])
            for n in range(DENSE[name]):
                if n >= 4:
                    pe.wait_ge(freed[name], n - 3)
                emit(n, banks[n % 4]).then_inc(done[name], 1)

        def turn_tiles(pe, src):
            def emit(n, bank):
                for t in range(4):
                    m = pe.transpose(bank[:, tok(t)], src(4 * n + t), ident)
                return m
            return emit

        def times(pe, w, cols):
            def emit(n, bank):
                return pe.matmul(bank[:, 0:cols], xT[:, tok(n)], w, start=True, stop=True)
            return emit

        def times4(pe, w):
            def emit(n, bank):
                for t in range(4):
                    m = pe.matmul(bank[:, tok(t)], xT[:, tok(4 * n + t)], w, start=True, stop=True)
                return m
            return emit

        UP0, DN0, W1_, W2_, DN1 = 0, 2, 4, 6, 8
        L1_, L2_, L3_, L4_, DN3, UP3, OUT3 = 10, 12, 16, 20, 22, 23, 25
        MOE = [(W1_, 2, 1, None, 1, "silu"), (W2_, 2, 1, None, 1, "times"),
               (UP0, 2, 1, None, 0, "gelu"), (L1_, 2, 1, None, 2, "gelu"), (DN3, 1, 1, None, 4, "gelu"),
               (L2_, 2, 2, 2, 3, "gelu"), (UP3, 2, 1, 4, 5, "gelu"), (L3_, 2, 2, 3, 2, "gelu")]
        MOE_UNITS = [(b + k_out * 1, k_out, ki, src, dst, f) for b, ko, ki, src, dst, f in MOE for k_out in range(ko)]
        NU = len(MOE_UNITS)
        LASTS = [(DN0, 0), (DN1, 1), (L4_, 2), (OUT3, 5)]

        def block_w(b):
            return moe_w[:, P * b:P * b + P]

        def unit_ready(src, u):
            _, _, _, s, d, _ = MOE_UNITS[u]
            ns = [v for v in range(u) if MOE_UNITS[v][4] == s and s is not None]
            return max(ns) + 1 if ns else 0

        def moe_pe(pe):
            pe.wait_ge(moe_in, 16)
            mbanks = banks
            for c in range(NCH):
                cols = slice(512 * c, 512 * c + 512)
                for u, (b, ko, ki, src, dst, f) in enumerate(MOE_UNITS):
                    n = NU * c + u
                    need(pe, moe_read, n - 3)
                    need(pe, moe_read, NU * c + unit_ready(None, u) if src is not None else 0)
                    for k in range(ki):
                        rhs = xT[:, cols] if src is None else hidden[src][:, k, :]
                        blk = b + (k * 2 if ki == 2 else 0)
                        m = pe.matmul(mbanks[n % 4], block_w(blk), rhs, start=(k == 0), stop=(k == ki - 1))
                    m.then_inc(moe_done, 1)
                pe.wait_ge(moe_read, NU * (c + 1))
                for t in range(4):
                    n = 4 * c + t
                    need(pe, mix_read, n - 1)
                    o = sq[n % 2]
                    for e, (b, src) in enumerate(LASTS):
                        for k in range(2):
                            m = pe.matmul(o[:, tok(e)], hidden[src][:, k, tok(t)], block_w(b + k),
                                          start=(k == 0), stop=(k == 1))
                    m.then_inc(mix_done, 1)

        @block.tensor
        def _(pe):
            pe.wait_ge(consts_in, 16)
            pe.wait_ge(cur_ready, NT)
            dense(pe, "xT0", turn_tiles(pe, lambda t: xn[:, t, :]))
            pe.wait_ge(freed["xT0"], 4)
            pe.wait_ge(w_in, 16 * 14)
            dense(pe, "kqv0", times(pe, w_kqv[:, :], 3 * C), "xT0")
            pe.wait_ge(freed["kqv0"], NT)
            pe.wait_ge(experts_in, 16 * 8)
            pe.wait_ge(consts_cast, 1)
            with pe.Fori(0, LAYERS) as l:
                pe.wait_ge(cur_ready, NT * (l + 1))
                for n in range(4):
                    for t in range(4):
                        m = pe.transpose(banks[n][:, tok(t)], xn[:, 4 * n + t, :], ident)
                    m.then_inc(curT_done, 1)
                pe.wait_ge(curT_read, 4 * (l + 1))
                for t in range(NT):
                    m = pe.matmul(oacc[:, E0 * t:E0 * t + E0], xT[:, tok(t)], routers[:, bass.ds(l * E0, E0)],
                                  start=True, stop=True)
                m.then_inc(logits_done, 1)
                pe.wait_ge(onehot_ready, l + 1)
                flat = ohb[:, :, :].rearrange("p t e -> p (t e)")
                pe.matmul(sq[0][:, 0:NT * E0], beforeb, flat, start=True, stop=False)
                for t in range(NT - 1):
                    m = pe.matmul(sq[0][:, E0 * (t + 1):NT * E0], onesb,
                                  ohb[:, t:t + 1, :].to_broadcast([P, NT - 1 - t, E0]),
                                  start=False, stop=(t == NT - 2))
                for t in range(NT):
                    m = pe.matmul(sq[1][:, 0:E0], onesb, ohb[:, t, :], start=(t == 0), stop=(t == NT - 1))
                m.then_inc(rank_done, 1)
                pe.wait_ge(owner_ready, l + 1)
                for s in range(NS + 3):
                    if s < NS:
                        i = s
                        pe.wait_ge(xs_loaded[i % 4], 16 * (tiles_in_ring(i % 4) * l + (i // 4 + 1)))
                        if i >= 2:
                            pe.wait_ge(xsT_read, NS * l + (i - 1))
                        pe.transpose(banks[i % 2][:, 0:P], xs[:, i % 4, :], ident).then_inc(xsT_done, 1)
                    if 0 <= s - 1 < NS:
                        i = s - 1
                        e = pe.value_load(owner[0:1, i:i + 1], min_val=0, max_val=E0 - 1)
                        pe.wait_ge(xsT_read, NS * l + (i + 1))
                        if i >= 2:
                            pe.wait_ge(silu_done, NS * l + (i - 1))
                        pe.matmul(banks[2 + i % 2], xsT[:, i % 2, :], w1[:, bass.ds(e * FF, FF)],
                                  start=True, stop=True).then_inc(up_done, 1)
                    if 0 <= s - 2 < NS:
                        i = s - 2
                        pe.wait_ge(silu_done, NS * l + (i + 1))
                        if i >= 2:
                            pe.wait_ge(hT_read, NS * l + (i - 1))
                        o = (oacc, misc)[i % 2]
                        for k in range(KF):
                            m = pe.transpose(o[:, tok(k)], hs[:, i % 2, tok(k)], ident)
                        m.then_inc(hT_done, 1)
                    if 0 <= s - 3 < NS:
                        i = s - 3
                        e = pe.value_load(owner[0:1, i:i + 1], min_val=0, max_val=E0 - 1)
                        pe.wait_ge(hT_read, NS * l + (i + 1))
                        if i >= 2:
                            pe.wait_ge(down_read, NS * l + (i - 1))
                        for k in range(KF):
                            m = pe.matmul(sq[i % 2][:, 0:C], hT[:, i % 2, tok(k)],
                                          w2[:, bass.ds(e * FF + k * C, C)], start=(k == 0), stop=(k == KF - 1))
                        m.then_inc(down_done, 1)
            pe.wait_ge(down_read, NS * LAYERS)
            pe.wait_ge(pads_zeroed, 1)
            bodies(pe, attn_pe, *L0)
            pe.wait_ge(y_done, 4 * GL)
            dense(pe, "yT0", turn_tiles(pe, lambda t: y[:, t, 0:GL, :].rearrange("p g c -> p (g c)")))
            pe.wait_ge(freed["yT0"], 4)
            dense(pe, "proj0", times4(pe, w_proj[:, :]), "yT0")
            pe.wait_ge(xn_ready, 1)
            dense(pe, "xT1", turn_tiles(pe, lambda t: xn[:, t, :]), "proj0")
            pe.wait_ge(freed["xT1"], 4)
            dense(pe, "mqa", times(pe, w_mqa[:, :], C + 2 * D), "xT1")
            pe.wait_ge(xn_ready, 2)
            dense(pe, "hT1", turn_tiles(pe, lambda t: scratch[:, tok(t)]), "mqa")
            pe.wait_ge(freed["hT1"], 4)
            dense(pe, "qkv1", times(pe, w_qkv1[:, :], 3 * C), "hT1")
            pe.wait_ge(freed["qkv1"], NT)
            bodies(pe, attn_pe, *L1)
            pe.wait_ge(y_done, 12 * GL)
            dense(pe, "yTa", turn_tiles(pe, lambda t: y[:, t, 0:GL, :].rearrange("p g c -> p (g c)")))
            pe.wait_ge(freed["yTa"], 4)
            dense(pe, "proja", times4(pe, w_mproj[:, :]), "yTa")
            dense(pe, "yTb", turn_tiles(pe, lambda t: y[:, t, GL:2 * GL, :].rearrange("p g c -> p (g c)")), "proja")
            pe.wait_ge(freed["yTb"], 4)
            dense(pe, "projb", times4(pe, w_o[:, :]), "yTb")
            pe.wait_ge(xn_ready, 3)
            dense(pe, "xfT", turn_tiles(pe, lambda t: scratch[:, tok(t)]), "projb")
            pe.wait_ge(freed["xfT"], 4)

            def gate(n, bank):
                for t in range(NT):
                    m = pe.matmul(bank[:, E1 * t:E1 * t + E1], xT[:, tok(t)], w_gate[:, :], start=True, stop=True)
                return m
            dense(pe, "gate", gate, "xfT")
            pe.wait_ge(freed["gate"], 1)
            moe_pe(pe)

        def attn_act(act, gp, ga, gb, gt, par, slot0):
            pb = nxt(ga, par, gb) if gb is not None else None

            def read_turn(g, gpar, c, kind):
                n = 8 * g + 2 * c + (kind == "Q")
                act.wait_ge(turned, n + 1)
                view = misc[:, :].bitcast(BF16).rearrange("p (a t) -> p a t", a=2)
                if kind == "K":
                    need(act, k_loaded[(c - 2) % NCH], 32 * (g + 1) if c >= 2 else 32 * g)
                    act.activation(kst[c % 2], view, ACT.Copy).then_inc(turn_read, 1)
                else:
                    act.activation(qT[gpar][:, :, 512 * c:512 * c + 512], view, ACT.Copy).then_inc(turn_read, 1)

            def read_max(g, c):
                act.wait_ge(mT_done, 4 * g + c + 1)
                need(act, m_loaded[(c - 2) % NCH], 64 * (g + 1) if c >= 2 else 64 * g)
                act.activation(mT[c % 2][0:2 * HG, :], misc[0:2 * HG, :].bitcast(BF16)[:, 0:512], ACT.Copy)\
                   .then_inc(mT_read, 1)

            def read_out(g, c):
                act.wait_ge(pv_done, NSTEP * g + (CHUNK_END[c] + 1))
                need(act, oT_done, 4 * g + (c - 1))
                act.activation(oT[c % 2], oacc[:, :], ACT.Copy).then_inc(o_read, 1)

            def exp(g, s):
                c, j = STEPS[s]
                off = 128 * max(0, j - 4 * c)
                for a_ in range(2):
                    act.wait_ge(st_done, 2 * NSTEP * g + (2 * s + a_ + 1))
                    need(act, pv_done, NSTEP * g + (s - 1))
                    act.activation(probs[s % 2][a_][:, :, off:512], st[a_][:, :, off:512], ACT.Exp)\
                       .then_inc(exp_done, 1)

            if gb is None and ga is None:
                read_out(gp, NCH - 1)
                return
            if ga is None:
                read_turn(gb, pb, 0, "K")
                read_turn(gb, pb, 0, "Q")
            for s in range(NSTEP + 1):
                if ga is not None and s < NSTEP:
                    exp(ga, s)
                if gp is not None and s == 0:
                    read_out(gp, NCH - 1)
                if gb is not None and s - 1 in TURN_AT:
                    read_turn(gb, pb, *TURN_AT[s - 1])
                if gb is not None and s - 1 in MAX_AT:
                    read_max(gb, MAX_AT[s - 1])
                if ga is not None and s - 1 == MAX_LAST_AT:
                    read_max(ga, NCH - 1)
                if ga is not None and s - 1 in CHUNK_END[:-1]:
                    read_out(ga, CHUNK_END.index(s - 1))
                if gt is not None and s - 1 in TURN_NEXT_AT:
                    read_turn(gt, 1 - pb, *TURN_NEXT_AT[s - 1])

        def copy_dense(act, name, dst):
            for n in range(DENSE[name]):
                act.wait_ge(done[name], n + 1)
                o, i = dst(n, banks[n % 4])
                act.activation(o, i, ACT.Copy).then_inc(freed[name], 1)

        def to_xT(n, bank):
            return xT[:, 512 * n:512 * n + 512], bank

        @block.scalar
        def _(act):
            act.wait_ge(var_ready, 1)
            act.activation(rstd[:, :], mv[:, :, 1], ACT.Sqrt).then_inc(sd_ready, 1)
            copy_dense(act, "xT0", to_xT)

            def kqv_out(n, bank):
                return (kqv[:, :, n, 0:GL, :].rearrange("p i g c -> p i (g c)"),
                        bank[:, 0:3 * C].rearrange("p (i c) -> p i c", i=3))
            copy_dense(act, "kqv0", kqv_out)
            for n in range(2):
                act.wait_ge(norm_sq, n + 1)
                act.activation(ss[:, :, :], ss[:, :, :], ACT.Sqrt).then_inc(norm_sd, 1)
            with act.Fori(0, LAYERS) as l:
                for n in range(4):
                    act.wait_ge(curT_done, 4 * l + (n + 1))
                    act.activation(xT[:, 512 * n:512 * n + 512], banks[n], ACT.Copy).then_inc(curT_read, 1)
                act.wait_ge(dif_ready, l + 1)
                act.activation(rt[:, 1, :], rt[:, 0, :], ACT.Exp).then_inc(exp_ready, 1)
                for s in range(NS + 2):
                    if s < NS:
                        act.wait_ge(up_done, NS * l + (s + 1))
                        if s >= 2:
                            act.wait_ge(hT_done, NS * l + (s - 1))
                        act.activation(hs[:, s % 2, :], banks[2 + s % 2], ACT.Silu).then_inc(silu_done, 1)
                    if s >= 2:
                        i = s - 2
                        act.wait_ge(down_done, NS * l + (i + 1))
                        if i >= 4:
                            act.wait_ge(ys_stored[i % 4], 16 * (tiles_in_ring(i % 4) * l + i // 4))
                        act.activation(yo[:, i % 4, :], sq[i % 2][:, 0:C], ACT.Copy).then_inc(down_read, 1)
            bodies(act, attn_act, *L0)
            copy_dense(act, "yT0", to_xT)
            act.wait_ge(var_ready, 2)
            act.activation(rstd[:, :], mv[:, :, 1], ACT.Sqrt).then_inc(sd_ready, 1)
            copy_dense(act, "xT1", to_xT)
            act.wait_ge(var_ready, 3)
            act.activation(rstd[:, :], mv[:, :, 1], ACT.Sqrt).then_inc(sd_ready, 1)
            copy_dense(act, "hT1", to_xT)

            def qkv1_out(n, bank):
                return (kqv[:, :, n, GL:2 * GL, :].rearrange("p i g c -> p i (g c)"),
                        bank[:, 0:3 * C].rearrange("p (i c) -> p i c", i=3))
            copy_dense(act, "qkv1", qkv1_out)
            for n in range(2, 4):
                act.wait_ge(norm_sq, n + 1)
                act.activation(ss[:, :, :], ss[:, :, :], ACT.Sqrt).then_inc(norm_sd, 1)
            bodies(act, attn_act, *L1)
            copy_dense(act, "yTa", to_xT)
            copy_dense(act, "yTb", to_xT)
            act.wait_ge(var_ready, 4)
            act.activation(rstd[:, :], mv[:, :, 1], ACT.Sqrt).then_inc(sd_ready, 1)
            copy_dense(act, "xfT", to_xT)
            act.wait_ge(gate_dif, 1)
            act.activation(rt[:, 1, 0:NT * E1], rt[:, 0, 0:NT * E1], ACT.Exp).then_inc(gate_exp, 1)
            for c in range(NCH):
                for u, (b, ko, ki, src, dst, f) in enumerate(MOE_UNITS):
                    n = NU * c + u
                    if f == "times":
                        continue
                    act.wait_ge(moe_done, n + 1)
                    need(act, moe_read, n)
                    if u == 0:
                        need(act, mix_done, 4 * c)
                    act.activation(hidden[dst][:, ko, :], banks[n % 4],
                                   ACT.Silu if f == "silu" else ACT.Gelu).then_inc(moe_read, 1)

        def attn_dve(dve, gp, ga, gb, gt, par, slot0, steps):
            def finish_max(g, c):
                dve.wait_ge(max_done, HG * NSTEP * g + HG * (CHUNK_END[c] + 1))
                need(dve, mT_done, 4 * g + (c - 1))
                steps(dve.tensor_reduce(negm[:, c % 2, :, :], mpart[:, c % 2, :, :, 0:c + 1], AX.X, ALU.max,
                                        negate=True))
                steps.sync()
                steps(dve.tensor_copy(mtok[:, c % 2, :, :, 0], negm[:, c % 2, :, :]))
                steps.sync()
                dve.tensor_tensor(mtok[:, c % 2, :, :, 1], negm[:, c % 2, :, :], mtok[:, c % 2, :, :, 0],
                                  ALU.subtract).then_inc(negm_ready, 1)

            def finish_out(g, c):
                dve.wait_ge(oT_done, 4 * g + c + 1)
                need(dve, y_done, 4 * g + (c - 1))
                view = misc[:, :].rearrange("p (t h d) -> p t h d", t=4, d=32)
                steps(dve.reciprocal(rec[:, c % 2, :, :], view[:, :, :, D]))
                steps.sync()
                slot_ = g - slot0
                if isinstance(slot_, int):
                    o = y[:, 4 * c:4 * c + 4, slot_, :].rearrange("p t (h d) -> p t h d", d=D)
                else:
                    o = y[:, 4 * c:4 * c + 4, bass.ds(slot_, 1), :].rearrange("p t a (h d) -> p t (a h) d", d=D)
                dve.tensor_tensor(o, view[:, :, :, 0:D],
                                  rec[:, c % 2, :, :].unsqueeze(3).to_broadcast([P, 4, HG, D]), ALU.mult)\
                    .then_inc(y_done, 1)

            if gb is None and ga is None:
                finish_out(gp, NCH - 1)
                return
            for s in range(NSTEP):
                if gb is not None:
                    t, kc = COMBOS[s]
                    n = min(512, (t + 1) * P - 512 * kc)
                    if t % 4 == 0 and kc == 0:
                        need(dve, negm_ready, 4 * gb + (t // 4 - 1))
                    for h in range(HG):
                        dve.wait_ge(sq_done, HG * NSTEP * gb + (HG * s + h + 1))
                        dve.tensor_reduce(mpart[:, (t // 4) % 2, t % 4, h, kc:kc + 1], sq[h % 2][:, 0:n], AX.X,
                                          ALU.max).then_inc(max_done, 1)
                    if s in CHUNK_END:
                        finish_max(gb, CHUNK_END.index(s))
                if ga is not None and s - 1 in OUT_AT:
                    finish_out(ga, OUT_AT[s - 1])
                if gp is not None and s - 1 == OUT_LAST_AT:
                    finish_out(gp, NCH - 1)

        def bc(ap, shape, axis):
            return ap.unsqueeze(axis).to_broadcast(shape)

        def add_banks(dve, name, where):
            for n in range(DENSE[name]):
                dve.wait_ge(done[name], n + 1)
                o, i0, i1 = where(n, banks[n % 4])
                dve.tensor_tensor(o, i0, i1, ALU.add).then_inc(freed[name], 1)

        @block.vector
        def _(dve):
            steps = Steps(dve, dve_step)
            big3 = [P, NT, C]

            def layer_norm(n, eps, dst, event, count):
                for t in range(NT):
                    steps(dve.bn_stats(stats[:, t, :], x[:, t, :]))
                steps.sync()
                for t in range(NT):
                    steps(dve.bn_aggr(mv[:, t, :], stats[:, t, :]))
                steps.sync()
                steps(dve.tensor_scalar(mv[:, :, 1], mv[:, :, 1], eps, None, ALU.add))
                steps.sync()
                dve.nop().then_inc(var_ready, 1)
                dve.wait_ge(sd_ready, n)
                steps(dve.reciprocal(rstd[:, :], rstd[:, :]))
                steps.sync()
                for t in range(NT):
                    i = dve.tensor_scalar(dst[:, t, :], x[:, t, :], mv[:, t, 0:1], rstd[:, t:t + 1],
                                          ALU.subtract, ALU.mult)
                    if event is not None:
                        i.then_inc(event, 1)
                    else:
                        steps(i)

            def rms_rows(src, n, w):
                half = scratch[:, 0:T].rearrange("p (t c) -> p t c", c=C)
                other = scratch[:, T:2 * T].rearrange("p (t c) -> p t c", c=C)
                steps.sync()
                steps(dve.tensor_tensor(other, src, src, ALU.mult))
                steps.sync()
                steps(dve.tensor_reduce(mv[:, :, 1], other, AX.X, ALU.add))
                steps.sync()
                steps(dve.tensor_scalar(mv[:, :, 1], mv[:, :, 1], 1.0 / C, 1.1920929e-07, ALU.mult, ALU.add))
                steps.sync()
                dve.nop().then_inc(var_ready, 1)
                dve.wait_ge(sd_ready, n)
                steps(dve.reciprocal(rstd[:, :], rstd[:, :]))
                steps.sync()
                steps(dve.tensor_tensor(other, src, bc(rstd[:, :], big3, 2), ALU.mult))
                steps.sync()
                steps(dve.tensor_tensor(half, other, bc(w, big3, 1), ALU.mult))
                steps.sync()

            def head_norm(i, lo, w, n, rotate, in_eps, out_eps, scale):
                def heads(ap):
                    return ap.rearrange("p t g (h d) -> p t (g h) d", d=D)
                v = heads(kqv[:, i, :, lo:lo + GL, :])
                shape = [P, NT, H, D]
                t1 = scratch[:, 0:T].rearrange("p (t h d) -> p t h d", h=H, d=D)
                t2 = scratch[:, T:2 * T].rearrange("p (t h d) -> p t h d", h=H, d=D)
                hd = D // 2
                steps.sync()
                if rotate:
                    half = [P, NT, H, hd]
                    steps(dve.tensor_tensor(t1[:, :, :, 0:hd], v[:, :, :, hd:D], bc(sin[:, :, 0:hd], half, 2), ALU.mult))
                    steps(dve.tensor_tensor(t1[:, :, :, hd:D], v[:, :, :, 0:hd], bc(sin[:, :, hd:D], half, 2), ALU.mult))
                    steps(dve.tensor_tensor(t2, v, bc(cos, shape, 2), ALU.mult))
                    steps.sync()
                    steps(dve.tensor_tensor(v, t1, t2, ALU.add))
                    steps.sync()
                steps(dve.tensor_tensor(t1, v, v, ALU.mult))
                steps.sync()
                steps(dve.tensor_reduce(ss[:, :, :], t1, AX.X, ALU.add))
                steps.sync()
                steps(dve.tensor_scalar(ss[:, :, :], ss[:, :, :], 1.0 / D, in_eps, ALU.mult, ALU.add))
                steps.sync()
                dve.nop().then_inc(norm_sq, 1)
                dve.wait_ge(norm_sd, n)
                steps(dve.tensor_scalar(ss[:, :, :], ss[:, :, :], out_eps, None, ALU.add))
                steps.sync()
                steps(dve.reciprocal(ss[:, :, :], ss[:, :, :]))
                if scale != 1.0:
                    steps(dve.tensor_scalar(w, w, scale, None, ALU.mult))
                steps.sync()
                steps(dve.tensor_tensor(t2, v, bc(ss[:, :, :], shape, 3), ALU.mult))
                steps.sync()
                wb = w.unsqueeze(1).unsqueeze(1).to_broadcast(shape)
                steps(dve.tensor_tensor(v, t2, wb, ALU.mult))
                steps.sync()

            dve.wait_ge(x_in, 16)
            layer_norm(1, 1e-05, xn, cur_ready, 0)
            dve.wait_ge(consts_in, 16)
            dve.tensor_copy(bcon[:, :], consts[:, 0:5 * 128]).then_inc(consts_cast, 1)
            dve.wait_ge(freed["kqv0"], NT)
            dve.wait_ge(w_in, 16 * 14)
            head_norm(1, 0, hnorm[:, 0, :], 1, True, 0.0, 1e-06, D ** -0.5)
            head_norm(0, 0, hnorm[:, 1, :], 2, True, 0.0, 1e-06, 1.0)
            dve.nop().then_inc(kqv_ready, 1)

            shape = [P, NT, E0]
            v3 = lambda i: rt[:, i, :].rearrange("p (t e) -> p t e", e=E0)
            iota_b = con["iota"].unsqueeze(1).to_broadcast(shape)
            STEPS_PER_LAYER = 18
            with dve.Fori(0, LAYERS) as l:
                base = steps.n
                steps.loop = l * STEPS_PER_LAYER
                dve.wait_ge(logits_done, l + 1)
                lg = oacc[:, 0:NT * E0].rearrange("p (t e) -> p t e", e=E0)
                steps(dve.tensor_reduce(small[:, 0, :], lg, AX.X, ALU.max))
                steps.sync()
                dve.tensor_tensor(v3(0), lg, bc(small[:, 0, :], shape, 2), ALU.subtract).then_inc(dif_ready, 1)
                dve.wait_ge(dif_ready, l + 1)
                steps(dve.tensor_scalar(rt[:, 2, :], rt[:, 0, :], 0.0, 64.0, ALU.is_lt, ALU.mult))
                steps.sync()
                steps(dve.tensor_tensor(v3(3), v3(2), iota_b, ALU.add))
                steps.sync()
                steps(dve.tensor_reduce(small[:, 1, :], v3(3), AX.X, ALU.min))
                steps.sync()
                dve.tensor_tensor(ohb[:, :, :], iota_b, bc(small[:, 1, :], shape, 2), ALU.is_equal)\
                    .then_inc(onehot_ready, 1)
                dve.wait_ge(exp_ready, l + 1)
                steps(dve.tensor_reduce(small[:, 2, :], v3(1), AX.X, ALU.add))
                steps.sync()
                steps(dve.reciprocal(wtop[:, :], small[:, 2, :]))
                dve.wait_ge(rank_done, l + 1)
                steps(dve.tensor_scalar(cnt_i[:, 0, :], sq[1][:, 0:E0], 127.0, None, ALU.add))
                steps.sync()
                steps(dve.tensor_scalar(cnt_i[:, 1, :], cnt_i[:, 0, :], 7, None, ALU.arith_shift_right))
                steps.sync()
                steps(dve.tensor_copy(ntile[:, 0, :], cnt_i[:, 1, :]))
                steps.sync()
                steps(dve.tensor_tensor(v3(2), upto, ntile[:, 0, :].unsqueeze(1).to_broadcast([P, E0, E0]), ALU.mult))
                steps.sync()
                steps(dve.tensor_reduce(ntile[:, 1, :], v3(2), AX.X, ALU.add))
                steps.sync()
                own = rt[:, 3:5, :].rearrange("p a e -> p (a e)")[:, 0:NS * E0].rearrange("p (s e) -> p s e", e=E0)
                steps(dve.tensor_tensor(own, con["tiles"].unsqueeze(2).to_broadcast([P, NS, E0]),
                                        ntile[:, 1, :].unsqueeze(1).to_broadcast([P, NS, E0]), ALU.is_ge))
                steps(dve.tensor_tensor(ntile[:, 2, :], ntile[:, 1, :], ntile[:, 0, :], ALU.subtract))
                steps.sync()
                steps(dve.tensor_reduce(owner_f[:, :], own, AX.X, ALU.add))
                steps(dve.tensor_scalar(ntile[:, 2, :], ntile[:, 2, :], 128.0, None, ALU.mult))
                steps.sync()
                dve.tensor_scalar(owner[:, :], owner_f[:, :], float(E0 - 1), None, ALU.min)\
                    .then_inc(owner_ready, 1)
                steps(dve.tensor_tensor(v3(5), sq[0][:, 0:NT * E0].rearrange("p (t e) -> p t e", e=E0),
                                        ntile[:, 2, :].unsqueeze(1).to_broadcast(shape), ALU.add))
                steps.sync()
                steps(dve.tensor_tensor(v3(2), v3(5), ohb[:, :, :], ALU.mult))
                steps.sync()
                steps(dve.tensor_reduce(small[:, 3, :], v3(2), AX.X, ALU.add))
                steps.sync()
                dve.tensor_copy(slot[:, :], small[:, 3, :]).then_inc(slot_ready, 1)
                for s in range(NS + 2):
                    if s < NS:
                        dve.wait_ge(xsT_done, NS * l + (s + 1))
                        if s >= 2:
                            dve.wait_ge(up_done, NS * l + (s - 1))
                        dve.tensor_copy(xsT[:, s % 2, :], banks[s % 2][:, 0:P]).then_inc(xsT_read, 1)
                    if s >= 2:
                        i = s - 2
                        dve.wait_ge(hT_done, NS * l + (i + 1))
                        if i >= 2:
                            dve.wait_ge(down_done, NS * l + (i - 1))
                        dve.tensor_copy(hT[:, i % 2, :], (oacc, misc)[i % 2][:, :]).then_inc(hT_read, 1)
                dve.wait_ge(gathered, 256 * (l + 1))
                for t in range(NT):
                    dve.tensor_scalar(xn[:, t, :], xn[:, t, :], wtop[:, t:t + 1], None, ALU.mult)\
                        .then_inc(cur_ready, 1)
                per = steps.n - base
                assert per == STEPS_PER_LAYER, per
            steps.loop = 0
            steps.n = base + per * LAYERS

            ATT_STEPS = 2 * NCH * 3

            def emit(eng, gp, ga, gb, gt, par, slot0):
                attn_dve(eng, gp, ga, gb, gt, par, slot0, steps)

            dve.wait_ge(cur_ready, NT * (LAYERS + 1))
            steps(dve.tensor_tensor(x[:, :, :], x[:, :, :], xn[:, :, :], ALU.add))
            bodies(dve, emit, *L0, steps, ATT_STEPS)
            steps.sync()
            add_banks(dve, "proj0", lambda n, bank: (x[:, 4 * n:4 * n + 4, :], x[:, 4 * n:4 * n + 4, :],
                                                     bank.rearrange("p (t c) -> p t c", t=4)))
            dve.wait_ge(freed["proj0"], NCH)
            layer_norm(2, 1e-05, xn, None, 0)
            steps.sync()
            dve.nop().then_inc(xn_ready, 1)
            rms_rows(xn[:, :, :], 3, cnorm[:, 0, :])
            for n in range(NT):
                dve.wait_ge(done["mqa"], n + 1)
                bank = banks[n % 4]
                steps(dve.tensor_scalar(kqv[:, 1, n, 0:GL, :].rearrange("p g c -> p (g c)"), bank[:, 0:C],
                                        D ** -0.5, None, ALU.mult))
                for i, lo in ((0, C), (2, C + D)):
                    o = kqv[:, i, n, 0:GL, :].rearrange("p g (h d) -> p (g h) d", d=D)
                    steps(dve.tensor_copy(o, bank[:, lo:lo + D].unsqueeze(1).to_broadcast([P, H, D])))
                steps.sync()
                dve.nop().then_inc(freed["mqa"], 1)
            dve.nop().then_inc(xn_ready, 1)
            dve.wait_ge(freed["qkv1"], NT)
            head_norm(1, GL, hnorm[:, 2, :], 3, False, 1.1920929e-07, 0.0, D ** -0.5)
            head_norm(0, GL, hnorm[:, 3, :], 4, False, 1.1920929e-07, 0.0, 1.0)
            dve.nop().then_inc(kqv_ready, 1)
            bodies(dve, emit, *L1, steps, ATT_STEPS)
            steps.sync()
            add_banks(dve, "proja", lambda n, bank: (x[:, 4 * n:4 * n + 4, :], x[:, 4 * n:4 * n + 4, :],
                                                     bank.rearrange("p (t c) -> p t c", t=4)))
            Mz = 32
            add_banks(dve, "projb", lambda n, bank: (xn[:, 4 * n:4 * n + 4, Mz:C], xn[:, 4 * n:4 * n + 4, Mz:C],
                                                     bank.rearrange("p (t c) -> p t c", t=4)[:, :, Mz:C]))
            dve.wait_ge(freed["projb"], NCH)
            rms_rows(xn[:, :, :], 4, cnorm[:, 1, :])
            dve.nop().then_inc(xn_ready, 1)
            dve.wait_ge(freed["proja"], NCH)
            steps(dve.tensor_tensor(x[:, :, :], x[:, :, :], xn[:, :, :], ALU.add))
            dve.wait_ge(done["gate"], 1)
            sh = [P, NT, E1]
            r4 = lambda i: rt[:, i, 0:NT * E1].rearrange("p (t e) -> p t e", e=E1)
            g4 = banks[0][:, 0:NT * E1].rearrange("p (t e) -> p t e", e=E1)
            io = con["iota"][:, 0:E1].unsqueeze(1).to_broadcast(sh)
            big_f = 3.4028235e38
            steps(dve.tensor_scalar(r4(5), g4, -big_f, big_f, ALU.max, ALU.min))
            steps.sync()
            dve.nop().then_inc(freed["gate"], 1)
            steps(dve.tensor_reduce(small[:, 0, :], r4(5), AX.X, ALU.max))
            steps.sync()
            dve.tensor_tensor(r4(0), r4(5), bc(small[:, 0, :], sh, 2), ALU.subtract).then_inc(gate_dif, 1)
            dve.wait_ge(gate_exp, 1)
            steps(dve.tensor_reduce(small[:, 1, :], r4(1), AX.X, ALU.add))
            steps.sync()
            steps(dve.reciprocal(small[:, 2, :], small[:, 1, :]))
            steps.sync()
            steps(dve.tensor_tensor(r4(0), r4(1), bc(small[:, 2, :], sh, 2), ALU.mult))
            steps.sync()

            def top(src, dst):
                steps(dve.tensor_reduce(small[:, 0, :], src, AX.X, ALU.max))
                steps.sync()
                steps(dve.tensor_tensor(r4(2), src, bc(small[:, 0, :], sh, 2), ALU.is_lt))
                steps.sync()
                steps(dve.scalar_tensor_tensor(out=r4(3), in0=r4(2), scalar=64.0, in1=io, op0=ALU.mult, op1=ALU.add))
                steps.sync()
                steps(dve.tensor_reduce(small[:, 3, :], r4(3), AX.X, ALU.min))
                steps.sync()
                steps(dve.tensor_tensor(dst, io, bc(small[:, 3, :], sh, 2), ALU.is_equal))
                steps.sync()

            top(r4(0), r4(4))
            steps(dve.tensor_copy(small[:, 1, :], small[:, 0, :]))
            steps(dve.scalar_tensor_tensor(out=r4(5), in0=r4(4), scalar=-2.0, in1=r4(0), op0=ALU.mult, op1=ALU.add))
            steps.sync()
            top(r4(5), r4(1))
            steps(dve.tensor_tensor(r4(2), r4(1), r4(4), ALU.add))
            steps(dve.tensor_tensor(small[:, 2, :], small[:, 0, :], small[:, 1, :], ALU.add))
            steps.sync()
            steps(dve.tensor_scalar(small[:, 2, :], small[:, 2, :], 1e-08, None, ALU.add))
            steps.sync()
            steps(dve.reciprocal(small[:, 3, :], small[:, 2, :]))
            steps(dve.tensor_tensor(r4(3), r4(2), r4(0), ALU.mult))
            steps.sync()
            steps(dve.tensor_tensor(r4(4), r4(3), bc(small[:, 3, :], sh, 2), ALU.mult))
            steps.sync()
            wts = r4(4)
            for c in range(NCH):
                for u, (b, ko, ki, src, dst, f) in enumerate(MOE_UNITS):
                    if f != "times":
                        continue
                    n = NU * c + u
                    dve.wait_ge(moe_done, n + 1)
                    need(dve, moe_read, n)
                    dve.tensor_tensor(hidden[1][:, ko, :], hidden[1][:, ko, :], banks[n % 4], ALU.mult)\
                        .then_inc(moe_read, 1)
                for t in range(4):
                    n = 4 * c + t
                    dve.wait_ge(mix_done, n + 1)
                    for e in range(E1):
                        i = dve.scalar_tensor_tensor(out=x[:, n, Mz:C], in0=sq[n % 2][:, P * e + Mz:P * e + C],
                                                     scalar=wts[:, n, e:e + 1], in1=x[:, n, Mz:C],
                                                     op0=ALU.mult, op1=ALU.add)
                        if e == E1 - 1:
                            i.then_inc(mix_read, 1)
                        else:
                            steps(i)
                            steps.sync()


def constants():
    at, n = const_at()
    c = np.zeros((P, n), np.float32)
    r = np.arange(P)
    put = lambda k, v: c.__setitem__((slice(None), slice(*at[k])), v)
    put("ident", np.eye(P))
    put("mask_kq", np.where(r[:, None] > r[None, :], MASKED, 0.0))
    put("mask_qk", np.where(r[None, :] > r[:, None], MASKED, 0.0))
    put("before", (r[:, None] < r[None, :]))
    put("ones", 1.0)
    inv = (np.float32(1.0) / np.float32(10000.0) ** (np.arange(0, D, 2, dtype=np.float32) / np.float32(D)))
    freq = np.arange(T, dtype=np.float32)[:, None] * inv.astype(np.float32)[None, :]
    freq = np.concatenate([freq, freq], 1).astype(np.float64)
    sign = np.where(np.arange(D) < D // 2, -1.0, 1.0)
    tiled = lambda v: v.reshape(NT, P, D).transpose(1, 0, 2).reshape(P, NT * D)
    put("cos", tiled(np.cos(freq)))
    put("sin", tiled(np.sin(freq) * sign))
    e = np.arange(E0)
    put("upto", np.broadcast_to((e[None, :] <= e[:, None]).reshape(1, -1), (P, E0 * E0)))
    put("iota", np.broadcast_to(e, (P, E0)))
    put("tiles", np.broadcast_to(np.arange(NS), (P, NS)))
    return c


def lay_out(i):
    T_ = lambda w: np.ascontiguousarray(np.asarray(w).T)

    def blocks(w):
        w = T_(w)
        return [w[P * k:P * k + P, P * o:P * o + P] for k in range(w.shape[0] // P) for o in range(w.shape[1] // P)]

    f = {k: np.asarray(v) for k, v in i.items()}
    row = lambda n: f[n].reshape(1, -1)
    moe = []
    for n in ("e0_up", "e0_down", "e1_w1", "e1_w2", "e1_down", "e2_l1", "e2_l2", "e2_l3", "e2_l4",
              "e3_down", "e3_up", "e3_out"):
        moe += blocks(f["L1_ffn_" + n])
    return {
        "x": np.ascontiguousarray(f["L0_attn_x"].reshape(NT, P, C).transpose(1, 0, 2)),
        "consts": constants(),
        "w_kqv": T_(f["L0_attn_W_kqv"]), "w_proj": T_(f["L0_attn_W_proj"]),
        "w_mqa": np.ascontiguousarray(f["L1_attn_w_attn"]), "w_mproj": np.ascontiguousarray(f["L1_attn_w_proj"]),
        "w_qkv1": np.concatenate([T_(f["L1_ffn_wk"]), T_(f["L1_ffn_wq"]), T_(f["L1_ffn_wv"])], 1),
        "w_o": T_(f["L1_ffn_wo"]), "w_gate": T_(f["L1_ffn_gate_w"]),
        "routers": np.ascontiguousarray(f["L0_ffn_routers"].transpose(1, 0, 2).reshape(C, LAYERS * E0)),
        "hq0": row("L0_attn_q_norm_w"), "hk0": row("L0_attn_k_norm_w"),
        "hq1": row("L1_ffn_qn_w"), "hk1": row("L1_ffn_kn_w"),
        "n1": row("L1_ffn_n1_w"), "n2": row("L1_ffn_n2_w"),
        "w1": np.ascontiguousarray(f["L0_ffn_W1"].transpose(1, 0, 2).reshape(C, E0 * FF)),
        "w2": np.ascontiguousarray(f["L0_ffn_W2"].reshape(E0, KF, P, C).transpose(2, 0, 1, 3).reshape(P, E0 * FF)),
        "moe_w": np.ascontiguousarray(np.concatenate(moe, 1)),
    }


def kernel(**inputs):
    import concourse.bacc as bacc
    from concourse.bass_utils import run_bass_kernel_spmd

    arrays = lay_out(inputs)
    nc = bacc.Bacc("TRN2", target_bir_lowering=False, num_devices=1)
    args = {n: nc.dram_tensor(f"in_{n}", v.shape, mybir.dt.from_np(v.dtype), kind="ExternalInput").ap()
            for n, v in arrays.items()}
    out = nc.dram_tensor("out_0", (P, NT, C), F32, kind="ExternalOutput").ap()
    build(nc, args, out)
    r = run_bass_kernel_spmd(nc, [{f"in_{n}": v for n, v in arrays.items()}], core_ids=[0])
    got = np.asarray(r.results[0]["out_0"])
    return np.ascontiguousarray(got.transpose(1, 0, 2)).reshape(1, T, C)
```

```python
from contextlib import ExitStack

import numpy as np
import concourse.bass as bass
from concourse import mybir

F32 = mybir.dt.float32
BF16 = mybir.dt.bfloat16
I32 = mybir.dt.int32
ALU = mybir.AluOpType
ACT = mybir.ActivationFunctionType
AX = mybir.AxisListType

P = 128
T = 2048
NT = T // P
C = 128
H = 16
D = C // H
HG = 4
GL = H // HG
NCH = T // 512
E0, FF, LAYERS = 16, 512, 4
KF = FF // P
NS = (T - E0) // P + E0
E1, HID = 4, 256
OPR = 64
MROW = 6 * D
MASKED = -1.0e30

STEPS = [(c, j) for c in range(NCH) for j in range(4 * c + 4)]
COMBOS = [(t, kc) for t in range(NT) for kc in range(t // 4 + 1)]
NSTEP = len(STEPS)
CHUNK_END = [STEPS.index((c, 4 * c + 3)) for c in range(NCH)]
TURN_AT = {0: (1, "K"), 1: (1, "Q"), 7: (2, "K"), 8: (2, "Q"), 17: (3, "K"), 18: (3, "Q")}
TURN_NEXT_AT = {33: (0, "K"), 34: (0, "Q")}
MAX_AT = {CHUNK_END[c] + 1: c for c in range(NCH - 1)}
MAX_LAST_AT, OUT_LAST_AT = 1, 2
OUT_AT = {CHUNK_END[c] + 2: c for c in range(NCH - 1)}

WINDOWS = {(0, "gather"): (0, 7), (1, "scatter"): (7, 14), (1, "gather"): (14, 21),
           (2, "scatter"): (21, 28), (2, "gather"): (28, 34), (3, "scatter"): (34, NSTEP)}

CONSTS = dict(ident=128, mask_kq=128, mask_qk=128, before=128, ones=128, cos=NT * D, sin=NT * D,
              upto=E0 * E0, iota=E0, tiles=NS)


def const_at():
    at, out = 0, {}
    for name, n in CONSTS.items():
        out[name] = (at, at + n)
        at += n
    return out, at


def need(eng, sem, value):
    if isinstance(value, int) and value <= 0:
        return
    eng.wait_ge(sem, value)


class Steps:

    def __init__(self, eng, sem, passed=None):
        self.eng, self.sem, self.n, self.loop, self.passed = eng, sem, 0, 0, passed

    def __call__(self, ins):
        ins.then_inc(self.sem, 1)
        self.n += 1

    def sync(self):
        need(self.eng, self.sem, self.n + self.loop)
        if self.passed is not None and not isinstance(self.loop, int):
            self.eng.sem_inc(self.passed, 1)


def build(nc, a, out):
    cat, ncon = const_at()
    with ExitStack() as ctx:
        def sb(name, shape, dt=F32):
            return ctx.enter_context(nc.sbuf_tensor(name, shape, dt))

        def ps(name, shape):
            return ctx.enter_context(nc.psum_tensor(name, shape, F32))

        def sem(name):
            return ctx.enter_context(nc.semaphore(name))

        consts = sb("consts", [P, ncon])
        con = {k: consts[:, lo:hi] for k, (lo, hi) in cat.items()}
        ident = con["ident"]
        cos = con["cos"].rearrange("p (t d) -> p t d", d=D)
        sin = con["sin"].rearrange("p (t d) -> p t d", d=D)
        upto = con["upto"].rearrange("p (a b) -> p a b", b=E0)
        bcon = sb("bcon", [P, 5 * 128], BF16)
        identb, mask_kq, mask_qk, beforeb, onesb = (bcon[:, 128 * i:128 * i + 128] for i in range(5))
        x = sb("x", [P, NT, C])
        xn = sb("xn", [P, NT, C])
        xT = sb("xT", [P, T])
        y = sb("y", [P, NT, 2 * GL, HG * D])
        scratch = y[:, :, :, :].rearrange("p t g c -> p (t g c)")
        w_kqv = sb("w_kqv", [P, 3 * C])
        w_proj = sb("w_proj", [P, C])
        w_mqa = sb("w_mqa", [P, C + 2 * D])
        w_qkv1 = sb("w_qkv1", [P, 3 * C])
        w_mproj = sb("w_mproj", [P, C])
        w_o = sb("w_o", [P, C])
        w_gate = sb("w_gate", [P, E1])
        routers = sb("routers", [P, LAYERS * E0])
        hnorm = sb("hnorm", [P, 4, D])
        cnorm = sb("cnorm", [P, 2, C])
        stats = sb("stats", [P, NT, 6])
        mv = sb("mv", [P, NT, 2])
        rstd = sb("rstd", [P, NT])
        ss = sb("ss", [P, NT, H])

        GW = 3 * NT * HG * D
        big = sb("big", [P, 25600 + 2 * GL * GW])
        kqv = big[:, 25600:25600 + 2 * GL * GW].rearrange("p (g i t c) -> p g i t c", g=2 * GL, i=3, t=NT)
        EXPERTS_AT = 12288
        w1 = big[:, EXPERTS_AT:EXPERTS_AT + E0 * FF]
        w2 = big[:, EXPERTS_AT + E0 * FF:EXPERTS_AT + 2 * E0 * FF]
        TABLES_AT = EXPERTS_AT + 2 * E0 * FF
        at = [0]

        def part(nwords):
            lo = at[0]
            at[0] += nwords
            return big[:, lo:at[0]]

        qtok = part(NT * HG * OPR // 2).bitcast(BF16).rearrange("p (t h r) -> p t h r", h=HG, r=OPR)
        ktok = part(NT * HG * OPR // 2).bitcast(BF16).rearrange("p (t h r) -> p t h r", h=HG, r=OPR)
        pair_tok = (big[:, 0:T], big[:, T:2 * T])
        moe_w = big[:, 0:27 * P]
        def q_operand():
            return part(T).bitcast(BF16).rearrange("p (a t) -> p a t", a=2)

        def k_operand():
            return part(2 * T).bitcast(BF16).rearrange("p (h t) -> p h t", h=HG)

        qT, kT = [q_operand()], [k_operand()]
        kst = [part(512).bitcast(BF16).rearrange("p (a t) -> p a t", a=2) for _ in range(2)]
        rest = part(NT * HG * D).rearrange("p (t h d) -> p t h d", h=HG, d=D)
        mT = [part(256).bitcast(BF16) for _ in range(2)]
        assert at[0] <= EXPERTS_AT
        qT.append(q_operand())
        kT.append(k_operand())
        vpad = [part(NT * HG * 32).rearrange("p (t h d) -> p t h d", h=HG, d=32) for _ in range(2)]
        probs = [[w.rearrange("p (a t) -> p a t", a=2) for w in (part(1024), xT[:, 1024 * i:1024 * i + 1024])]
                 for i in range(2)]
        oT = [part(512) for _ in range(2)]
        assert at[0] <= 25600
        hidden = [big[:, 27 * P + 1024 * i:27 * P + 1024 * i + 1024].rearrange("p (k t) -> p k t", k=2)
                  for i in range(6)]
        mpart = sb("mpart", [P, 2, 4, HG, NCH])
        negm = sb("negm", [P, 2, 4, HG])
        mtok = sb("mtok", [P, 2, 4, HG, 2], BF16)
        rec = sb("rec", [P, 2, 4, HG])

        rt = big[:, TABLES_AT + C:TABLES_AT + C + 6 * NT * E0].rearrange("p (i n) -> p i n", i=6)
        ohb = sb("ohb", [P, NT, E0], BF16)
        wtop = sb("wtop", [P, NT])
        small = sb("small", [P, 4, NT])
        slot = sb("slot", [P, NT], I32)
        cnt_i = sb("cnt_i", [P, 2, E0], I32)
        ntile = sb("ntile", [P, 3, E0])
        owner_f = sb("owner_f", [P, NS])
        owner = sb("owner", [P, NS], I32)
        xs = scratch[:, 0:8 * C].rearrange("p (b c) -> p b c", c=C)
        w1s = scratch[:, 8 * C:16 * C].rearrange("p (b c) -> p b c", c=FF)
        hT = scratch[:, 16 * C:28 * C].rearrange("p (b c) -> p b c", c=FF)
        TILES_AT = TABLES_AT + C + 6 * NT * E0
        yo = big[:, TILES_AT:TILES_AT + 8 * C].rearrange("p (b c) -> p b c", c=C)
        xsT = big[:, TILES_AT + 8 * C:TILES_AT + 10 * C].rearrange("p (b c) -> p b c", c=P)
        assert TILES_AT + 10 * C <= 25600 + GL * GW
        zeros = big[:, TABLES_AT:TABLES_AT + C]
        xs_dram = nc.dram_tensor("xs_dram", [NS * P, C], F32, kind="Internal").ap()
        ys_dram = nc.dram_tensor("ys_dram", [NS * P, C], F32, kind="Internal").ap()

        st = [ps("st0", [P, 2, 512]), ps("st1", [P, 2, 512])]
        oacc = ps("oacc", [P, 512])
        sq = [ps("sq0", [P, 512]), ps("sq1", [P, 512])]
        misc = ps("misc", [P, 512])
        banks = [st[0][:, 0, :], st[0][:, 1, :], st[1][:, 0, :], st[1][:, 1, :]]

        consts_in = sem("consts_in")
        x_in = sem("x_in")
        w_in = sem("w_in")
        experts_in = sem("experts_in")
        moe_in = sem("moe_in")
        out_done = sem("out_done")
        dve_step = sem("dve_step")
        pool_step, pool_passed = sem("pool_step"), sem("pool_passed")
        consts_cast = sem("consts_cast")
        slots_zeroed = sem("slots_zeroed")
        var_ready, sd_ready = sem("var_ready"), sem("sd_ready")
        cur_ready = sem("cur_ready")
        DENSE = {"xT0": 4, "kqv0": NT, "yT0": 4, "proj0": 4, "xT1": 4, "mqa": NT, "hT1": 4, "qkv1": NT,
                 "yTa": 4, "proja": 4, "yTb": 4, "projb": 4, "xfT": 4, "gate": 1}
        done = {k: sem(f"{k}_done") for k in DENSE}
        freed = {k: sem(f"{k}_read") for k in DENSE}
        norm_sq, norm_sd = sem("norm_sq"), sem("norm_sd")
        kqv_ready = sem("kqv_ready")
        xn_ready = sem("xn_ready")
        curT_done, curT_read = sem("curT_done"), sem("curT_read")
        logits_done, exp_ready = sem("logits_done"), sem("exp_ready")
        dif_ready, onehot_ready, rank_done = sem("dif_ready"), sem("onehot_ready"), sem("rank_done")
        slot_ready, owner_ready = sem("slot_ready"), sem("owner_ready")
        scattered, gathered = sem("scattered"), sem("gathered")
        xs_loaded = [sem(f"xs_loaded{i}") for i in range(2)]
        ys_stored = [sem(f"ys_stored{i}") for i in range(2)]
        xsT_done, xsT_read = sem("xsT_done"), sem("xsT_read")
        w1_picked, up_done, silu_done = sem("w1_picked"), sem("up_done"), sem("silu_done")
        down_done, down_read = sem("down_done"), sem("down_read")
        pads_zeroed = sem("pads_zeroed")
        vpad_set = sem("vpad_set")
        qk_packed, v_packed = sem("qk_packed"), sem("v_packed")
        turned, turn_read = sem("turned"), sem("turn_read")
        k_loaded = [sem(f"k_loaded{c}") for c in range(NCH)]
        m_loaded = [sem(f"m_loaded{c}") for c in range(NCH)]
        sq_done, max_done = sem("sq_done"), sem("max_done")
        negm_ready, mT_done, mT_read = sem("negm_ready"), sem("mT_done"), sem("mT_read")
        st_done, exp_done, pv_done = sem("st_done"), sem("exp_done"), sem("pv_done")
        o_read, oT_done, y_done = sem("o_read"), sem("oT_done"), sem("y_done")
        wts_ready, gate_exp, gate_dif = sem("wts_ready"), sem("gate_exp"), sem("gate_dif")
        moe_done, moe_read = sem("moe_done"), sem("moe_read")
        mix_done, mix_read, gated = sem("mix_done"), sem("mix_read"), sem("gated")

        block = ctx.enter_context(nc.Block())

        def tok(tile):
            return slice(tile * P, tile * P + P)

        def group(i, slot_):
            if isinstance(slot_, int):
                return kqv[:, slot_, i, :, :].rearrange("p t (h d) -> p t h d", d=D)
            return kqv[:, bass.ds(slot_, 1), i, :, :].rearrange("p a t (h d) -> p (a t) h d", d=D)

        def bodies(eng, emit, first, last, slot0, steps=None, per_pair=0):
            emit(eng, None, first, first + 1, first + 2, first % 2, slot0)
            g = first + 1
            pairs = (last - 1 - g) // 2
            if pairs > 1:
                with eng.Fori(0, pairs) as i:
                    if steps is not None:
                        base, steps.loop = steps.n, i * per_pair
                    for b in range(2):
                        n = g + b + i * 2
                        emit(eng, n - 1, n, n + 1, n + 2, (g + b) % 2, slot0)
                if steps is not None:
                    assert steps.n - base == per_pair, steps.n - base
                    steps.n, steps.loop = base + per_pair * pairs, 0
                g += 2 * pairs
            while g <= last:
                emit(eng, g - 1, g, g + 1 if g < last else None, g + 2 if g + 1 < last else None, g % 2, slot0)
                g += 1
            emit(eng, last, None, None, None, 0, slot0)

        L0 = (0, GL - 1, -GL)
        L1 = (GL, 3 * GL - 1, GL)

        def sp_attention(sp, gp, ga, gb, gt, par, slot0, part_=None):
            if gb is None and ga is None:
                return
            pb = None if gb is None else nxt(ga, par, gb)
            for s in range(*(part_ or (0, NSTEP))):
                if ga is None and s == 0:
                    keys_to(sp, gb, pb, 0)
                if gb is not None:
                    if s in TURN_AT and TURN_AT[s][1] == "K":
                        keys_to(sp, gb, pb, TURN_AT[s][0])
                    if s in MAX_AT:
                        max_to(sp, gb, pb, MAX_AT[s])
                if ga is not None and s == MAX_LAST_AT:
                    max_to(sp, ga, par, NCH - 1)
                if gt is not None and s in TURN_NEXT_AT and TURN_NEXT_AT[s][1] == "K":
                    keys_to(sp, gt, 1 - pb, 0)

        def nxt(ga, par, gb):
            return gb % 2 if ga is None else 1 - par

        def fill(emit, eng, l, move):
            if (l, move) in WINDOWS:
                emit(eng, None, None, 0, None, 0, -GL, WINDOWS[l, move])

        def keys_to(sp, g, par, c):
            sp.wait_ge(turn_read, 8 * g + 2 * c + 1)
            cols = slice(512 * c, 512 * c + 512)
            for b in range(2):
                rows = slice(64 * b, 64 * b + 64)
                sp.dma_start(kT[par][rows, b:HG:2, cols], kst[c % 2][rows, :, :]).then_inc(k_loaded[c], 16)

        def max_to(sp, g, par, c):
            sp.wait_ge(mT_read, 4 * g + c + 1)
            for h in range(HG):
                row = 64 * (h % 2) + MROW
                sp.dma_start(qT[par][row:row + 2, h // 2, 512 * c:512 * c + 512],
                             mT[c % 2][2 * h:2 * h + 2, :]).then_inc(m_loaded[c], 16)

        QUAD = 4
        NQ = -(-NS // QUAD)
        xs_tiles = xs_dram.rearrange("(s p) c -> p s c", p=P)
        ys_tiles = ys_dram.rearrange("(s p) c -> p s c", p=P)

        def quad_size(q):
            return min(QUAD, NS - QUAD * q)

        def moves(l, q):
            return len(range(q % 2, NQ, 2)) * l + q // 2 + 1

        @block.sync
        def _(sp):
            sp.dma_start(x[:, :, :], a["x"]).then_inc(x_in, 16)
            sp.dma_start(consts[:, :], a["consts"]).then_inc(consts_in, 16)
            for dst, name in ((w_kqv, "w_kqv"), (w_proj, "w_proj"), (w_mqa, "w_mqa"), (w_qkv1, "w_qkv1"),
                              (w_mproj, "w_mproj"), (w_o, "w_o"), (w_gate, "w_gate"), (routers, "routers")):
                sp.dma_start(dst[:, :], a[name]).then_inc(w_in, 16)
            for i, name in enumerate(("hq0", "hk0", "hq1", "hk1")):
                sp.dma_start(hnorm[:, i, :], a[name].to_broadcast([P, D])).then_inc(w_in, 16)
            for i, name in enumerate(("n1", "n2")):
                sp.dma_start(cnorm[:, i, :], a[name].to_broadcast([P, C])).then_inc(w_in, 16)
            for q in range(4):
                n = E0 * FF // 4
                sp.dma_start(w1[:, n * q:n * q + n], a["w1"][:, n * q:n * q + n]).then_inc(experts_in, 16)
                sp.dma_start(w2[:, n * q:n * q + n], a["w2"][:, n * q:n * q + n]).then_inc(experts_in, 16)
            for l in range(LAYERS):
                fill(sp_attention, sp, l, "scatter")
                sp.wait_ge(scattered, 256 * (l + 1))
                for q in range(NQ + 2):
                    if q < NQ:
                        if q >= 2:
                            sp.wait_ge(xsT_done, NS * l + QUAD * (q - 1))
                        lo, n = QUAD * q, quad_size(q)
                        sp.dma_start(xs[:, QUAD * (q % 2):QUAD * (q % 2) + n, :],
                                     xs_tiles[:, lo:lo + n, :]).then_inc(xs_loaded[q % 2], 16)
                    if q >= 2:
                        lo, n = QUAD * (q - 2), quad_size(q - 2)
                        sp.wait_ge(down_read, NS * l + (lo + n))
                        sp.dma_start(ys_tiles[:, lo:lo + n, :], yo[:, QUAD * (q % 2):QUAD * (q % 2) + n, :])\
                          .then_inc(ys_stored[q % 2], 16)
                fill(sp_attention, sp, l, "gather")
            keys_to(sp, 1, 1, 0)
            bodies(sp, sp_attention, *L0)
            sp_attention(sp, None, None, GL, GL + 1, 0, GL)
            bodies(sp, sp_attention, *L1)
            sp.wait_ge(turned, 8 * 3 * GL)
            sp.dma_start(moe_w, a["moe_w"]).then_inc(moe_in, 16)
            sp.wait_ge(mix_read, NT)
            sp.dma_start(out, x[:, :, :]).then_inc(out_done, 16)
            sp.wait_ge(out_done, 16)

        def pack(pool, steps, g, slot_, which):
            src = group(1 if which == "Q" else 0, slot_)
            dst = qtok if which == "Q" else ktok
            places = ((0, 1, 3), (2, 4), (5,)) if which == "Q" else ((0, 2, 5), (1, 4), (3,))
            left = src
            for i, cols in enumerate(places):
                for col in cols:
                    steps(pool.tensor_copy(dst[:, :, :, D * col:D * col + D], left))
                if i < 2:
                    r = rest
                    steps.sync()
                    steps(pool.tensor_tensor(r, left, dst[:, :, :, D * cols[0]:D * cols[0] + D], ALU.subtract))
                    steps.sync()
                    left = r

        def pool_qk(pool, steps, g, slot_):
            need(pool, turned, 8 * g)
            steps.sync()
            pack(pool, steps, g, slot_, "K")
            steps.sync()
            pack(pool, steps, g, slot_, "Q")
            steps.sync()
            pool.nop().then_inc(qk_packed, 1)

        def pool_v(pool, steps, g, par, slot_):
            if not isinstance(g, int) or g >= 2:
                pool.wait_ge(pv_done, NSTEP * (g - 1))
                pool.sem_inc(pool_passed, 1)
            pool.tensor_copy(vpad[par][:, :, :, 0:D], group(2, slot_)).then_inc(v_packed, 1)

        PACK_STEPS = 2 * 8

        @block.gpsimd
        def _(pool):
            steps = Steps(pool, pool_step, passed=pool_passed)
            steps(pool.memset(zeros, 0.0))
            steps.sync()
            pool.dma_start(xs_dram.rearrange("(s p) c -> p s c", p=P),
                           zeros.unsqueeze(1).to_broadcast([P, NS, C])).then_inc(slots_zeroed, 16)

            def zero_pad(par):
                for b in range(2):
                    steps.sync()
                    steps(pool.memset(kT[par][64 * (1 - b):64 * (1 - b) + 64, b:HG:2, :], 0.0))
                steps.sync()

            zero_pad(0)
            pool.nop().then_inc(pads_zeroed, 1)
            pool.wait_ge(slots_zeroed, 16)
            for l in range(LAYERS):
                pool.wait_ge(slot_ready, l + 1)
                for t in range(NT):
                    pool.indirect_dma_start(xs_dram, bass.IndirectOffsetOnAxis(ap=slot[:, t:t + 1], axis=0),
                                            xn[:, t, :], None).then_inc(scattered, 16)
                if l == 0:
                    pool.wait_ge(kqv_ready, 1)
                    steps(pool.memset(qtok[:, :, :, MROW:OPR], 0.0))
                    steps(pool.memset(ktok[:, :, :, MROW:MROW + 2], 1.0))
                    steps(pool.memset(ktok[:, :, :, MROW + 2:OPR], 0.0))
                    pool_qk(pool, steps, 0, GL)
                if l == 2:
                    pool_qk(pool, steps, 1, GL + 1)
                pool.wait_ge(scattered, 256 * (l + 1))
                for q in (NQ - 2, NQ - 1):
                    pool.wait_ge(ys_stored[q % 2], 16 * moves(l, q))
                for t in range(NT):
                    pool.indirect_dma_start(xn[:, t, :], None, ys_dram,
                                            bass.IndirectOffsetOnAxis(ap=slot[:, t:t + 1], axis=0))\
                        .then_inc(gathered, 16)
            pool.wait_ge(down_done, NS * LAYERS)
            zero_pad(1)
            pool.nop().then_inc(pads_zeroed, 1)
            pool_v(pool, steps, 0, 0, GL)

            def emit(eng, gp, ga, gb, gt, par, slot0):
                if gb is not None:
                    pool_v(eng, steps, gb, nxt(ga, par, gb), gb - slot0)
                if gt is not None:
                    pool_qk(eng, steps, gt, gt - slot0)

            bodies(pool, emit, *L0, steps, 2 * PACK_STEPS)
            pool.wait_ge(kqv_ready, 2)
            pool_qk(pool, steps, GL, 0)
            pool_v(pool, steps, GL, 0, 0)
            pool_qk(pool, steps, GL + 1, 1)
            bodies(pool, emit, *L1, steps, 2 * PACK_STEPS)

        prev = []

        def take_misc(pe, next_reader):
            for s_, v in prev:
                need(pe, s_, v)
            prev[:] = [next_reader]

        def attn_pe(pe, gp, ga, gb, gt, par, slot0, part_=None):
            pb = nxt(ga, par, gb) if gb is not None else None

            def turn(g, c, kind):
                n = 8 * g + 2 * c + (kind == "Q")
                take_misc(pe, (turn_read, n + 1))
                need(pe, qk_packed, g + 1)
                view = misc[:, :].bitcast(BF16).rearrange("p (a t) -> p a t", a=2)
                src = ktok if kind == "K" else qtok
                for a_ in range(2):
                    for t in range(4):
                        m = pe.transpose(view[:, a_, tok(t)],
                                         src[:, 4 * c + t, 2 * a_:2 * a_ + 2, :].rearrange("p h r -> p (h r)"),
                                         identb)
                m.then_inc(turned, 1)

            def turn_max(g, c):
                take_misc(pe, (mT_read, 4 * g + c + 1))
                pe.wait_ge(negm_ready, 4 * g + c + 1)
                view = misc[0:2 * HG, :].bitcast(BF16)
                for t in range(4):
                    m = pe.transpose(view[:, tok(t)], mtok[:, c % 2, t, :, :].rearrange("p h e -> p (h e)"),
                                     identb)
                m.then_inc(mT_done, 1)

            def turn_out(g, c):
                take_misc(pe, (y_done, 4 * g + c + 1))
                pe.wait_ge(o_read, 4 * g + c + 1)
                for t in range(4):
                    m = pe.transpose(misc[:, tok(t)], oT[c % 2][:, tok(t)], ident)
                m.then_inc(oT_done, 1)

            def scores_t(g, gpar, s, a_):
                c, j = STEPS[s]
                off = 128 * max(0, j - 4 * c)
                if j == 0:
                    pe.wait_ge(m_loaded[c], 64 * (g + 1))
                need(pe, exp_done, 2 * NSTEP * g + (2 * (s - 1) + a_ + 1))
                for b in range(2):
                    o = st[a_][:, b, :]
                    m = pe.matmul(o[:, off:512], kT[gpar][:, 2 * a_ + b, tok(j)],
                                  qT[gpar][:, a_, 512 * c + off:512 * c + 512], start=True, stop=j < 4 * c)
                    if j >= 4 * c:
                        m = pe.matmul(o[:, off:off + 128], identb, mask_kq, start=False, stop=True)
                m.then_inc(st_done, 1)

            def scores(g, gpar, s, h):
                t, kc = COMBOS[s]
                c = t // 4
                if t % 4 == 0 and kc == 0 and h == 0:
                    pe.wait_ge(turn_read, 8 * g + 2 * c + 2)
                    pe.wait_ge(k_loaded[c], 32 * (g + 1))
                n = min(512, (t + 1) * P - 512 * kc)
                need(pe, max_done, HG * NSTEP * g + (HG * s + h - 1))
                o = sq[h % 2]
                m = pe.matmul(o[:, 0:n], qT[gpar][:, h // 2, tok(t)],
                              kT[gpar][:, h, 512 * kc:512 * kc + n], start=True, stop=kc < c)
                if kc == c:
                    m = pe.matmul(o[:, n - 128:n], identb, mask_qk, start=False, stop=True)
                m.then_inc(sq_done, 1)

            def weigh(g, gpar, s):
                c, j = STEPS[s]
                off = 128 * max(0, j - 4 * c)
                pe.wait_ge(exp_done, 2 * NSTEP * g + (2 * s + 2))
                if s == 0:
                    pe.wait_ge(vpad_set, 3)
                    pe.wait_ge(v_packed, g + 1)
                if j == 0:
                    need(pe, o_read, 4 * g + c)
                for h in range(HG):
                    m = pe.matmul(oacc[32 * h:32 * h + 32, off:512], vpad[gpar][:, j, h, :],
                                  probs[s % 2][h // 2][:, h % 2, off:512], start=(j == 0), stop=(j == 4 * c + 3),
                                  tile_position=(0, 32 * h))
                m.then_inc(pv_done, 1)

            if ga is None and gb is None:
                prev[:] = [(y_done, 4 * gp + 3)]
                turn_out(gp, NCH - 1)
                return
            if ga is not None and gb is None:
                prev[:] = [(y_done, 4 * gp + 3)]
            elif ga is not None:
                prev[:] = [(turn_read, 8 * gb + 2)]
            lo, hi = part_ or (0, NSTEP)
            if ga is None and lo == 0:
                turn(gb, 0, "K")
                turn(gb, 0, "Q")
            for s in range(lo, hi):
                units = iter(range(HG))
                if gb is not None:
                    scores(gb, pb, s, next(units))
                for a_ in range(2):
                    if ga is not None and s + 1 < NSTEP:
                        scores_t(ga, par, s + 1, a_)
                    elif ga is not None and gb is not None:
                        scores_t(gb, pb, 0, a_)
                    if gb is not None:
                        scores(gb, pb, s, next(units))
                if ga is not None:
                    weigh(ga, par, s)
                if gb is not None:
                    scores(gb, pb, s, next(units))
                if gb is not None and s in TURN_AT:
                    turn(gb, *TURN_AT[s])
                if gb is not None and s in MAX_AT:
                    turn_max(gb, MAX_AT[s])
                if ga is not None and s == MAX_LAST_AT:
                    turn_max(ga, NCH - 1)
                if ga is not None and s in OUT_AT:
                    turn_out(ga, OUT_AT[s])
                if gp is not None and s == OUT_LAST_AT:
                    turn_out(gp, NCH - 1)
                if gt is not None and s in TURN_NEXT_AT:
                    turn(gt, *TURN_NEXT_AT[s])
            if ga is None and part_ == (NSTEP, NSTEP):
                turn(gt, 0, "K")
                turn(gt, 0, "Q")
            if ga is None and lo in (NSTEP, 0) and hi == NSTEP:
                for a_ in range(2):
                    scores_t(gb, pb, 0, a_)

        def dense(pe, name, emit, before=None):
            if before is not None:
                pe.wait_ge(freed[before], DENSE[before])
            for n in range(DENSE[name]):
                if n >= 4:
                    pe.wait_ge(freed[name], n - 3)
                emit(n, banks[n % 4]).then_inc(done[name], 1)

        def turn_tiles(pe, src):
            def emit(n, bank):
                for t in range(4):
                    m = pe.transpose(bank[:, tok(t)], src(4 * n + t), ident)
                return m
            return emit

        def times(pe, w, cols):
            def emit(n, bank):
                return pe.matmul(bank[:, 0:cols], xT[:, tok(n)], w, start=True, stop=True)
            return emit

        def times4(pe, w):
            def emit(n, bank):
                for t in range(4):
                    m = pe.matmul(bank[:, tok(t)], xT[:, tok(4 * n + t)], w, start=True, stop=True)
                return m
            return emit

        UP0, DN0, W1_, W2_, DN1 = 0, 2, 4, 6, 8
        L1_, L2_, L3_, L4_, DN3, UP3, OUT3 = 10, 12, 16, 20, 22, 23, 25
        MOE = [(W1_, 2, 1, None, 1, "silu"), (W2_, 2, 1, None, 1, "times"),
               (UP0, 2, 1, None, 0, "gelu"), (L1_, 2, 1, None, 2, "gelu"), (DN3, 1, 1, None, 4, "gelu"),
               (L2_, 2, 2, 2, 3, "gelu"), (UP3, 2, 1, 4, 5, "gelu"), (L3_, 2, 2, 3, 2, "gelu")]
        MOE_UNITS = [(b + k_out * 1, k_out, ki, src, dst, f) for b, ko, ki, src, dst, f in MOE for k_out in range(ko)]
        NU = len(MOE_UNITS)
        LASTS = [(DN0, 0), (DN1, 1), (L4_, 2), (OUT3, 5)]

        def block_w(b):
            return moe_w[:, P * b:P * b + P]

        def unit_ready(src, u):
            _, _, _, s, d, _ = MOE_UNITS[u]
            ns = [v for v in range(u) if MOE_UNITS[v][4] == s and s is not None]
            return max(ns) + 1 if ns else 0

        def moe_pe(pe):
            pe.wait_ge(moe_in, 16)
            mbanks = banks
            for c in range(NCH):
                cols = slice(512 * c, 512 * c + 512)
                for u, (b, ko, ki, src, dst, f) in enumerate(MOE_UNITS):
                    n = NU * c + u
                    need(pe, moe_read, n - 3)
                    need(pe, moe_read, NU * c + unit_ready(None, u) if src is not None else 0)
                    for k in range(ki):
                        rhs = xT[:, cols] if src is None else hidden[src][:, k, :]
                        blk = b + (k * 2 if ki == 2 else 0)
                        m = pe.matmul(mbanks[n % 4], block_w(blk), rhs, start=(k == 0), stop=(k == ki - 1))
                    m.then_inc(moe_done, 1)
                pe.wait_ge(moe_read, NU * (c + 1))
                for t in range(4):
                    n = 4 * c + t
                    need(pe, mix_read, n - 1)
                    o = sq[n % 2]
                    for e, (b, src) in enumerate(LASTS):
                        for k in range(2):
                            m = pe.matmul(o[:, tok(e)], hidden[src][:, k, tok(t)], block_w(b + k),
                                          start=(k == 0), stop=(k == 1))
                    m.then_inc(mix_done, 1)

        @block.tensor
        def _(pe):
            pe.wait_ge(consts_in, 16)
            pe.wait_ge(cur_ready, NT)
            dense(pe, "xT0", turn_tiles(pe, lambda t: xn[:, t, :]))
            pe.wait_ge(freed["xT0"], 4)
            pe.wait_ge(w_in, 16 * 14)
            pe.wait_ge(consts_cast, 1)
            for l in range(LAYERS):
                if l > 0:
                    pe.wait_ge(cur_ready, NT * (l + 1))
                    for n in range(4):
                        for t in range(4):
                            m = pe.transpose(banks[n][:, tok(t)], xn[:, 4 * n + t, :], ident)
                        m.then_inc(curT_done, 1)
                    pe.wait_ge(curT_read, 4 * l)
                for t in range(NT):
                    m = pe.matmul(oacc[:, E0 * t:E0 * t + E0], xT[:, tok(t)], routers[:, l * E0:l * E0 + E0],
                                  start=True, stop=True)
                m.then_inc(logits_done, 1)
                if l == 0:
                    dense(pe, "kqv0", times(pe, w_kqv[:, :], 3 * C), "xT0")
                    pe.wait_ge(freed["kqv0"], NT)
                pe.wait_ge(onehot_ready, l + 1)
                flat = ohb[:, :, :].rearrange("p t e -> p (t e)")
                pe.matmul(banks[0][:, 0:NT * E0], beforeb, flat, start=True, stop=False)
                for t in range(NT - 1):
                    pe.matmul(banks[0][:, E0 * (t + 1):NT * E0], onesb,
                              ohb[:, t:t + 1, :].to_broadcast([P, NT - 1 - t, E0]),
                              start=False, stop=(t == NT - 2))
                for t in range(NT):
                    m = pe.matmul(banks[1][:, 0:E0], onesb, ohb[:, t, :], start=(t == 0), stop=(t == NT - 1))
                m.then_inc(rank_done, 1)
                fill(attn_pe, pe, l, "scatter")
                pe.wait_ge(owner_ready, l + 1)
                need(pe, max_done, HG * max([0] + [hi for (k, w), (lo, hi) in WINDOWS.items()
                                                   if k < l or (k == l and w == "scatter")]))
                if l == 0:
                    pe.wait_ge(experts_in, 16 * 8)
                expert = {}
                for s in range(NS + 3):
                    if s < NS:
                        i = s
                        expert[i] = pe.value_load(owner[0:1, i:i + 1], min_val=0, max_val=E0 - 1)
                        if i % QUAD == 0:
                            pe.wait_ge(xs_loaded[i // QUAD % 2], 16 * moves(l, i // QUAD))
                        if i >= 2:
                            pe.wait_ge(xsT_read, NS * l + (i - 1))
                        pe.transpose(banks[i % 2][:, 0:P], xs[:, i % 8, :], ident).then_inc(xsT_done, 1)
                    if 0 <= s - 1 < NS:
                        i = s - 1
                        pe.wait_ge(xsT_read, NS * l + (i + 1))
                        pe.wait_ge(w1_picked, NS * l + (i + 1))
                        if i >= 2:
                            pe.wait_ge(silu_done, NS * l + (i - 1))
                        for k in range(KF):
                            m = pe.matmul(banks[2 + i % 2][:, tok(k)], w1s[:, i % 2, tok(k)], xsT[:, i % 2, :],
                                          start=True, stop=True)
                        m.then_inc(up_done, 1)
                    if 0 <= s - 3 < NS:
                        i = s - 3
                        e = expert.pop(i)
                        pe.wait_ge(silu_done, NS * l + (i + 1))
                        if i >= 2:
                            pe.wait_ge(down_read, NS * l + (i - 1))
                        for k in range(KF):
                            m = pe.matmul(sq[i % 2][:, 0:C], hT[:, i % 3, tok(k)],
                                          w2[:, bass.ds(e * FF + k * C, C)], start=(k == 0), stop=(k == KF - 1))
                        m.then_inc(down_done, 1)
                pe.wait_ge(down_read, NS * (l + 1))
                if l == 0:
                    pe.wait_ge(pads_zeroed, 1)
                fill(attn_pe, pe, l, "gather")
            pe.wait_ge(pads_zeroed, 2)
            attn_pe(pe, None, None, 0, 1, 0, -GL, (NSTEP, NSTEP))
            bodies(pe, attn_pe, *L0)
            pe.wait_ge(y_done, 4 * GL)
            dense(pe, "yT0", turn_tiles(pe, lambda t: y[:, t, GL:2 * GL, :].rearrange("p g c -> p (g c)")))
            pe.wait_ge(freed["yT0"], 4)
            dense(pe, "proj0", times4(pe, w_proj[:, :]), "yT0")
            pe.wait_ge(xn_ready, 1)
            dense(pe, "xT1", turn_tiles(pe, lambda t: xn[:, t, :]), "proj0")
            pe.wait_ge(freed["xT1"], 4)
            dense(pe, "mqa", times(pe, w_mqa[:, :], C + 2 * D), "xT1")
            pe.wait_ge(xn_ready, 2)
            dense(pe, "hT1", turn_tiles(pe, lambda t: scratch[:, tok(t)]), "mqa")
            pe.wait_ge(freed["hT1"], 4)
            dense(pe, "qkv1", times(pe, w_qkv1[:, :], 3 * C), "hT1")
            pe.wait_ge(freed["qkv1"], NT)
            attn_pe(pe, None, None, GL, GL + 1, 0, GL)
            bodies(pe, attn_pe, *L1)
            pe.wait_ge(y_done, 12 * GL)
            dense(pe, "yTa", turn_tiles(pe, lambda t: y[:, t, 0:GL, :].rearrange("p g c -> p (g c)")))
            pe.wait_ge(freed["yTa"], 4)
            dense(pe, "proja", times4(pe, w_mproj[:, :]), "yTa")
            dense(pe, "yTb", turn_tiles(pe, lambda t: y[:, t, GL:2 * GL, :].rearrange("p g c -> p (g c)")), "proja")
            pe.wait_ge(freed["yTb"], 4)
            dense(pe, "projb", times4(pe, w_o[:, :]), "yTb")
            pe.wait_ge(xn_ready, 3)
            dense(pe, "xfT", turn_tiles(pe, lambda t: scratch[:, tok(t)]), "projb")
            pe.wait_ge(freed["xfT"], 4)

            def gate(n, bank):
                for t in range(NT):
                    m = pe.matmul(bank[:, E1 * t:E1 * t + E1], xT[:, tok(t)], w_gate[:, :], start=True, stop=True)
                return m
            dense(pe, "gate", gate, "xfT")
            pe.wait_ge(freed["gate"], 1)
            moe_pe(pe)

        def attn_act(act, gp, ga, gb, gt, par, slot0, part_=None):
            pb = nxt(ga, par, gb) if gb is not None else None

            def read_turn(g, gpar, c, kind):
                n = 8 * g + 2 * c + (kind == "Q")
                act.wait_ge(turned, n + 1)
                view = misc[:, :].bitcast(BF16).rearrange("p (a t) -> p a t", a=2)
                if kind == "K":
                    need(act, k_loaded[(c - 2) % NCH], 32 * (g + 1) if c >= 2 else 32 * g)
                    act.activation(kst[c % 2], view, ACT.Copy).then_inc(turn_read, 1)
                else:
                    act.activation(qT[gpar][:, :, 512 * c:512 * c + 512], view, ACT.Copy).then_inc(turn_read, 1)

            def read_max(g, c):
                act.wait_ge(mT_done, 4 * g + c + 1)
                need(act, m_loaded[(c - 2) % NCH], 64 * (g + 1) if c >= 2 else 64 * g)
                act.activation(mT[c % 2][0:2 * HG, :], misc[0:2 * HG, :].bitcast(BF16)[:, 0:512], ACT.Copy)\
                   .then_inc(mT_read, 1)

            def read_out(g, c):
                act.wait_ge(pv_done, NSTEP * g + (CHUNK_END[c] + 1))
                need(act, oT_done, 4 * g + (c - 1))
                act.activation(oT[c % 2], oacc[:, :], ACT.Copy).then_inc(o_read, 1)

            def exp(g, s):
                c, j = STEPS[s]
                off = 128 * max(0, j - 4 * c)
                for a_ in range(2):
                    act.wait_ge(st_done, 2 * NSTEP * g + (2 * s + a_ + 1))
                    need(act, pv_done, NSTEP * g + (s - 1))
                    act.activation(probs[s % 2][a_][:, :, off:512], st[a_][:, :, off:512], ACT.Exp)\
                       .then_inc(exp_done, 1)

            if gb is None and ga is None:
                read_out(gp, NCH - 1)
                return
            lo, hi = part_ or (0, NSTEP)
            if ga is None and lo == 0:
                read_turn(gb, pb, 0, "K")
                read_turn(gb, pb, 0, "Q")
            late = int(ga is not None)
            for s in range(lo, hi + late):
                if ga is not None and s < NSTEP:
                    exp(ga, s)
                u = s - late
                if gp is not None and s == 0:
                    read_out(gp, NCH - 1)
                if gb is not None and u in TURN_AT:
                    read_turn(gb, pb, *TURN_AT[u])
                if gb is not None and u in MAX_AT:
                    read_max(gb, MAX_AT[u])
                if ga is not None and u == MAX_LAST_AT:
                    read_max(ga, NCH - 1)
                if ga is not None and u in CHUNK_END[:-1]:
                    read_out(ga, CHUNK_END.index(u))
                if gt is not None and u in TURN_NEXT_AT:
                    read_turn(gt, 1 - pb, *TURN_NEXT_AT[u])
            if ga is None and part_ == (NSTEP, NSTEP):
                read_turn(gt, 1 - pb, 0, "K")
                read_turn(gt, 1 - pb, 0, "Q")

        def copy_dense(act, name, dst):
            for n in range(DENSE[name]):
                act.wait_ge(done[name], n + 1)
                o, i = dst(n, banks[n % 4])
                act.activation(o, i, ACT.Copy).then_inc(freed[name], 1)

        def to_xT(n, bank):
            return xT[:, 512 * n:512 * n + 512], bank

        @block.scalar
        def _(act):
            act.wait_ge(var_ready, 1)
            act.activation(rstd[:, :], mv[:, :, 1], ACT.Sqrt).then_inc(sd_ready, 1)
            copy_dense(act, "xT0", to_xT)

            def kqv_out(n, bank):
                return (kqv[:, GL:2 * GL, :, n, :].rearrange("p g i c -> p i g c"),
                        bank[:, 0:3 * C].rearrange("p (i g c) -> p i g c", i=3, g=GL))
            copy_dense(act, "kqv0", kqv_out)
            for l in range(LAYERS):
                for n in range(4):
                    if l == 0:
                        break
                    act.wait_ge(curT_done, 4 * (l - 1) + (n + 1))
                    act.activation(xT[:, 512 * n:512 * n + 512], banks[n], ACT.Copy).then_inc(curT_read, 1)
                act.wait_ge(dif_ready, l + 1)
                act.activation(rt[:, 1, :], rt[:, 0, :], ACT.Exp).then_inc(exp_ready, 1)
                for n in range(2):
                    if l == 0:
                        act.wait_ge(norm_sq, n + 1)
                        act.activation(ss[:, :, :], ss[:, :, :], ACT.Sqrt).then_inc(norm_sd, 1)
                fill(attn_act, act, l, "scatter")
                for s in range(NS + 2):
                    if s < NS:
                        act.wait_ge(up_done, NS * l + (s + 1))
                        if s >= 3:
                            act.wait_ge(down_done, NS * l + (s - 2))
                        act.activation(hT[:, s % 3, :], banks[2 + s % 2], ACT.Silu).then_inc(silu_done, 1)
                    if s >= 2:
                        i = s - 2
                        act.wait_ge(down_done, NS * l + (i + 1))
                        if i >= 2 * QUAD and i % QUAD == 0:
                            act.wait_ge(ys_stored[i // QUAD % 2], 16 * (moves(l, i // QUAD) - 1))
                        act.activation(yo[:, i % 8, :], sq[i % 2][:, 0:C], ACT.Copy).then_inc(down_read, 1)
                fill(attn_act, act, l, "gather")
            attn_act(act, None, None, 0, 1, 0, -GL, (NSTEP, NSTEP))
            bodies(act, attn_act, *L0)
            copy_dense(act, "yT0", to_xT)
            act.wait_ge(var_ready, 2)
            act.activation(rstd[:, :], mv[:, :, 1], ACT.Sqrt).then_inc(sd_ready, 1)
            copy_dense(act, "xT1", to_xT)
            act.wait_ge(var_ready, 3)
            act.activation(rstd[:, :], mv[:, :, 1], ACT.Sqrt).then_inc(sd_ready, 1)
            copy_dense(act, "hT1", to_xT)

            def qkv1_out(n, bank):
                return (kqv[:, GL:2 * GL, :, n, :].rearrange("p g i c -> p i g c"),
                        bank[:, 0:3 * C].rearrange("p (i g c) -> p i g c", i=3, g=GL))
            copy_dense(act, "qkv1", qkv1_out)
            for n in range(2, 4):
                act.wait_ge(norm_sq, n + 1)
                act.activation(ss[:, :, :], ss[:, :, :], ACT.Sqrt).then_inc(norm_sd, 1)
            attn_act(act, None, None, GL, GL + 1, 0, GL)
            bodies(act, attn_act, *L1)
            copy_dense(act, "yTa", to_xT)
            copy_dense(act, "yTb", to_xT)
            act.wait_ge(var_ready, 4)
            act.activation(rstd[:, :], mv[:, :, 1], ACT.Sqrt).then_inc(sd_ready, 1)
            copy_dense(act, "xfT", to_xT)
            act.wait_ge(gate_dif, 1)
            act.activation(rt[:, 1, 0:NT * E1], rt[:, 0, 0:NT * E1], ACT.Exp).then_inc(gate_exp, 1)
            for c in range(NCH):
                for u, (b, ko, ki, src, dst, f) in enumerate(MOE_UNITS):
                    n = NU * c + u
                    if f == "times":
                        continue
                    act.wait_ge(moe_done, n + 1)
                    need(act, moe_read, n)
                    if u == 0:
                        need(act, mix_done, 4 * c)
                    act.activation(hidden[dst][:, ko, :], banks[n % 4],
                                   ACT.Silu if f == "silu" else ACT.Gelu).then_inc(moe_read, 1)

        def attn_dve(dve, gp, ga, gb, gt, par, slot0, steps, part_=None):
            def finish_max(g, c):
                dve.wait_ge(max_done, HG * NSTEP * g + HG * (CHUNK_END[c] + 1))
                need(dve, mT_done, 4 * g + (c - 1))
                steps(dve.tensor_reduce(negm[:, c % 2, :, :], mpart[:, c % 2, :, :, 0:c + 1], AX.X, ALU.max,
                                        negate=True))
                steps.sync()
                steps(dve.tensor_copy(mtok[:, c % 2, :, :, 0], negm[:, c % 2, :, :]))
                steps.sync()
                dve.tensor_tensor(mtok[:, c % 2, :, :, 1], negm[:, c % 2, :, :], mtok[:, c % 2, :, :, 0],
                                  ALU.subtract).then_inc(negm_ready, 1)

            def finish_out(g, c):
                dve.wait_ge(oT_done, 4 * g + c + 1)
                need(dve, y_done, 4 * g + (c - 1))
                view = misc[:, :].rearrange("p (t h d) -> p t h d", t=4, d=32)
                steps(dve.reciprocal(rec[:, c % 2, :, :], view[:, :, :, D]))
                steps.sync()
                slot_ = g - slot0
                if isinstance(slot_, int):
                    o = y[:, 4 * c:4 * c + 4, slot_, :].rearrange("p t (h d) -> p t h d", d=D)
                else:
                    o = y[:, 4 * c:4 * c + 4, bass.ds(slot_, 1), :].rearrange("p t a (h d) -> p t (a h) d", d=D)
                dve.tensor_tensor(o, view[:, :, :, 0:D],
                                  rec[:, c % 2, :, :].unsqueeze(3).to_broadcast([P, 4, HG, D]), ALU.mult)\
                    .then_inc(y_done, 1)

            if gb is None and ga is None:
                finish_out(gp, NCH - 1)
                return
            for s in range(*(part_ or (0, NSTEP))):
                if gb is not None:
                    t, kc = COMBOS[s]
                    n = min(512, (t + 1) * P - 512 * kc)
                    if t % 4 == 0 and kc == 0:
                        need(dve, negm_ready, 4 * gb + (t // 4 - 1))
                    for h in range(HG):
                        dve.wait_ge(sq_done, HG * NSTEP * gb + (HG * s + h + 1))
                        dve.tensor_reduce(mpart[:, (t // 4) % 2, t % 4, h, kc:kc + 1], sq[h % 2][:, 0:n], AX.X,
                                          ALU.max).then_inc(max_done, 1)
                    if s in CHUNK_END:
                        finish_max(gb, CHUNK_END.index(s))
                if ga is not None and s - 1 in OUT_AT:
                    finish_out(ga, OUT_AT[s - 1])
                if gp is not None and s - 1 == OUT_LAST_AT:
                    finish_out(gp, NCH - 1)

        def bc(ap, shape, axis):
            return ap.unsqueeze(axis).to_broadcast(shape)

        def add_banks(dve, name, where):
            for n in range(DENSE[name]):
                dve.wait_ge(done[name], n + 1)
                o, i0, i1 = where(n, banks[n % 4])
                dve.tensor_tensor(o, i0, i1, ALU.add).then_inc(freed[name], 1)

        @block.vector
        def _(dve):
            steps = Steps(dve, dve_step)
            big3 = [P, NT, C]

            def layer_norm(n, eps, dst, event, count):
                for t in range(NT):
                    steps(dve.bn_stats(stats[:, t, :], x[:, t, :]))
                steps.sync()
                for t in range(NT):
                    steps(dve.bn_aggr(mv[:, t, :], stats[:, t, :]))
                steps.sync()
                steps(dve.tensor_scalar(mv[:, :, 1], mv[:, :, 1], eps, None, ALU.add))
                steps.sync()
                dve.nop().then_inc(var_ready, 1)
                dve.wait_ge(sd_ready, n)
                steps(dve.reciprocal(rstd[:, :], rstd[:, :]))
                steps.sync()
                for t in range(NT):
                    i = dve.tensor_scalar(dst[:, t, :], x[:, t, :], mv[:, t, 0:1], rstd[:, t:t + 1],
                                          ALU.subtract, ALU.mult)
                    if event is not None:
                        i.then_inc(event, 1)
                    else:
                        steps(i)

            def rms_rows(src, n, w):
                half = scratch[:, 0:T].rearrange("p (t c) -> p t c", c=C)
                other = scratch[:, T:2 * T].rearrange("p (t c) -> p t c", c=C)
                steps.sync()
                steps(dve.tensor_tensor(other, src, src, ALU.mult))
                steps.sync()
                steps(dve.tensor_reduce(mv[:, :, 1], other, AX.X, ALU.add))
                steps.sync()
                steps(dve.tensor_scalar(mv[:, :, 1], mv[:, :, 1], 1.0 / C, 1.1920929e-07, ALU.mult, ALU.add))
                steps.sync()
                dve.nop().then_inc(var_ready, 1)
                dve.wait_ge(sd_ready, n)
                steps(dve.reciprocal(rstd[:, :], rstd[:, :]))
                steps.sync()
                steps(dve.tensor_tensor(other, src, bc(rstd[:, :], big3, 2), ALU.mult))
                steps.sync()
                steps(dve.tensor_tensor(half, other, bc(w, big3, 1), ALU.mult))
                steps.sync()

            def head_norm(i, w, n, rotate, in_eps, out_eps, scale, t1, t2):
                flat = lambda ap: ap.rearrange("p (g n d) -> p g n d", g=GL, d=D)
                shape = [P, GL, NT * HG, D]
                v = kqv[:, GL:2 * GL, i, :, :].rearrange("p g t (h d) -> p g (t h) d", d=D)
                norms = ss[:, :, :].rearrange("p t h -> p (t h)")
                hd = D // 2
                steps.sync()
                if rotate:
                    for g in range(GL):
                        vg = group(i, GL + g)
                        r1, r2 = (t[:, 512 * g:512 * g + 512].rearrange("p (t h d) -> p t h d", h=HG, d=D)
                                  for t in (t1, t2))
                        half = [P, NT, HG, hd]
                        steps(dve.tensor_tensor(r1[:, :, :, 0:hd], vg[:, :, :, hd:D], bc(sin[:, :, 0:hd], half, 2),
                                                ALU.mult))
                        steps(dve.tensor_tensor(r1[:, :, :, hd:D], vg[:, :, :, 0:hd], bc(sin[:, :, hd:D], half, 2),
                                                ALU.mult))
                        steps(dve.tensor_tensor(r2, vg, bc(cos, [P, NT, HG, D], 2), ALU.mult))
                    steps.sync()
                    steps(dve.tensor_tensor(v, flat(t1), flat(t2), ALU.add))
                    steps.sync()
                steps(dve.tensor_tensor(flat(t1), v, v, ALU.mult))
                steps.sync()
                steps(dve.tensor_reduce(norms, t1.rearrange("p (n d) -> p n d", d=D), AX.X, ALU.add))
                steps.sync()
                steps(dve.tensor_scalar(norms, norms, 1.0 / D, in_eps, ALU.mult, ALU.add))
                steps.sync()
                dve.nop().then_inc(norm_sq, 1)
                dve.wait_ge(norm_sd, n)
                steps(dve.tensor_scalar(norms, norms, out_eps, None, ALU.add))
                steps.sync()
                steps(dve.reciprocal(norms, norms))
                if scale != 1.0:
                    steps(dve.tensor_scalar(w, w, scale, None, ALU.mult))
                steps.sync()
                steps(dve.tensor_tensor(flat(t2), v, bc(norms.rearrange("p (g n) -> p g n", g=GL), shape, 3), ALU.mult))
                steps.sync()
                steps(dve.tensor_tensor(v, flat(t2), w.unsqueeze(1).unsqueeze(1).to_broadcast(shape), ALU.mult))
                steps.sync()

            dve.wait_ge(x_in, 16)
            layer_norm(1, 1e-05, xn, cur_ready, 0)
            dve.wait_ge(consts_in, 16)
            dve.tensor_copy(bcon[:, :], consts[:, 0:5 * 128]).then_inc(consts_cast, 1)

            ATT_STEPS = 2 * NCH * 3

            def emit(eng, gp, ga, gb, gt, par, slot0, part_=None):
                attn_dve(eng, gp, ga, gb, gt, par, slot0, steps, part_)

            shape = [P, NT, E0]
            v3 = lambda i: rt[:, i, :].rearrange("p (t e) -> p t e", e=E0)
            iota_b = con["iota"].unsqueeze(1).to_broadcast(shape)
            for l in range(LAYERS):
                steps.sync()
                dve.wait_ge(logits_done, l + 1)
                lg = oacc[:, 0:NT * E0].rearrange("p (t e) -> p t e", e=E0)
                steps(dve.tensor_reduce(small[:, 0, :], lg, AX.X, ALU.max))
                steps.sync()
                dve.tensor_tensor(v3(0), lg, bc(small[:, 0, :], shape, 2), ALU.subtract).then_inc(dif_ready, 1)
                dve.wait_ge(dif_ready, l + 1)
                steps(dve.tensor_scalar(rt[:, 2, :], rt[:, 0, :], 0.0, 64.0, ALU.is_lt, ALU.mult))
                steps.sync()
                steps(dve.tensor_tensor(v3(3), v3(2), iota_b, ALU.add))
                steps.sync()
                steps(dve.tensor_reduce(small[:, 1, :], v3(3), AX.X, ALU.min))
                steps.sync()
                dve.tensor_tensor(ohb[:, :, :], iota_b, bc(small[:, 1, :], shape, 2), ALU.is_equal)\
                    .then_inc(onehot_ready, 1)
                dve.wait_ge(exp_ready, l + 1)
                steps(dve.tensor_reduce(small[:, 2, :], v3(1), AX.X, ALU.add))
                steps.sync()
                steps(dve.reciprocal(wtop[:, :], small[:, 2, :]))
                dve.wait_ge(rank_done, l + 1)
                steps(dve.tensor_scalar(cnt_i[:, 0, :], banks[1][:, 0:E0], 127.0, None, ALU.add))
                steps.sync()
                steps(dve.tensor_scalar(cnt_i[:, 1, :], cnt_i[:, 0, :], 7, None, ALU.arith_shift_right))
                steps.sync()
                steps(dve.tensor_copy(ntile[:, 0, :], cnt_i[:, 1, :]))
                steps.sync()
                steps(dve.tensor_tensor(v3(2), upto, ntile[:, 0, :].unsqueeze(1).to_broadcast([P, E0, E0]), ALU.mult))
                steps.sync()
                steps(dve.tensor_reduce(ntile[:, 1, :], v3(2), AX.X, ALU.add))
                steps.sync()
                own = rt[:, 3:5, :].rearrange("p a e -> p (a e)")[:, 0:NS * E0].rearrange("p (s e) -> p s e", e=E0)
                steps(dve.tensor_tensor(own, con["tiles"].unsqueeze(2).to_broadcast([P, NS, E0]),
                                        ntile[:, 1, :].unsqueeze(1).to_broadcast([P, NS, E0]), ALU.is_ge))
                steps(dve.tensor_tensor(ntile[:, 2, :], ntile[:, 1, :], ntile[:, 0, :], ALU.subtract))
                steps.sync()
                steps(dve.tensor_reduce(owner_f[:, :], own, AX.X, ALU.add))
                steps(dve.tensor_scalar(ntile[:, 2, :], ntile[:, 2, :], 128.0, None, ALU.mult))
                steps.sync()
                dve.tensor_scalar(owner[:, :], owner_f[:, :], float(E0 - 1), None, ALU.min)\
                    .then_inc(owner_ready, 1)
                steps(dve.tensor_tensor(v3(5), banks[0][:, 0:NT * E0].rearrange("p (t e) -> p t e", e=E0),
                                        ntile[:, 2, :].unsqueeze(1).to_broadcast(shape), ALU.add))
                steps.sync()
                steps(dve.tensor_tensor(v3(2), v3(5), ohb[:, :, :], ALU.mult))
                steps.sync()
                steps(dve.tensor_reduce(small[:, 3, :], v3(2), AX.X, ALU.add))
                steps.sync()
                dve.tensor_copy(slot[:, :], small[:, 3, :]).then_inc(slot_ready, 1)
                if l == 0:
                    dve.wait_ge(freed["kqv0"], NT)
                    for i, w in ((1, 0), (0, 1)):
                        head_norm(i, hnorm[:, w, :], w + 1, True, 0.0, 1e-06, (D ** -0.5, 1.0)[w], *pair_tok)
                    dve.nop().then_inc(kqv_ready, 1)
                fill(emit, dve, l, "scatter")
                for s in range(NS):
                    e = dve.value_load(owner[0:1, s:s + 1], min_val=0, max_val=E0 - 1)
                    if l == 0 and s == 0:
                        dve.wait_ge(experts_in, 16 * 8)
                    if s >= 2:
                        dve.wait_ge(up_done, NS * l + (s - 1))
                    dve.tensor_copy(w1s[:, s % 2, :], w1[:, bass.ds(e * FF, FF)]).then_inc(w1_picked, 1)
                    dve.wait_ge(xsT_done, NS * l + (s + 1))
                    dve.tensor_copy(xsT[:, s % 2, :], banks[s % 2][:, 0:P]).then_inc(xsT_read, 1)
                fill(emit, dve, l, "gather")
                dve.wait_ge(gathered, 256 * (l + 1))
                for t in range(NT):
                    dve.tensor_scalar(xn[:, t, :], xn[:, t, :], wtop[:, t:t + 1], None, ALU.mult)\
                        .then_inc(cur_ready, 1)
            dve.wait_ge(cur_ready, NT * (LAYERS + 1))
            dve.wait_ge(down_done, NS * LAYERS)
            for par in range(2):
                steps(dve.memset(vpad[par][:, :, :, D + 1:32], 0.0))
                dve.memset(vpad[par][:, :, :, D:D + 1], 1.0).then_inc(vpad_set, 1)
            steps(dve.tensor_tensor(x[:, :, :], x[:, :, :], xn[:, :, :], ALU.add))
            steps.sync()
            dve.nop().then_inc(vpad_set, 1)
            bodies(dve, emit, *L0, steps, ATT_STEPS)
            steps.sync()
            add_banks(dve, "proj0", lambda n, bank: (x[:, 4 * n:4 * n + 4, :], x[:, 4 * n:4 * n + 4, :],
                                                     bank.rearrange("p (t c) -> p t c", t=4)))
            dve.wait_ge(freed["proj0"], NCH)
            layer_norm(2, 1e-05, xn, None, 0)
            steps.sync()
            dve.nop().then_inc(xn_ready, 1)
            rms_rows(xn[:, :, :], 3, cnorm[:, 0, :])
            for n in range(NT):
                dve.wait_ge(done["mqa"], n + 1)
                bank = banks[n % 4]
                steps(dve.tensor_scalar(kqv[:, 0:GL, 1, n, :], bank[:, 0:C].rearrange("p (g c) -> p g c", g=GL),
                                        D ** -0.5, None, ALU.mult))
                for i, lo in ((0, C), (2, C + D)):
                    o = kqv[:, 0:GL, i, n, :].rearrange("p g (h d) -> p g h d", d=D)
                    steps(dve.tensor_copy(o, bank[:, lo:lo + D].unsqueeze(1).unsqueeze(1)
                                          .to_broadcast([P, GL, HG, D])))
                steps.sync()
                dve.nop().then_inc(freed["mqa"], 1)
            dve.nop().then_inc(xn_ready, 1)
            dve.wait_ge(freed["qkv1"], NT)
            halves = (scratch[:, 0:T], scratch[:, T:2 * T])
            head_norm(1, hnorm[:, 2, :], 3, False, 1.1920929e-07, 0.0, D ** -0.5, *halves)
            head_norm(0, hnorm[:, 3, :], 4, False, 1.1920929e-07, 0.0, 1.0, *halves)
            dve.nop().then_inc(kqv_ready, 1)
            emit(dve, None, None, GL, GL + 1, 0, GL)
            bodies(dve, emit, *L1, steps, ATT_STEPS)
            steps.sync()
            add_banks(dve, "proja", lambda n, bank: (x[:, 4 * n:4 * n + 4, :], x[:, 4 * n:4 * n + 4, :],
                                                     bank.rearrange("p (t c) -> p t c", t=4)))
            Mz = 32
            add_banks(dve, "projb", lambda n, bank: (xn[:, 4 * n:4 * n + 4, Mz:C], xn[:, 4 * n:4 * n + 4, Mz:C],
                                                     bank.rearrange("p (t c) -> p t c", t=4)[:, :, Mz:C]))
            dve.wait_ge(freed["projb"], NCH)
            rms_rows(xn[:, :, :], 4, cnorm[:, 1, :])
            dve.nop().then_inc(xn_ready, 1)
            dve.wait_ge(freed["proja"], NCH)
            steps(dve.tensor_tensor(x[:, :, :], x[:, :, :], xn[:, :, :], ALU.add))
            dve.wait_ge(done["gate"], 1)
            sh = [P, NT, E1]
            r4 = lambda i: rt[:, i, 0:NT * E1].rearrange("p (t e) -> p t e", e=E1)
            g4 = banks[0][:, 0:NT * E1].rearrange("p (t e) -> p t e", e=E1)
            io = con["iota"][:, 0:E1].unsqueeze(1).to_broadcast(sh)
            big_f = 3.4028235e38
            steps(dve.tensor_scalar(r4(5), g4, -big_f, big_f, ALU.max, ALU.min))
            steps.sync()
            dve.nop().then_inc(freed["gate"], 1)
            steps(dve.tensor_reduce(small[:, 0, :], r4(5), AX.X, ALU.max))
            steps.sync()
            dve.tensor_tensor(r4(0), r4(5), bc(small[:, 0, :], sh, 2), ALU.subtract).then_inc(gate_dif, 1)
            dve.wait_ge(gate_exp, 1)
            steps(dve.tensor_reduce(small[:, 1, :], r4(1), AX.X, ALU.add))
            steps.sync()
            steps(dve.reciprocal(small[:, 2, :], small[:, 1, :]))
            steps.sync()
            steps(dve.tensor_tensor(r4(0), r4(1), bc(small[:, 2, :], sh, 2), ALU.mult))
            steps.sync()

            def top(src, dst):
                steps(dve.tensor_reduce(small[:, 0, :], src, AX.X, ALU.max))
                steps.sync()
                steps(dve.tensor_tensor(r4(2), src, bc(small[:, 0, :], sh, 2), ALU.is_lt))
                steps.sync()
                steps(dve.scalar_tensor_tensor(out=r4(3), in0=r4(2), scalar=64.0, in1=io, op0=ALU.mult, op1=ALU.add))
                steps.sync()
                steps(dve.tensor_reduce(small[:, 3, :], r4(3), AX.X, ALU.min))
                steps.sync()
                steps(dve.tensor_tensor(dst, io, bc(small[:, 3, :], sh, 2), ALU.is_equal))
                steps.sync()

            top(r4(0), r4(4))
            steps(dve.tensor_copy(small[:, 1, :], small[:, 0, :]))
            steps(dve.scalar_tensor_tensor(out=r4(5), in0=r4(4), scalar=-2.0, in1=r4(0), op0=ALU.mult, op1=ALU.add))
            steps.sync()
            top(r4(5), r4(1))
            steps(dve.tensor_tensor(r4(2), r4(1), r4(4), ALU.add))
            steps(dve.tensor_tensor(small[:, 2, :], small[:, 0, :], small[:, 1, :], ALU.add))
            steps.sync()
            steps(dve.tensor_scalar(small[:, 2, :], small[:, 2, :], 1e-08, None, ALU.add))
            steps.sync()
            steps(dve.reciprocal(small[:, 3, :], small[:, 2, :]))
            steps(dve.tensor_tensor(r4(3), r4(2), r4(0), ALU.mult))
            steps.sync()
            steps(dve.tensor_tensor(r4(4), r4(3), bc(small[:, 3, :], sh, 2), ALU.mult))
            steps.sync()
            wts = r4(4)
            for c in range(NCH):
                for u, (b, ko, ki, src, dst, f) in enumerate(MOE_UNITS):
                    if f != "times":
                        continue
                    n = NU * c + u
                    dve.wait_ge(moe_done, n + 1)
                    need(dve, moe_read, n)
                    dve.tensor_tensor(hidden[1][:, ko, :], hidden[1][:, ko, :], banks[n % 4], ALU.mult)\
                        .then_inc(moe_read, 1)
                for t in range(4):
                    n = 4 * c + t
                    dve.wait_ge(mix_done, n + 1)
                    for e in range(E1):
                        i = dve.scalar_tensor_tensor(out=x[:, n, Mz:C], in0=sq[n % 2][:, P * e + Mz:P * e + C],
                                                     scalar=wts[:, n, e:e + 1], in1=x[:, n, Mz:C],
                                                     op0=ALU.mult, op1=ALU.add)
                        if e == E1 - 1:
                            i.then_inc(mix_read, 1)
                        else:
                            steps(i)
                            steps.sync()


def constants():
    at, n = const_at()
    c = np.zeros((P, n), np.float32)
    r = np.arange(P)
    put = lambda k, v: c.__setitem__((slice(None), slice(*at[k])), v)
    put("ident", np.eye(P))
    put("mask_kq", np.where(r[:, None] > r[None, :], MASKED, 0.0))
    put("mask_qk", np.where(r[None, :] > r[:, None], MASKED, 0.0))
    put("before", (r[:, None] < r[None, :]))
    put("ones", 1.0)
    inv = (np.float32(1.0) / np.float32(10000.0) ** (np.arange(0, D, 2, dtype=np.float32) / np.float32(D)))
    freq = np.arange(T, dtype=np.float32)[:, None] * inv.astype(np.float32)[None, :]
    freq = np.concatenate([freq, freq], 1).astype(np.float64)
    sign = np.where(np.arange(D) < D // 2, -1.0, 1.0)
    tiled = lambda v: v.reshape(NT, P, D).transpose(1, 0, 2).reshape(P, NT * D)
    put("cos", tiled(np.cos(freq)))
    put("sin", tiled(np.sin(freq) * sign))
    e = np.arange(E0)
    put("upto", np.broadcast_to((e[None, :] <= e[:, None]).reshape(1, -1), (P, E0 * E0)))
    put("iota", np.broadcast_to(e, (P, E0)))
    put("tiles", np.broadcast_to(np.arange(NS), (P, NS)))
    return c


def lay_out(i):
    T_ = lambda w: np.ascontiguousarray(np.asarray(w).T)

    def blocks(w):
        w = T_(w)
        return [w[P * k:P * k + P, P * o:P * o + P] for k in range(w.shape[0] // P) for o in range(w.shape[1] // P)]

    f = {k: np.asarray(v) for k, v in i.items()}
    row = lambda n: f[n].reshape(1, -1)
    moe = []
    for n in ("e0_up", "e0_down", "e1_w1", "e1_w2", "e1_down", "e2_l1", "e2_l2", "e2_l3", "e2_l4",
              "e3_down", "e3_up", "e3_out"):
        moe += blocks(f["L1_ffn_" + n])
    return {
        "x": np.ascontiguousarray(f["L0_attn_x"].reshape(NT, P, C).transpose(1, 0, 2)),
        "consts": constants(),
        "w_kqv": T_(f["L0_attn_W_kqv"]), "w_proj": T_(f["L0_attn_W_proj"]),
        "w_mqa": np.ascontiguousarray(f["L1_attn_w_attn"]), "w_mproj": np.ascontiguousarray(f["L1_attn_w_proj"]),
        "w_qkv1": np.concatenate([T_(f["L1_ffn_wk"]), T_(f["L1_ffn_wq"]), T_(f["L1_ffn_wv"])], 1),
        "w_o": T_(f["L1_ffn_wo"]), "w_gate": T_(f["L1_ffn_gate_w"]),
        "routers": np.ascontiguousarray(f["L0_ffn_routers"].transpose(1, 0, 2).reshape(C, LAYERS * E0)),
        "hq0": row("L0_attn_q_norm_w"), "hk0": row("L0_attn_k_norm_w"),
        "hq1": row("L1_ffn_qn_w"), "hk1": row("L1_ffn_kn_w"),
        "n1": row("L1_ffn_n1_w"), "n2": row("L1_ffn_n2_w"),
        "w1": np.ascontiguousarray(f["L0_ffn_W1"].transpose(1, 0, 2).reshape(C, E0 * FF)),
        "w2": np.ascontiguousarray(f["L0_ffn_W2"].reshape(E0, KF, P, C).transpose(2, 0, 1, 3).reshape(P, E0 * FF)),
        "moe_w": np.ascontiguousarray(np.concatenate(moe, 1)),
    }


def kernel(**inputs):
    import concourse.bacc as bacc
    from concourse.bass_utils import run_bass_kernel_spmd

    arrays = lay_out(inputs)
    nc = bacc.Bacc("TRN2", target_bir_lowering=False, num_devices=1)
    args = {n: nc.dram_tensor(f"in_{n}", v.shape, mybir.dt.from_np(v.dtype), kind="ExternalInput").ap()
            for n, v in arrays.items()}
    out = nc.dram_tensor("out_0", (P, NT, C), F32, kind="ExternalOutput").ap()
    build(nc, args, out)
    r = run_bass_kernel_spmd(nc, [{f"in_{n}": v for n, v in arrays.items()}], core_ids=[0])
    got = np.asarray(r.results[0]["out_0"])
    return np.ascontiguousarray(got.transpose(1, 0, 2)).reshape(1, T, C)
```

```python
from contextlib import ExitStack

import numpy as np
import concourse.bass as bass
from concourse import mybir

F32 = mybir.dt.float32
BF16 = mybir.dt.bfloat16
I32 = mybir.dt.int32
ALU = mybir.AluOpType
ACT = mybir.ActivationFunctionType
AX = mybir.AxisListType

P = 128
T = 2048
NT = T // P
C = 128
H = 16
D = C // H
HG = 4
GL = H // HG
NCH = T // 512
E0, FF, LAYERS = 16, 512, 4
KF = FF // P
NS = (T - E0) // P + E0
Mz = 32
E1, HID = 4, 256
OPR = 64
MROW = 6 * D
MASKED = -1.0e30

STEPS = [(c, j) for c in range(NCH) for j in range(4 * c + 4)]
COMBOS = [tk for c in range(NCH) for tk in [(4 * c + i, kc) for i in range(4) for kc in range(c)]
          + [(4 * c + 3 - i, c) for i in range(4)]]
NSTEP = len(STEPS)
CHUNK_END = [STEPS.index((c, 4 * c + 3)) for c in range(NCH)]
CHUNK_START = [0] + [e + 1 for e in CHUNK_END[:-1]]
TURN_AT = {0: (1, "K"), 1: (1, "Q"), 7: (2, "K"), 8: (2, "Q"), 17: (3, "K"), 18: (3, "Q")}
TURN_NEXT_AT = {33: (0, "K"), 34: (0, "Q")}
MAX_AT = {CHUNK_END[c] + 1: c for c in range(NCH - 1)}
MAX_LAST_AT, OUT_LAST_AT = 1, 2
OUT_AT = {CHUNK_END[c] + 2: c for c in range(NCH - 1)}

WINDOWS = {(1, "gather"): (0, 8), (2, "scatter"): (8, 16), (2, "gather"): (16, 24),
           (3, "scatter"): (24, 32), (3, "gather"): (32, NSTEP)}

UNIT_AT = {**{2 + n: ("hT1", n) for n in range(4)}, **{8 + n: ("qkv1", n) for n in range(NT)}}
PROJECT_AT = {**{3 + n: ("yTa", n) for n in range(4)}, **{9 + n: ("proja", n) for n in range(4)}}
NORM_AT = 14

CONSTS = dict(ident=128, mask_kq=128, mask_qk=128, before=128, ones=128, cos=NT * D, sin=NT * D,
              upto=E0 * E0, iota=E0, tiles=NS)


def const_at():
    at, out = 0, {}
    for name, n in CONSTS.items():
        out[name] = (at, at + n)
        at += n
    return out, at


def need(eng, sem, value):
    if isinstance(value, int) and value <= 0:
        return
    eng.wait_ge(sem, value)


class Steps:

    def __init__(self, eng, sem, passed=None):
        self.eng, self.sem, self.n, self.loop, self.passed = eng, sem, 0, 0, passed

    def __call__(self, ins):
        ins.then_inc(self.sem, 1)
        self.n += 1

    def sync(self):
        need(self.eng, self.sem, self.n + self.loop)
        if self.passed is not None and not isinstance(self.loop, int):
            self.eng.sem_inc(self.passed, 1)


def build(nc, a, out):
    cat, ncon = const_at()
    with ExitStack() as ctx:
        def sb(name, shape, dt=F32):
            return ctx.enter_context(nc.sbuf_tensor(name, shape, dt))

        def ps(name, shape):
            return ctx.enter_context(nc.psum_tensor(name, shape, F32))

        def sem(name):
            return ctx.enter_context(nc.semaphore(name))

        consts = sb("consts", [P, ncon])
        con = {k: consts[:, lo:hi] for k, (lo, hi) in cat.items()}
        ident = con["ident"]
        cos = con["cos"].rearrange("p (t d) -> p t d", d=D)
        sin = con["sin"].rearrange("p (t d) -> p t d", d=D)
        upto = con["upto"].rearrange("p (a b) -> p a b", b=E0)
        bcon = sb("bcon", [P, 5 * 128], BF16)
        identb, mask_kq, mask_qk, beforeb, onesb = (bcon[:, 128 * i:128 * i + 128] for i in range(5))
        x = sb("x", [P, NT, C])
        xn = sb("xn", [P, NT, C])
        xT = sb("xT", [P, T])
        y = sb("y", [P, NT, 2 * GL, HG * D])
        scratch = y[:, :, :, :].rearrange("p t g c -> p (t g c)")
        w_kqv = sb("w_kqv", [P, 3 * C])
        w_proj = sb("w_proj", [P, C])
        w_mqa = sb("w_mqa", [P, C + 2 * D])
        w_qkv1 = sb("w_qkv1", [P, 3 * C])
        w_mproj = sb("w_mproj", [P, C])
        w_o = sb("w_o", [P, C])
        w_gate = sb("w_gate", [P, E1])
        routers = sb("routers", [P, LAYERS * E0])
        hnorm = sb("hnorm", [P, 4, D])
        cnorm = sb("cnorm", [P, 2, C])
        stats = sb("stats", [P, NT, 6])
        mv = sb("mv", [P, NT, 2])
        rstd = sb("rstd", [P, NT])
        ss = sb("ss", [P, NT, H])

        GW = 3 * NT * HG * D
        big = sb("big", [P, 25600 + 2 * GL * GW])
        kqv = big[:, 25600:25600 + 2 * GL * GW].rearrange("p (g i t c) -> p g i t c", g=2 * GL, i=3, t=NT)
        EXPERTS_AT = 12288
        w1 = big[:, EXPERTS_AT:EXPERTS_AT + E0 * FF]
        w2 = big[:, EXPERTS_AT + E0 * FF:EXPERTS_AT + 2 * E0 * FF]
        TABLES_AT = EXPERTS_AT + 2 * E0 * FF
        at = [0]

        def part(nwords):
            lo = at[0]
            at[0] += nwords
            return big[:, lo:at[0]]

        qtok = part(NT * HG * OPR // 2).bitcast(BF16).rearrange("p (t h r) -> p t h r", h=HG, r=OPR)
        ktok = part(NT * HG * OPR // 2).bitcast(BF16).rearrange("p (t h r) -> p t h r", h=HG, r=OPR)
        moe_w = big[:, 0:27 * P]
        def q_operand():
            return part(T).bitcast(BF16).rearrange("p (a t) -> p a t", a=2)

        def k_operand():
            return part(2 * T).bitcast(BF16).rearrange("p (h t) -> p h t", h=HG)

        qT, kT = [q_operand()], [k_operand()]
        ya_T = big[:, at[0] - 2 * T:at[0] - T]
        kst = [part(512).bitcast(BF16).rearrange("p (a t) -> p a t", a=2) for _ in range(2)]
        rest = part(NT * HG * D).rearrange("p (t h d) -> p t h d", h=HG, d=D)
        mT = [part(256).bitcast(BF16) for _ in range(2)]
        assert at[0] <= EXPERTS_AT
        qT.append(q_operand())
        kT.append(k_operand())
        vpad = [part(NT * HG * 32).rearrange("p (t h d) -> p t h d", h=HG, d=32) for _ in range(2)]
        mqa_rows = big[:, at[0]:at[0] + NT * (C + 2 * D)].rearrange("p (t c) -> p t c", t=NT)
        probs = [[w.rearrange("p (a t) -> p a t", a=2) for w in (part(1024), xT[:, 1024 * i:1024 * i + 1024])]
                 for i in range(2)]
        oT = [part(512) for _ in range(2)]
        assert at[0] <= 25600
        hidden = [big[:, 27 * P + 1024 * i:27 * P + 1024 * i + 1024].rearrange("p (k t) -> p k t", k=2)
                  for i in range(2 * 6)]
        mask_row = sb("mask_row", [P, 512], BF16)
        masked = sb("masked", [P, 2, 512], BF16)
        mpart = sb("mpart", [P, 2, 4, HG, NCH])
        negm = sb("negm", [P, 2, 4, HG])
        mtok = sb("mtok", [P, 2, 4, HG, 2], BF16)
        rec = sb("rec", [P, 2, 4, HG])

        rt = big[:, TABLES_AT + C:TABLES_AT + C + 6 * NT * E0].rearrange("p (i n) -> p i n", i=6)
        ohb = sb("ohb", [P, NT, E0], BF16)
        wtop = sb("wtop", [P, NT])
        small = sb("small", [P, 4, NT])
        slot = sb("slot", [P, NT], I32)
        cnt_i = sb("cnt_i", [P, 2, E0], I32)
        ntile = sb("ntile", [P, 3, E0])
        owner_f = sb("owner_f", [P, NS])
        owner = sb("owner", [P, NS], I32)
        xs = scratch[:, 0:8 * C].rearrange("p (b c) -> p b c", c=C)
        w1s = scratch[:, 8 * C:16 * C].rearrange("p (b c) -> p b c", c=FF)
        hT = scratch[:, 16 * C:28 * C].rearrange("p (b c) -> p b c", c=FF)
        TILES_AT = TABLES_AT + C + 6 * NT * E0
        yo = big[:, TILES_AT:TILES_AT + 8 * C].rearrange("p (b c) -> p b c", c=C)
        xsT = big[:, TILES_AT + 8 * C:TILES_AT + 10 * C].rearrange("p (b c) -> p b c", c=P)
        assert TILES_AT + 10 * C <= 25600 + GL * GW
        zeros = big[:, TABLES_AT:TABLES_AT + C]
        xs_dram = nc.dram_tensor("xs_dram", [NS * P, C], F32, kind="Internal").ap()
        ys_dram = nc.dram_tensor("ys_dram", [NS * P, C], F32, kind="Internal").ap()

        st = [ps("st0", [P, 2, 512]), ps("st1", [P, 2, 512])]
        oacc = ps("oacc", [P, 512])
        sq = [ps("sq0", [P, 512]), ps("sq1", [P, 512])]
        misc = ps("misc", [P, 512])
        banks = [st[0][:, 0, :], st[0][:, 1, :], st[1][:, 0, :], st[1][:, 1, :]]

        consts_in = sem("consts_in")
        x_in = sem("x_in")
        w_in, routers_in, w_kqv_in = sem("w_in"), sem("routers_in"), sem("w_kqv_in")
        experts_in = sem("experts_in")
        moe_in = sem("moe_in")
        out_done = sem("out_done")
        dve_step = sem("dve_step")
        pool_step, pool_passed = sem("pool_step"), sem("pool_passed")
        consts_cast = sem("consts_cast")
        slots_zeroed = sem("slots_zeroed")
        var_ready, sd_ready = sem("var_ready"), sem("sd_ready")
        cur_ready = sem("cur_ready")
        DENSE = {"xT0": 4, "kqv0": NT, "yT0": 4, "proj0": 4, "xT1": 4, "mqa": NT, "hT1": 4, "qkv1": NT,
                 "yTa": 4, "proja": 4, "yTb": 4, "projb": 4, "xfT": 4, "gate": 1}
        done = {k: sem(f"{k}_done") for k in DENSE}
        freed = {k: sem(f"{k}_read") for k in DENSE}
        norm_sq, norm_sd, norm_recip = sem("norm_sq"), sem("norm_sd"), sem("norm_recip")
        kqv_ready = sem("kqv_ready")
        xn_ready = sem("xn_ready")
        mqa_spread = sem("mqa_spread")
        curT_done, curT_read = sem("curT_done"), sem("curT_read")
        logits_done, exp_ready = sem("logits_done"), sem("exp_ready")
        dif_ready, onehot_ready, rank_done = sem("dif_ready"), sem("onehot_ready"), sem("rank_done")
        slot_ready, owner_ready = sem("slot_ready"), sem("owner_ready")
        scattered, gathered = sem("scattered"), [sem(f"gathered{q}") for q in range(4)]
        count_done = sem("count_done")
        xs_loaded = [sem(f"xs_loaded{i}") for i in range(2)]
        ys_stored = [sem(f"ys_stored{i}") for i in range(2)]
        xsT_done, xsT_read = sem("xsT_done"), sem("xsT_read")
        w1_picked, up_done, silu_done = sem("w1_picked"), sem("up_done"), sem("silu_done")
        down_done, down_read = sem("down_done"), sem("down_read")
        pads_zeroed = sem("pads_zeroed")
        vpad_set = sem("vpad_set")
        qk_packed, v_packed = sem("qk_packed"), sem("v_packed")
        turned, turn_read = sem("turned"), sem("turn_read")
        k_loaded = [sem(f"k_loaded{c}") for c in range(NCH)]
        m_loaded = [sem(f"m_loaded{c}") for c in range(NCH)]
        sq_done, max_done = sem("sq_done"), sem("max_done")
        negm_ready, mT_done, mT_read = sem("negm_ready"), sem("mT_done"), sem("mT_read")
        st_done, exp_done, pv_done = sem("st_done"), sem("exp_done"), sem("pv_done")
        o_read, oT_done, y_done = sem("o_read"), sem("oT_done"), sem("y_done")
        wts_ready, gate_exp, gate_dif = sem("wts_ready"), sem("gate_exp"), sem("gate_dif")
        moe_done, moe_read = sem("moe_done"), sem("moe_read")
        mix_done, mix_read, gated = sem("mix_done"), sem("mix_read"), sem("gated")

        block = ctx.enter_context(nc.Block())

        def tok(tile):
            return slice(tile * P, tile * P + P)

        def group(i, slot_):
            if isinstance(slot_, int):
                return kqv[:, slot_, i, :, :].rearrange("p t (h d) -> p t h d", d=D)
            return kqv[:, bass.ds(slot_, 1), i, :, :].rearrange("p a t (h d) -> p (a t) h d", d=D)

        def mqa_part(i, g):
            if i == 1:
                return kqv[:, g, 1, :, :], mqa_rows[:, :, HG * D * g:HG * D * g + HG * D]
            lo = C if i == 0 else C + D
            return group(i, g), mqa_rows[:, :, lo:lo + D].unsqueeze(2).to_broadcast([P, NT, HG, D])

        def bodies(eng, emit, first, last, slot0, steps=None, per_pair=0, peel=1):
            g = first
            while g < first + peel:
                emit(eng, g - 1 if g > first else None, g, g + 1, g + 2, g % 2, slot0)
                g += 1
            pairs = (last - 1 - g) // 2
            if pairs > 1:
                with eng.Fori(0, pairs) as i:
                    if steps is not None:
                        base, steps.loop = steps.n, i * per_pair
                    for b in range(2):
                        n = g + b + i * 2
                        emit(eng, n - 1, n, n + 1, n + 2, (g + b) % 2, slot0)
                if steps is not None:
                    assert steps.n - base == per_pair, steps.n - base
                    steps.n, steps.loop = base + per_pair * pairs, 0
                g += 2 * pairs
            while g <= last:
                emit(eng, g - 1, g, g + 1 if g < last else None, g + 2 if g + 1 < last else None, g % 2, slot0)
                g += 1
            emit(eng, last, None, None, None, 0, slot0)

        L0 = (0, GL - 1, -GL)
        L1 = (GL, 3 * GL - 1, GL)
        PEEL1 = 3

        def sp_attention(sp, gp, ga, gb, gt, par, slot0, part_=None):
            if gb is None and ga is None:
                return
            pb = None if gb is None else nxt(ga, par, gb)
            for s in range(*(part_ or (0, NSTEP))):
                if ga is None and s == 0:
                    keys_to(sp, gb, pb, 0)
                if gb is not None:
                    if s in TURN_AT and TURN_AT[s][1] == "K":
                        keys_to(sp, gb, pb, TURN_AT[s][0])
                    if s in MAX_AT:
                        max_to(sp, gb, pb, MAX_AT[s])
                if ga is not None and s == MAX_LAST_AT:
                    max_to(sp, ga, par, NCH - 1)
                if gt is not None and s in TURN_NEXT_AT and TURN_NEXT_AT[s][1] == "K":
                    keys_to(sp, gt, 1 - pb, 0)

        def nxt(ga, par, gb):
            return gb % 2 if ga is None else 1 - par

        def fill(emit, eng, l, move):
            if (l, move) in WINDOWS:
                emit(eng, None, None, 0, None, 0, -GL, WINDOWS[l, move])

        def fill_quarter(emit, eng, l, q):
            if (l, "gather") in WINDOWS:
                lo, hi = WINDOWS[l, "gather"]
                at_ = [lo + (hi - lo) * i // 4 for i in range(5)]
                emit(eng, None, None, 0, None, 0, -GL, (at_[q], at_[q + 1]))

        def keys_to(sp, g, par, c):
            sp.wait_ge(turn_read, 8 * g + 2 * c + 1)
            cols = slice(512 * c, 512 * c + 512)
            for b in range(2):
                rows = slice(64 * b, 64 * b + 64)
                sp.dma_start(kT[par][rows, b:HG:2, cols], kst[c % 2][rows, :, :]).then_inc(k_loaded[c], 16)

        def max_to(sp, g, par, c):
            sp.wait_ge(mT_read, 4 * g + c + 1)
            for h in range(HG):
                row = 64 * (h % 2) + MROW
                sp.dma_start(qT[par][row:row + 2, h // 2, 512 * c:512 * c + 512],
                             mT[c % 2][2 * h:2 * h + 2, :]).then_inc(m_loaded[c], 16)

        QUAD = 4
        NQ = -(-NS // QUAD)
        xs_tiles = xs_dram.rearrange("(s p) c -> p s c", p=P)
        ys_tiles = ys_dram.rearrange("(s p) c -> p s c", p=P)

        def quad_size(q):
            return min(QUAD, NS - QUAD * q)

        def moves(l, q):
            return len(range(q % 2, NQ, 2)) * l + q // 2 + 1

        @block.sync
        def _(sp):
            sp.dma_start(x[:, :, :], a["x"]).then_inc(x_in, 16)
            sp.dma_start(consts[:, :], a["consts"]).then_inc(consts_in, 16)
            sp.dma_start(routers[:, :], a["routers"]).then_inc(routers_in, 16)
            sp.dma_start(w_kqv[:, :], a["w_kqv"]).then_inc(w_kqv_in, 16)
            for dst, name in ((w_proj, "w_proj"), (w_mqa, "w_mqa"), (w_qkv1, "w_qkv1"),
                              (w_mproj, "w_mproj"), (w_o, "w_o"), (w_gate, "w_gate")):
                sp.dma_start(dst[:, :], a[name]).then_inc(w_in, 16)
            for i, name in enumerate(("hq0", "hk0", "hq1", "hk1")):
                sp.dma_start(hnorm[:, i, :], a[name].to_broadcast([P, D])).then_inc(w_in, 16)
            for i, name in enumerate(("n1", "n2")):
                sp.dma_start(cnorm[:, i, :], a[name].to_broadcast([P, C])).then_inc(w_in, 16)
            for q in range(4):
                n = E0 * FF // 4
                sp.dma_start(w1[:, n * q:n * q + n], a["w1"][:, n * q:n * q + n]).then_inc(experts_in, 16)
                sp.dma_start(w2[:, n * q:n * q + n], a["w2"][:, n * q:n * q + n]).then_inc(experts_in, 16)
            for l in range(LAYERS):
                fill(sp_attention, sp, l, "scatter")
                sp.wait_ge(scattered, 256 * (l + 1))
                if l < 2:
                    sp.wait_ge(kqv_ready, l + 1)
                for q in range(NQ + 2):
                    if q < NQ:
                        if q >= 2:
                            sp.wait_ge(xsT_done, NS * l + QUAD * (q - 1))
                        lo, n = QUAD * q, quad_size(q)
                        sp.dma_start(xs[:, QUAD * (q % 2):QUAD * (q % 2) + n, :],
                                     xs_tiles[:, lo:lo + n, :]).then_inc(xs_loaded[q % 2], 16)
                    if q >= 2:
                        lo, n = QUAD * (q - 2), quad_size(q - 2)
                        sp.wait_ge(down_read, NS * l + (lo + n))
                        sp.dma_start(ys_tiles[:, lo:lo + n, :], yo[:, QUAD * (q % 2):QUAD * (q % 2) + n, :])\
                          .then_inc(ys_stored[q % 2], 16)
                fill(sp_attention, sp, l, "gather")
            keys_to(sp, 1, 1, 0)
            bodies(sp, sp_attention, *L0)
            sp_attention(sp, None, None, GL, GL + 1, 0, GL)
            bodies(sp, sp_attention, *L1, peel=PEEL1)
            sp.wait_ge(turned, 8 * 3 * GL)
            sp.dma_start(moe_w, a["moe_w"]).then_inc(moe_in, 16)
            sp.wait_ge(mix_read, NT)
            sp.dma_start(out, x[:, :, :]).then_inc(out_done, 16)
            sp.wait_ge(out_done, 16)

        def pack(eng, steps, g, slot_, which):
            for i in range(3):
                pack_part(eng, steps, slot_, which, i)

        def pack_part(eng, steps, slot_, which, i):
            src = group(1 if which == "Q" else 0, slot_)
            dst = qtok if which == "Q" else ktok
            places = ((0, 1, 3), (2, 4), (5,)) if which == "Q" else ((0, 2, 5), (1, 4), (3,))
            cols = places[i]
            left = src if i == 0 else rest
            for col in cols:
                steps(eng.tensor_copy(dst[:, :, :, D * col:D * col + D], left))
            if i < 2:
                steps.sync()
                steps(eng.tensor_tensor(rest, left, dst[:, :, :, D * cols[0]:D * cols[0] + D], ALU.subtract))
                steps.sync()

        def pool_qk(pool, steps, g, slot_):
            need(pool, turned, 8 * g)
            steps.sync()
            pack(pool, steps, g, slot_, "K")
            steps.sync()
            pack(pool, steps, g, slot_, "Q")
            steps.sync()
            pool.nop().then_inc(qk_packed, 1)

        def pool_v(pool, steps, g, par, slot_):
            if not isinstance(g, int) or g >= 2:
                pool.wait_ge(pv_done, NSTEP * (g - 1))
                pool.sem_inc(pool_passed, 1)
            pool.tensor_copy(vpad[par][:, :, :, 0:D], group(2, slot_)).then_inc(v_packed, 1)

        PACK_STEPS = 2 * 8

        @block.gpsimd
        def _(pool):
            steps = Steps(pool, pool_step, passed=pool_passed)
            steps(pool.memset(zeros, 0.0))
            steps.sync()
            pool.dma_start(xs_dram.rearrange("(s p) c -> p s c", p=P),
                           zeros.unsqueeze(1).to_broadcast([P, NS, C])).then_inc(slots_zeroed, 16)

            def zero_pad(par):
                for b in range(2):
                    steps.sync()
                    steps(pool.memset(kT[par][64 * (1 - b):64 * (1 - b) + 64, b:HG:2, :], 0.0))
                steps.sync()

            steps(pool.memset(qtok[:, :, :, MROW:OPR], 0.0))
            steps(pool.memset(ktok[:, :, :, MROW:MROW + 2], 1.0))
            steps(pool.memset(ktok[:, :, :, MROW + 2:OPR], 0.0))
            zero_pad(0)
            pool.nop().then_inc(pads_zeroed, 1)
            pool.wait_ge(slots_zeroed, 16)
            for l in range(LAYERS):
                pool.wait_ge(slot_ready, l + 1)
                for t in range(NT):
                    pool.indirect_dma_start(xs_dram, bass.IndirectOffsetOnAxis(ap=slot[:, t:t + 1], axis=0),
                                            xn[:, t, :], None).then_inc(scattered, 16)
                if l == LAYERS - 1:
                    pool_qk(pool, steps, 1, GL + 1)
                pool.wait_ge(scattered, 256 * (l + 1))
                for q in (NQ - 2, NQ - 1):
                    pool.wait_ge(ys_stored[q % 2], 16 * moves(l, q))
                for t in range(NT):
                    pool.indirect_dma_start(xn[:, t, :], None, ys_dram,
                                            bass.IndirectOffsetOnAxis(ap=slot[:, t:t + 1], axis=0))\
                        .then_inc(gathered[t // 4], 16)
            pool.wait_ge(down_done, NS * LAYERS)
            zero_pad(1)
            pool.nop().then_inc(pads_zeroed, 1)
            pool_v(pool, steps, 0, 0, GL)

            def emit(eng, gp, ga, gb, gt, par, slot0):
                if gb is not None:
                    pool_v(eng, steps, gb, nxt(ga, par, gb), gb - slot0)
                if slot0 == GL and isinstance(ga, int) and ga in (GL, GL + 1):
                    heads_norm(ga - GL)
                if gt is not None:
                    pool_qk(eng, steps, gt, gt - slot0)

            def heads_norm(n):
                i, w = 1 - n, hnorm[:, 2 + n, :]
                shape = [P, GL, NT * HG, D]
                v = kqv[:, GL:2 * GL, i, :, :].rearrange("p g t (h d) -> p g (t h) d", d=D)
                square = y[:, :, GL:2 * GL, :].rearrange("p t g c -> p t (g c)").rearrange(
                    "p (g t) (a d) -> p g t a d", g=GL, d=D)
                square = square.rearrange("p g t a d -> p (g t) a d")
                norms = ss[:, :, :].rearrange("p t h -> p (t h)").rearrange("p (g n) -> p g n", g=GL)
                if n == 0:
                    pool.wait_ge(freed["qkv1"], NT)
                for g in range(GL):
                    vg = kqv[:, GL + g, i, :, :].rearrange("p (t b) (h d) -> p t (b h) d", t=GL, d=D)
                    steps(pool.tensor_tensor(square[:, GL * g:GL * g + GL, :, :], vg, vg, ALU.mult))
                steps.sync()
                width = D
                while width > 2:
                    width //= 2
                    steps(pool.tensor_tensor(square[:, :, :, 0:width], square[:, :, :, 0:width],
                                             square[:, :, :, width:2 * width], ALU.add))
                    steps.sync()
                steps(pool.tensor_tensor(ss[:, :, :], square[:, :, :, 0], square[:, :, :, 1], ALU.add))
                steps.sync()
                steps(pool.tensor_scalar(ss[:, :, :], ss[:, :, :], 1.0 / D, 1.1920929e-07, ALU.mult, ALU.add))
                steps.sync()
                pool.nop().then_inc(norm_sq, 1)
                if n == 0:
                    steps(pool.tensor_scalar(w, w, D ** -0.5, None, ALU.mult))
                pool.wait_ge(norm_recip, n + 1)
                steps(pool.tensor_tensor(v, v, norms.unsqueeze(3).to_broadcast(shape), ALU.mult))
                steps.sync()
                steps(pool.tensor_tensor(v, v, w.unsqueeze(1).unsqueeze(1).to_broadcast(shape), ALU.mult))
                steps.sync()

            bodies(pool, emit, *L0, steps, 2 * PACK_STEPS)
            pool.wait_ge(mqa_spread, 3 * GL - 2)
            pool_v(pool, steps, GL, 0, 0)
            pool_qk(pool, steps, GL + 1, 1)
            bodies(pool, emit, *L1, steps, 2 * PACK_STEPS, peel=PEEL1)

        project = {}
        other_attention = {}
        prev = []

        def take_misc(pe, next_reader):
            for s_, v in prev:
                need(pe, s_, v)
            prev[:] = [next_reader]

        def attn_pe(pe, gp, ga, gb, gt, par, slot0, part_=None):
            pb = nxt(ga, par, gb) if gb is not None else None

            def turn(g, c, kind):
                n = 8 * g + 2 * c + (kind == "Q")
                take_misc(pe, (turn_read, n + 1))
                need(pe, qk_packed, g + 1)
                view = misc[:, :].bitcast(BF16).rearrange("p (a t) -> p a t", a=2)
                src = ktok if kind == "K" else qtok
                for a_ in range(2):
                    for t in range(4):
                        m = pe.transpose(view[:, a_, tok(t)],
                                         src[:, 4 * c + t, 2 * a_:2 * a_ + 2, :].rearrange("p h r -> p (h r)"),
                                         identb)
                m.then_inc(turned, 1)

            def turn_max(g, c):
                take_misc(pe, (mT_read, 4 * g + c + 1))
                pe.wait_ge(negm_ready, 4 * g + c + 1)
                view = misc[0:2 * HG, :].bitcast(BF16)
                for t in range(4):
                    m = pe.transpose(view[:, tok(t)], mtok[:, c % 2, t, :, :].rearrange("p h e -> p (h e)"),
                                     identb)
                m.then_inc(mT_done, 1)

            def turn_out(g, c):
                take_misc(pe, (y_done, 4 * g + c + 1))
                pe.wait_ge(o_read, 4 * g + c + 1)
                for t in range(4):
                    m = pe.transpose(misc[:, tok(t)], oT[c % 2][:, tok(t)], ident)
                m.then_inc(oT_done, 1)

            def scores_t(g, gpar, s, a_):
                c, j = STEPS[s]
                off = 128 * max(0, j - 4 * c)
                if j == 0:
                    pe.wait_ge(m_loaded[c], 64 * (g + 1))
                need(pe, exp_done, 2 * NSTEP * g + (2 * (s - 1) + a_ + 1))
                for b in range(2):
                    o = st[a_][:, b, :]
                    m = pe.matmul(o[:, off:512], kT[gpar][:, 2 * a_ + b, tok(j)],
                                  qT[gpar][:, a_, 512 * c + off:512 * c + 512], start=True, stop=j < 4 * c)
                    if j >= 4 * c:
                        m = pe.matmul(o[:, off:off + 128], identb, mask_kq, start=False, stop=True)
                m.then_inc(st_done, 1)

            def scores(g, gpar, s, h):
                t, kc = COMBOS[s]
                c = t // 4
                if s in CHUNK_START and h == 0:
                    pe.wait_ge(turn_read, 8 * g + 2 * c + 2)
                    pe.wait_ge(k_loaded[c], 32 * (g + 1))
                n = min(512, (t + 1) * P - 512 * kc)
                need(pe, max_done, HG * NSTEP * g + (HG * s + h - 1))
                o = sq[h % 2]
                pe.matmul(o[:, 0:n], qT[gpar][:, h // 2, tok(t)], kT[gpar][:, h, 512 * kc:512 * kc + n],
                          start=True, stop=True).then_inc(sq_done, 1)

            def weigh(g, gpar, s):
                c, j = STEPS[s]
                off = 128 * max(0, j - 4 * c)
                pe.wait_ge(exp_done, 2 * NSTEP * g + (2 * s + 2))
                if s == 0:
                    pe.wait_ge(vpad_set, 3)
                    pe.wait_ge(v_packed, g + 1)
                if j == 0:
                    need(pe, o_read, 4 * g + c)
                for h in range(HG):
                    m = pe.matmul(oacc[32 * h:32 * h + 32, off:512], vpad[gpar][:, j, h, :],
                                  probs[s % 2][h // 2][:, h % 2, off:512], start=(j == 0), stop=(j == 4 * c + 3),
                                  tile_position=(0, 32 * h))
                m.then_inc(pv_done, 1)

            if ga is None and gb is None:
                prev[:] = [(y_done, 4 * gp + 3)]
                turn_out(gp, NCH - 1)
                return
            if ga is not None and gb is None:
                prev[:] = [(y_done, 4 * gp + 3)]
            elif ga is not None:
                prev[:] = [(turn_read, 8 * gb + 2)]
            lo, hi = part_ or (0, NSTEP)
            if ga is None and lo == 0:
                turn(gb, 0, "K")
                turn(gb, 0, "Q")
            for s in range(lo, hi):
                units = iter(range(HG))
                if gb is not None:
                    scores(gb, pb, s, next(units))
                for a_ in range(2):
                    if ga is not None and s + 1 < NSTEP:
                        scores_t(ga, par, s + 1, a_)
                    elif ga is not None and gb is not None:
                        scores_t(gb, pb, 0, a_)
                    if gb is not None:
                        scores(gb, pb, s, next(units))
                if ga is not None:
                    weigh(ga, par, s)
                if gb is not None:
                    scores(gb, pb, s, next(units))
                if gb is not None and s in TURN_AT:
                    turn(gb, *TURN_AT[s])
                if gb is not None and s in MAX_AT:
                    turn_max(gb, MAX_AT[s])
                if ga is not None and s == MAX_LAST_AT:
                    turn_max(ga, NCH - 1)
                if ga is not None and s in OUT_AT:
                    turn_out(ga, OUT_AT[s])
                if gp is not None and s == OUT_LAST_AT:
                    turn_out(gp, NCH - 1)
                if gt is not None and s in TURN_NEXT_AT:
                    turn(gt, *TURN_NEXT_AT[s])
                if ga is None and gb == GL and s in UNIT_AT:
                    name, n = UNIT_AT[s]
                    if name == "hT1" and n == 0:
                        pe.wait_ge(xn_ready, 2)
                    if name == "qkv1" and n == 0:
                        pe.wait_ge(freed["hT1"], 4)
                    if n >= 4:
                        pe.wait_ge(freed[name], n - 3)
                    other_attention[name](n, banks[n % 4]).then_inc(done[name], 1)
                if ga == 3 * GL - 1 and s in PROJECT_AT:
                    name, n = PROJECT_AT[s]
                    if name == "yTa" and n == 0:
                        pe.wait_ge(max_done, HG * NSTEP * 3 * GL)
                    if name == "proja" and n == 0:
                        pe.wait_ge(freed["yTa"], 4)
                    need(pe, freed[name], n - 1)
                    project[name](n, sq[n % 2]).then_inc(done[name], 1)
            if ga is None and part_ == (NSTEP, NSTEP):
                turn(gt, 0, "K")
                turn(gt, 0, "Q")
            if ga is None and lo in (NSTEP, 0) and hi == NSTEP:
                if gb == GL:
                    pe.wait_ge(freed["qkv1"], NT)
                for a_ in range(2):
                    scores_t(gb, pb, 0, a_)

        def dense(pe, name, emit, before=None, units=None):
            if before is not None:
                pe.wait_ge(freed[before], DENSE[before])
            for n in units or range(DENSE[name]):
                if n >= 4:
                    pe.wait_ge(freed[name], n - 3)
                emit(n, banks[n % 4]).then_inc(done[name], 1)

        def turn_tiles(pe, src):
            def emit(n, bank):
                for t in range(4):
                    m = pe.transpose(bank[:, tok(t)], src(4 * n + t), ident)
                return m
            return emit

        def times(pe, w, cols):
            def emit(n, bank):
                return pe.matmul(bank[:, 0:cols], xT[:, tok(n)], w, start=True, stop=True)
            return emit

        def times4(pe, w, src=xT):
            def emit(n, bank):
                for t in range(4):
                    m = pe.matmul(bank[:, tok(t)], src[:, tok(4 * n + t)], w, start=True, stop=True)
                return m
            return emit

        UP0, DN0, W1_, W2_, DN1 = 0, 2, 4, 6, 8
        L1_, L2_, L3_, L4_, DN3, UP3, OUT3 = 10, 12, 16, 20, 22, 23, 25
        MOE = [(W1_, 2, 1, None, 1, "silu"), (W2_, 2, 1, None, 1, "times"),
               (UP0, 2, 1, None, 0, "gelu"), (L1_, 2, 1, None, 2, "gelu"), (DN3, 1, 1, None, 4, "gelu"),
               (L2_, 2, 2, 2, 3, "gelu"), (UP3, 2, 1, 4, 5, "gelu"), (L3_, 2, 2, 3, 2, "gelu")]
        MOE_UNITS = [(b + k_out * 1, k_out, ki, src, dst, f) for b, ko, ki, src, dst, f in MOE for k_out in range(ko)]
        NU = len(MOE_UNITS)
        LAST_AT = [NU * (2 * i + 1) // 8 for i in range(4)]
        LASTS = [(DN0, 0), (DN1, 1), (L4_, 2), (OUT3, 5)]

        def block_w(b):
            return moe_w[:, P * b:P * b + P]

        def unit_ready(src, u):
            _, _, _, s, d, _ = MOE_UNITS[u]
            ns = [v for v in range(u) if MOE_UNITS[v][4] == s and s is not None]
            return max(ns) + 1 if ns else 0

        def moe_pe(pe):
            pe.wait_ge(moe_in, 16)
            mbanks = banks

            def unit(c, u):
                b, ko, ki, src, dst, f = MOE_UNITS[u]
                if (c, u) == (0, 4):
                    for t in range(NT):
                        m = pe.matmul(oacc[:, E1 * t:E1 * t + E1], xT[:, tok(t)], w_gate[:, :],
                                      start=True, stop=True)
                    m.then_inc(done["gate"], 1)
                n = NU * c + u
                need(pe, moe_read, n - 3)
                need(pe, moe_read, NU * c + unit_ready(src, u) if src is not None else 0)
                for k in range(ki):
                    rhs = xT[:, 512 * c:512 * c + 512] if src is None else hidden[6 * (c % 2) + src][:, k, :]
                    blk = b + (k * 2 if ki == 2 else 0)
                    m = pe.matmul(banks[n % 4], block_w(blk), rhs, start=(k == 0), stop=(k == ki - 1))
                m.then_inc(moe_done, 1)

            def last(c, t):
                n = 4 * c + t
                need(pe, mix_read, n - 1)
                o = sq[n % 2]
                for e, (b, src) in enumerate(LASTS):
                    for k in range(2):
                        m = pe.matmul(o[:, P * e + Mz:P * e + C], hidden[6 * (c % 2) + src][:, k, tok(t)],
                                      block_w(b + k)[:, Mz:C], start=(k == 0), stop=(k == 1))
                m.then_inc(mix_done, 1)

            for c in range(NCH + 1):
                for u in range(NU):
                    if c < NCH:
                        unit(c, u)
                    if c > 0 and u in LAST_AT:
                        if u == LAST_AT[0]:
                            pe.wait_ge(moe_read, NU * c)
                        last(c - 1, LAST_AT.index(u))

        @block.tensor
        def _(pe):
            pe.wait_ge(consts_in, 16)
            pe.wait_ge(cur_ready, NT)
            dense(pe, "xT0", turn_tiles(pe, lambda t: xn[:, t, :]))
            pe.wait_ge(freed["xT0"], 4)
            pe.wait_ge(routers_in, 16)

            def turn_rows(l, n):
                pe.wait_ge(cur_ready, NT * (l + 1) - 4 * (3 - n))
                for t in range(4):
                    m = pe.transpose(banks[n][:, tok(t)], xn[:, 4 * n + t, :], ident)
                m.then_inc(curT_done, 1)

            def logits(l, n):
                if l > 0:
                    pe.wait_ge(curT_read, 4 * (l - 1) + n + 1)
                for t in range(4 * n, 4 * n + 4):
                    m = pe.matmul(oacc[:, E0 * t:E0 * t + E0], xT[:, tok(t)], routers[:, l * E0:l * E0 + E0],
                                  start=True, stop=True)
                if n == 3:
                    m.then_inc(logits_done, 1)

            for l in range(LAYERS):
                count, rank = (sq[0], sq[1]) if l == 0 else (banks[0], banks[1])
                if l == 0:
                    for n in range(4):
                        logits(l, n)
                    pe.wait_ge(consts_cast, 1)
                pe.wait_ge(onehot_ready, l + 1)
                for t in range(NT):
                    m = pe.matmul(count[:, 0:E0], onesb, ohb[:, t, :], start=(t == 0), stop=(t == NT - 1))
                m.then_inc(count_done, 1)
                pe.matmul(rank[:, 0:NT * E0], beforeb, ohb[:, :, :].rearrange("p t e -> p (t e)"),
                          start=True, stop=False)
                for t in range(NT - 1):
                    m = pe.matmul(rank[:, E0 * (t + 1):NT * E0], onesb,
                                  ohb[:, t:t + 1, :].to_broadcast([P, NT - 1 - t, E0]),
                                  start=False, stop=(t == NT - 2))
                m.then_inc(rank_done, 1)
                if l == 0:
                    pe.wait_ge(w_kqv_in, 16)
                    dense(pe, "kqv0", times(pe, w_kqv[:, :], 3 * C), "xT0")
                    pe.wait_ge(freed["kqv0"], NT)
                fill(attn_pe, pe, l, "scatter")
                pe.wait_ge(owner_ready, l + 1)
                need(pe, max_done, HG * max([0] + [hi for (k, w), (lo, hi) in WINDOWS.items()
                                                   if k < l or (k == l and w == "scatter")]))
                if l == 0:
                    pe.wait_ge(experts_in, 16 * 8)
                expert = {}
                for s in range(NS + 3):
                    if s < NS:
                        i = s
                        expert[i] = pe.value_load(owner[0:1, i:i + 1], min_val=0, max_val=E0 - 1)
                        if i % QUAD == 0:
                            pe.wait_ge(xs_loaded[i // QUAD % 2], 16 * moves(l, i // QUAD))
                        if i >= 2:
                            pe.wait_ge(xsT_read, NS * l + (i - 1))
                        pe.transpose(banks[i % 2][:, 0:P], xs[:, i % 8, :], ident).then_inc(xsT_done, 1)
                    if 0 <= s - 1 < NS:
                        i = s - 1
                        pe.wait_ge(xsT_read, NS * l + (i + 1))
                        pe.wait_ge(w1_picked, NS * l + (i + 1))
                        if i >= 2:
                            pe.wait_ge(silu_done, NS * l + (i - 1))
                        for k in range(KF):
                            m = pe.matmul(banks[2 + i % 2][:, tok(k)], w1s[:, i % 2, tok(k)], xsT[:, i % 2, :],
                                          start=True, stop=True)
                        m.then_inc(up_done, 1)
                    if 0 <= s - 3 < NS:
                        i = s - 3
                        e = expert.pop(i)
                        pe.wait_ge(silu_done, NS * l + (i + 1))
                        if i >= 2:
                            pe.wait_ge(down_read, NS * l + (i - 1))
                        for k in range(KF):
                            m = pe.matmul(sq[i % 2][:, 0:C], hT[:, i % 3, tok(k)],
                                          w2[:, bass.ds(e * FF + k * C, C)], start=(k == 0), stop=(k == KF - 1))
                        m.then_inc(down_done, 1)
                pe.wait_ge(down_read, NS * (l + 1))
                if l == 0:
                    pe.wait_ge(pads_zeroed, 1)
                for q in range(4):
                    fill_quarter(attn_pe, pe, l, q)
                    if l + 1 < LAYERS:
                        turn_rows(l + 1, q)
                        if q > 0:
                            logits(l + 1, q - 1)
                if l + 1 < LAYERS:
                    logits(l + 1, 3)
            pe.wait_ge(w_in, 16 * 12)
            pe.wait_ge(pads_zeroed, 2)
            attn_pe(pe, None, None, 0, 1, 0, -GL, (NSTEP, NSTEP))
            bodies(pe, attn_pe, *L0)
            pe.wait_ge(y_done, 4 * GL)
            dense(pe, "yT0", turn_tiles(pe, lambda t: y[:, t, GL:2 * GL, :].rearrange("p g c -> p (g c)")))
            pe.wait_ge(freed["yT0"], 4)
            dense(pe, "proj0", times4(pe, w_proj[:, :]), "yT0")
            pe.wait_ge(xn_ready, 1)
            dense(pe, "xT1", turn_tiles(pe, lambda t: xn[:, t, :]), "proj0")
            pe.wait_ge(freed["xT1"], 4)
            dense(pe, "mqa", times(pe, w_mqa[:, :], C + 2 * D), "xT1")
            pe.wait_ge(freed["mqa"], NT)
            other_attention.update({"hT1": turn_tiles(pe, lambda t: y[:, t, GL:2 * GL, :].rearrange("p g c -> p (g c)")),
                                    "qkv1": times(pe, w_qkv1[:, :], 3 * C)})
            attn_pe(pe, None, None, GL, GL + 1, 0, GL)
            project["yTa"] = turn_tiles(pe, lambda t: y[:, t, 0:GL, :].rearrange("p g c -> p (g c)"))
            project["proja"] = times4(pe, w_mproj[:, :], ya_T)
            bodies(pe, attn_pe, *L1, peel=PEEL1)
            other_y = turn_tiles(pe, lambda t: y[:, t, GL:2 * GL, :].rearrange("p g c -> p (g c)"))

            def turn_chunk(n, bank):
                pe.wait_ge(y_done, 4 * (3 * GL - 1) + n + 1)
                return other_y(n, bank)
            dense(pe, "yTb", turn_chunk)

            def project_chunk(n, bank):
                pe.wait_ge(freed["yTb"], n + 1)
                return times4(pe, w_o[:, :])(n, bank)
            dense(pe, "projb", project_chunk, None)

            def turn_normed(n, bank):
                pe.wait_ge(xn_ready, 3 + n)
                return turn_tiles(pe, lambda t: scratch[:, tok(t)])(n, bank)
            dense(pe, "xfT", turn_normed, "projb")
            pe.wait_ge(freed["xfT"], 4)

            moe_pe(pe)

        def attn_act(act, gp, ga, gb, gt, par, slot0, part_=None):
            pb = nxt(ga, par, gb) if gb is not None else None

            def read_turn(g, gpar, c, kind):
                n = 8 * g + 2 * c + (kind == "Q")
                act.wait_ge(turned, n + 1)
                view = misc[:, :].bitcast(BF16).rearrange("p (a t) -> p a t", a=2)
                if kind == "K":
                    need(act, k_loaded[(c - 2) % NCH], 32 * (g + 1) if c >= 2 else 32 * g)
                    act.activation(kst[c % 2], view, ACT.Copy).then_inc(turn_read, 1)
                else:
                    act.activation(qT[gpar][:, :, 512 * c:512 * c + 512], view, ACT.Copy).then_inc(turn_read, 1)

            def read_max(g, c):
                act.wait_ge(mT_done, 4 * g + c + 1)
                need(act, m_loaded[(c - 2) % NCH], 64 * (g + 1) if c >= 2 else 64 * g)
                act.activation(mT[c % 2][0:2 * HG, :], misc[0:2 * HG, :].bitcast(BF16)[:, 0:512], ACT.Copy)\
                   .then_inc(mT_read, 1)

            def read_out(g, c):
                act.wait_ge(pv_done, NSTEP * g + (CHUNK_END[c] + 1))
                need(act, oT_done, 4 * g + (c - 1))
                act.activation(oT[c % 2], oacc[:, :], ACT.Copy).then_inc(o_read, 1)

            def exp(g, s):
                c, j = STEPS[s]
                off = 128 * max(0, j - 4 * c)
                for a_ in range(2):
                    act.wait_ge(st_done, 2 * NSTEP * g + (2 * s + a_ + 1))
                    need(act, pv_done, NSTEP * g + (s - 1))
                    act.activation(probs[s % 2][a_][:, :, off:512], st[a_][:, :, off:512], ACT.Exp)\
                       .then_inc(exp_done, 1)

            if gb is None and ga is None:
                read_out(gp, NCH - 1)
                return
            lo, hi = part_ or (0, NSTEP)
            if ga is None and lo == 0:
                read_turn(gb, pb, 0, "K")
                read_turn(gb, pb, 0, "Q")
            if ga is None and gb == GL:
                act.wait_ge(var_ready, 3)
                act.activation(rstd[:, :], mv[:, :, 1], ACT.Sqrt).then_inc(sd_ready, 1)
            late = int(ga is not None)
            for s in range(lo, hi + late):
                if ga is not None and s < NSTEP:
                    exp(ga, s)
                u = s - late
                if gp is not None and s == 0:
                    read_out(gp, NCH - 1)
                if gb is not None and u in TURN_AT:
                    read_turn(gb, pb, *TURN_AT[u])
                if gb is not None and u in MAX_AT:
                    read_max(gb, MAX_AT[u])
                if ga is not None and u == MAX_LAST_AT:
                    read_max(ga, NCH - 1)
                if ga is not None and u in CHUNK_END[:-1]:
                    read_out(ga, CHUNK_END.index(u))
                if gt is not None and u in TURN_NEXT_AT:
                    read_turn(gt, 1 - pb, *TURN_NEXT_AT[u])
                if ga is None and gb == GL and u in UNIT_AT:
                    name, n = UNIT_AT[u]
                    act.wait_ge(done[name], n + 1)
                    o, i = (to_xT if name == "hT1" else kqv_out)(n, banks[n % 4])
                    act.activation(o, i, ACT.Copy).then_inc(freed[name], 1)
                if isinstance(ga, int) and ga in (GL, GL + 1) and u == NORM_AT:
                    act.wait_ge(norm_sq, ga - GL + 3)
                    act.activation(ss[:, :, :], ss[:, :, :], ACT.Sqrt).then_inc(norm_sd, 1)
            if ga is None and part_ == (NSTEP, NSTEP):
                read_turn(gt, 1 - pb, 0, "K")
                read_turn(gt, 1 - pb, 0, "Q")

        def copy_dense(act, name, dst):
            for n in range(DENSE[name]):
                act.wait_ge(done[name], n + 1)
                o, i = dst(n, banks[n % 4])
                act.activation(o, i, ACT.Copy).then_inc(freed[name], 1)

        def kqv_out(n, bank):
            return (kqv[:, GL:2 * GL, :, n, :].rearrange("p g i c -> p i g c"),
                    bank[:, 0:3 * C].rearrange("p (i g c) -> p i g c", i=3, g=GL))

        def to_xT(n, bank):
            return xT[:, 512 * n:512 * n + 512], bank

        @block.scalar
        def _(act):
            act.wait_ge(var_ready, 1)
            act.activation(rstd[:, :], mv[:, :, 1], ACT.Sqrt).then_inc(sd_ready, 1)
            copy_dense(act, "xT0", to_xT)

            for l in range(LAYERS):
                act.wait_ge(dif_ready, l + 1)
                act.activation(rt[:, 1, :], rt[:, 0, :], ACT.Exp).then_inc(exp_ready, 1)
                if l == 0:
                    copy_dense(act, "kqv0", kqv_out)
                if l < 2:
                    act.wait_ge(norm_sq, l + 1)
                    act.activation(ss[:, :, :], ss[:, :, :], ACT.Sqrt).then_inc(norm_sd, 1)
                fill(attn_act, act, l, "scatter")
                for s in range(NS + 2):
                    if s < NS:
                        act.wait_ge(up_done, NS * l + (s + 1))
                        if s >= 3:
                            act.wait_ge(down_done, NS * l + (s - 2))
                        act.activation(hT[:, s % 3, :], banks[2 + s % 2], ACT.Silu).then_inc(silu_done, 1)
                    if s >= 2:
                        i = s - 2
                        act.wait_ge(down_done, NS * l + (i + 1))
                        if i >= 2 * QUAD and i % QUAD == 0:
                            act.wait_ge(ys_stored[i // QUAD % 2], 16 * (moves(l, i // QUAD) - 1))
                        act.activation(yo[:, i % 8, :], sq[i % 2][:, 0:C], ACT.Copy).then_inc(down_read, 1)
                for q in range(4):
                    fill_quarter(attn_act, act, l, q)
                    if l + 1 < LAYERS:
                        act.wait_ge(curT_done, 4 * l + q + 1)
                        act.activation(xT[:, 512 * q:512 * q + 512], banks[q], ACT.Copy).then_inc(curT_read, 1)
            attn_act(act, None, None, 0, 1, 0, -GL, (NSTEP, NSTEP))
            bodies(act, attn_act, *L0)
            copy_dense(act, "yT0", to_xT)
            act.wait_ge(var_ready, 2)
            act.activation(rstd[:, :], mv[:, :, 1], ACT.Sqrt).then_inc(sd_ready, 1)
            copy_dense(act, "xT1", to_xT)
            copy_dense(act, "mqa", lambda n, bank: (mqa_rows[:, n, :], bank[:, 0:C + 2 * D]))
            act.wait_ge(freed["mqa"], NT)
            for i, g in [(2, 0)] + [(i, g) for g in range(1, GL) for i in range(3)]:
                to, rows = mqa_part(i, g)
                act.activation(to, rows, ACT.Copy, scale=D ** -0.5 if i == 1 else 1.0).then_inc(mqa_spread, 1)
            attn_act(act, None, None, GL, GL + 1, 0, GL)
            bodies(act, attn_act, *L1, peel=PEEL1)
            copy_dense(act, "yTb", to_xT)
            act.wait_ge(var_ready, 4)
            act.activation(rstd[:, :], mv[:, :, 1], ACT.Sqrt).then_inc(sd_ready, 1)
            copy_dense(act, "xfT", to_xT)
            for c in range(NCH):
                for u, (b, ko, ki, src, dst, f) in enumerate(MOE_UNITS):
                    n = NU * c + u
                    if (c, u) == (0, 6):
                        act.wait_ge(gate_dif, 1)
                        act.activation(rt[:, 1, 0:NT * E1], rt[:, 0, 0:NT * E1], ACT.Exp).then_inc(gate_exp, 1)
                    if f == "times":
                        continue
                    act.wait_ge(moe_done, n + 1)
                    need(act, moe_read, n)
                    if u == 0:
                        need(act, mix_done, 4 * (c - 1))
                    act.activation(hidden[6 * (c % 2) + dst][:, ko, :], banks[n % 4],
                                   ACT.Silu if f == "silu" else ACT.Gelu).then_inc(moe_read, 1)

        def attn_dve(dve, gp, ga, gb, gt, par, slot0, steps, part_=None):
            def finish_max(g, c):
                dve.wait_ge(max_done, HG * NSTEP * g + HG * (CHUNK_END[c] + 1))
                need(dve, mT_done, 4 * g + (c - 1))
                steps(dve.tensor_reduce(negm[:, c % 2, :, :], mpart[:, c % 2, :, :, 0:c + 1], AX.X, ALU.max,
                                        negate=True))
                steps.sync()
                steps(dve.tensor_copy(mtok[:, c % 2, :, :, 0], negm[:, c % 2, :, :]))
                steps.sync()
                dve.tensor_tensor(mtok[:, c % 2, :, :, 1], negm[:, c % 2, :, :], mtok[:, c % 2, :, :, 0],
                                  ALU.subtract).then_inc(negm_ready, 1)

            def finish_out(g, c):
                dve.wait_ge(oT_done, 4 * g + c + 1)
                need(dve, y_done, 4 * g + (c - 1))
                view = misc[:, :].rearrange("p (t h d) -> p t h d", t=4, d=32)
                steps(dve.reciprocal(rec[:, c % 2, :, :], view[:, :, :, D]))
                steps.sync()
                slot_ = g - slot0
                if isinstance(slot_, int):
                    o = y[:, 4 * c:4 * c + 4, slot_, :].rearrange("p t (h d) -> p t h d", d=D)
                else:
                    o = y[:, 4 * c:4 * c + 4, bass.ds(slot_, 1), :].rearrange("p t a (h d) -> p t (a h) d", d=D)
                dve.tensor_tensor(o, view[:, :, :, 0:D],
                                  rec[:, c % 2, :, :].unsqueeze(3).to_broadcast([P, 4, HG, D]), ALU.mult)\
                    .then_inc(y_done, 1)

            if gb is None and ga is None:
                finish_out(gp, NCH - 1)
                return
            for s in range(*(part_ or (0, NSTEP))):
                if gb is not None:
                    t, kc = COMBOS[s]
                    n = min(512, (t + 1) * P - 512 * kc)
                    if s in CHUNK_START:
                        need(dve, negm_ready, 4 * gb + (t // 4 - 1))
                    for h in range(HG):
                        dve.wait_ge(sq_done, HG * NSTEP * gb + (HG * s + h + 1))
                        m = mpart[:, (t // 4) % 2, t % 4, h, kc:kc + 1]
                        if kc == t // 4:
                            dve.tensor_tensor_reduce(masked[:, h % 2, 0:n], sq[h % 2][:, 0:n],
                                                     mask_row[:, 512 - n:512], 1.0, -3.0e38, ALU.add, ALU.max,
                                                     accum_out=m).then_inc(max_done, 1)
                        else:
                            dve.tensor_reduce(m, sq[h % 2][:, 0:n], AX.X, ALU.max).then_inc(max_done, 1)
                    if s in CHUNK_END:
                        finish_max(gb, CHUNK_END.index(s))
                if isinstance(ga, int) and ga in (GL, GL + 1) and s == NORM_AT + 2:
                    dve.wait_ge(norm_sd, ga - GL + 3)
                    dve.reciprocal(ss[:, :, :], ss[:, :, :]).then_inc(norm_recip, 1)
                if ga == 3 * GL - 1 and s - 1 in PROJECT_AT:
                    name, n = PROJECT_AT[s - 1]
                    dve.wait_ge(done[name], n + 1)
                    if name == "yTa":
                        dve.tensor_copy(ya_T[:, 512 * n:512 * n + 512], sq[n % 2][:, :]).then_inc(freed[name], 1)
                    else:
                        rows = x[:, 4 * n:4 * n + 4, :]
                        dve.tensor_tensor(rows, rows, sq[n % 2][:, :].rearrange("p (t c) -> p t c", t=4), ALU.add)\
                            .then_inc(freed[name], 1)
                if ga is not None and s - 1 in OUT_AT:
                    finish_out(ga, OUT_AT[s - 1])
                if gp is not None and s - 1 == OUT_LAST_AT:
                    finish_out(gp, NCH - 1)

        def bc(ap, shape, axis):
            return ap.unsqueeze(axis).to_broadcast(shape)

        def add_banks(dve, name, where):
            for n in range(DENSE[name]):
                dve.wait_ge(done[name], n + 1)
                o, i0, i1 = where(n, banks[n % 4])
                dve.tensor_tensor(o, i0, i1, ALU.add).then_inc(freed[name], 1)

        @block.vector
        def _(dve):
            steps = Steps(dve, dve_step)
            big3 = [P, NT, C]

            def layer_norm(n, eps, dst, event, count):
                for t in range(NT):
                    steps(dve.bn_stats(stats[:, t, :], x[:, t, :]))
                steps.sync()
                for t in range(NT):
                    steps(dve.bn_aggr(mv[:, t, :], stats[:, t, :]))
                steps.sync()
                steps(dve.tensor_scalar(mv[:, :, 1], mv[:, :, 1], eps, None, ALU.add))
                steps.sync()
                dve.nop().then_inc(var_ready, 1)
                dve.wait_ge(sd_ready, n)
                steps(dve.reciprocal(rstd[:, :], rstd[:, :]))
                steps.sync()
                for t in range(NT):
                    i = dve.tensor_scalar(dst[:, t, :], x[:, t, :], mv[:, t, 0:1], rstd[:, t:t + 1],
                                          ALU.subtract, ALU.mult)
                    if event is not None:
                        i.then_inc(event, 1)
                    else:
                        steps(i)

            def rms_rows(src, n, w, half, other):
                steps.sync()
                steps(dve.tensor_tensor(other, src, src, ALU.mult))
                steps.sync()
                steps(dve.tensor_reduce(mv[:, :, 1], other, AX.X, ALU.add))
                steps.sync()
                steps(dve.tensor_scalar(mv[:, :, 1], mv[:, :, 1], 1.0 / C, 1.1920929e-07, ALU.mult, ALU.add))
                steps.sync()
                dve.nop().then_inc(var_ready, 1)
                dve.wait_ge(sd_ready, n)
                steps(dve.reciprocal(rstd[:, :], rstd[:, :]))
                steps.sync()
                steps(dve.tensor_tensor(other, src, bc(rstd[:, :], big3, 2), ALU.mult))
                steps.sync()
                steps(dve.tensor_tensor(half, other, bc(w, big3, 1), ALU.mult))
                steps.sync()

            halves = (scratch[:, 0:T], scratch[:, T:2 * T])

            def rotate_heads(i, g):
                v = group(i, GL + g)
                t1, t2 = (t[:, 512 * g:512 * g + 512].rearrange("p (t h d) -> p t h d", h=HG, d=D) for t in halves)
                hd = D // 2
                half = [P, NT, HG, hd]
                steps(dve.tensor_tensor(t1[:, :, :, 0:hd], v[:, :, :, hd:D], bc(sin[:, :, 0:hd], half, 2), ALU.mult))
                steps(dve.tensor_tensor(t1[:, :, :, hd:D], v[:, :, :, 0:hd], bc(sin[:, :, hd:D], half, 2), ALU.mult))
                steps(dve.tensor_tensor(t2, v, bc(cos, [P, NT, HG, D], 2), ALU.mult))
                steps.sync()
                steps(dve.tensor_tensor(v, t1, t2, ALU.add))

            def head_norm(i, w, n, out_eps, scale):
                flat = lambda ap: ap.rearrange("p (g n d) -> p g n d", g=GL, d=D)
                t1, t2 = halves
                shape = [P, GL, NT * HG, D]
                v = kqv[:, GL:2 * GL, i, :, :].rearrange("p g t (h d) -> p g (t h) d", d=D)
                norms = ss[:, :, :].rearrange("p t h -> p (t h)")
                steps.sync()
                steps(dve.tensor_tensor(flat(t1), v, v, ALU.mult))
                steps.sync()
                steps(dve.tensor_reduce(norms, t1.rearrange("p (n d) -> p n d", d=D), AX.X, ALU.add))
                steps.sync()
                steps(dve.tensor_scalar(norms, norms, 1.0 / D, None, ALU.mult))
                steps.sync()
                dve.nop().then_inc(norm_sq, 1)
                dve.wait_ge(norm_sd, n)
                steps(dve.tensor_scalar(norms, norms, out_eps, None, ALU.add))
                steps.sync()
                steps(dve.reciprocal(norms, norms))
                if scale != 1.0:
                    steps(dve.tensor_scalar(w, w, scale, None, ALU.mult))
                steps.sync()
                steps(dve.tensor_tensor(flat(t2), v, bc(norms.rearrange("p (g n) -> p g n", g=GL), shape, 3), ALU.mult))
                steps.sync()
                steps(dve.tensor_tensor(v, flat(t2), w.unsqueeze(1).unsqueeze(1).to_broadcast(shape), ALU.mult))
                steps.sync()

            dve.wait_ge(x_in, 16)
            layer_norm(1, 1e-05, xn, cur_ready, 0)
            dve.wait_ge(consts_in, 16)
            dve.tensor_copy(bcon[:, :], consts[:, 0:5 * 128]).then_inc(consts_cast, 1)
            steps(dve.memset(mask_row[:, 0:384], 0.0))
            steps(dve.tensor_copy(mask_row[:, 384:512], con["mask_qk"]))

            ATT_STEPS = 2 * NCH * 3

            def emit(eng, gp, ga, gb, gt, par, slot0, part_=None):
                attn_dve(eng, gp, ga, gb, gt, par, slot0, steps, part_)

            shape = [P, NT, E0]
            v3 = lambda i: rt[:, i, :].rearrange("p (t e) -> p t e", e=E0)
            iota_b = con["iota"].unsqueeze(1).to_broadcast(shape)
            for l in range(LAYERS):
                steps.sync()
                count, rank = (sq[0], sq[1]) if l == 0 else (banks[0], banks[1])
                dve.wait_ge(logits_done, l + 1)
                lg = oacc[:, 0:NT * E0].rearrange("p (t e) -> p t e", e=E0)
                steps(dve.tensor_reduce(small[:, 0, :], lg, AX.X, ALU.max))
                steps.sync()
                dve.tensor_tensor(v3(0), lg, bc(small[:, 0, :], shape, 2), ALU.subtract).then_inc(dif_ready, 1)
                dve.wait_ge(dif_ready, l + 1)
                steps(dve.tensor_scalar(rt[:, 2, :], rt[:, 0, :], 0.0, 64.0, ALU.is_lt, ALU.mult))
                steps.sync()
                steps(dve.tensor_tensor(v3(3), v3(2), iota_b, ALU.add))
                steps.sync()
                steps(dve.tensor_reduce(small[:, 1, :], v3(3), AX.X, ALU.min))
                steps.sync()
                dve.tensor_tensor(ohb[:, :, :], iota_b, bc(small[:, 1, :], shape, 2), ALU.is_equal)\
                    .then_inc(onehot_ready, 1)
                dve.wait_ge(count_done, l + 1)
                steps(dve.tensor_scalar(cnt_i[:, 0, :], count[:, 0:E0], 127.0, None, ALU.add))
                steps.sync()
                steps(dve.tensor_scalar(cnt_i[:, 1, :], cnt_i[:, 0, :], 7, None, ALU.arith_shift_right))
                steps.sync()
                steps(dve.tensor_copy(ntile[:, 0, :], cnt_i[:, 1, :]))
                steps.sync()
                steps(dve.tensor_tensor(v3(2), upto, ntile[:, 0, :].unsqueeze(1).to_broadcast([P, E0, E0]), ALU.mult))
                steps.sync()
                steps(dve.tensor_reduce(ntile[:, 1, :], v3(2), AX.X, ALU.add))
                steps.sync()
                own = rt[:, 3:5, :].rearrange("p a e -> p (a e)")[:, 0:NS * E0].rearrange("p (s e) -> p s e", e=E0)
                steps(dve.tensor_tensor(own, con["tiles"].unsqueeze(2).to_broadcast([P, NS, E0]),
                                        ntile[:, 1, :].unsqueeze(1).to_broadcast([P, NS, E0]), ALU.is_ge))
                steps(dve.tensor_tensor(ntile[:, 2, :], ntile[:, 1, :], ntile[:, 0, :], ALU.subtract))
                steps.sync()
                steps(dve.tensor_reduce(owner_f[:, :], own, AX.X, ALU.add))
                steps(dve.tensor_scalar(ntile[:, 2, :], ntile[:, 2, :], 128.0, None, ALU.mult))
                steps.sync()
                dve.tensor_scalar(owner[:, :], owner_f[:, :], float(E0 - 1), None, ALU.min)\
                    .then_inc(owner_ready, 1)
                dve.wait_ge(rank_done, l + 1)
                steps(dve.tensor_tensor(v3(5), rank[:, 0:NT * E0].rearrange("p (t e) -> p t e", e=E0),
                                        ntile[:, 2, :].unsqueeze(1).to_broadcast(shape), ALU.add))
                steps.sync()
                steps(dve.tensor_tensor(v3(2), v3(5), ohb[:, :, :], ALU.mult))
                steps.sync()
                steps(dve.tensor_reduce(small[:, 3, :], v3(2), AX.X, ALU.add))
                steps.sync()
                dve.tensor_copy(slot[:, :], small[:, 3, :]).then_inc(slot_ready, 1)
                dve.wait_ge(exp_ready, l + 1)
                steps(dve.tensor_reduce(small[:, 2, :], v3(1), AX.X, ALU.add))
                steps.sync()
                steps(dve.reciprocal(wtop[:, :], small[:, 2, :]))
                if l == 0:
                    dve.wait_ge(freed["kqv0"], NT)
                    dve.wait_ge(w_in, 16 * 12)
                    for g in range(GL):
                        rotate_heads(1, g)
                    head_norm(1, hnorm[:, 0, :], 1, 1e-06, D ** -0.5)
                if l == 1:
                    head_norm(0, hnorm[:, 1, :], 2, 1e-06, 1.0)
                if l < 2:
                    dve.nop().then_inc(kqv_ready, 1)
                fill(emit, dve, l, "scatter")
                for s in range(NS):
                    e = dve.value_load(owner[0:1, s:s + 1], min_val=0, max_val=E0 - 1)
                    if l == 0 and s == 0:
                        dve.wait_ge(experts_in, 16 * 8)
                    if s >= 2:
                        dve.wait_ge(up_done, NS * l + (s - 1))
                    dve.tensor_copy(w1s[:, s % 2, :], w1[:, bass.ds(e * FF, FF)]).then_inc(w1_picked, 1)
                    dve.wait_ge(xsT_done, NS * l + (s + 1))
                    dve.tensor_copy(xsT[:, s % 2, :], banks[s % 2][:, 0:P]).then_inc(xsT_read, 1)
                    if l < 2 and s in (6, 12, 18):
                        pack_part(dve, steps, GL, "QK"[l], s // 6 - 1)
                if l == 1:
                    steps.sync()
                    dve.nop().then_inc(qk_packed, 1)
                if l == 0:
                    dve.wait_ge(down_done, NS)
                for q in range(4):
                    fill_quarter(emit, dve, l, q)
                    if l == 0:
                        rotate_heads(0, q)
                    dve.wait_ge(gathered[q], 64 * (l + 1))
                    for t in range(4 * q, 4 * q + 4):
                        dve.tensor_scalar(xn[:, t, :], xn[:, t, :], wtop[:, t:t + 1], None, ALU.mult)\
                            .then_inc(cur_ready, 1)
            dve.wait_ge(cur_ready, NT * (LAYERS + 1))
            dve.wait_ge(down_done, NS * LAYERS)
            for par in range(2):
                steps(dve.memset(vpad[par][:, :, :, D + 1:32], 0.0))
                dve.memset(vpad[par][:, :, :, D:D + 1], 1.0).then_inc(vpad_set, 1)
            steps(dve.tensor_tensor(x[:, :, :], x[:, :, :], xn[:, :, :], ALU.add))
            steps.sync()
            dve.nop().then_inc(vpad_set, 1)
            bodies(dve, emit, *L0, steps, ATT_STEPS)
            steps.sync()
            add_banks(dve, "proj0", lambda n, bank: (x[:, 4 * n:4 * n + 4, :], x[:, 4 * n:4 * n + 4, :],
                                                     bank.rearrange("p (t c) -> p t c", t=4)))
            dve.wait_ge(freed["proj0"], NCH)
            layer_norm(2, 1e-05, xn, None, 0)
            steps.sync()
            dve.nop().then_inc(xn_ready, 1)
            dve.wait_ge(freed["mqa"], NT)
            for i in range(2):
                to, rows = mqa_part(i, 0)
                steps(dve.tensor_scalar(to, rows, D ** -0.5 if i == 1 else 1.0, None, ALU.mult))
            steps.sync()
            for which in ("K", "Q"):
                pack(dve, steps, GL, 0, which)
                steps.sync()
            dve.nop().then_inc(qk_packed, 1)
            rms_rows(xn[:, :, :], 3, cnorm[:, 0, :], y[:, :, GL:2 * GL, :].rearrange("p t g c -> p t (g c)"),
                     y[:, :, 0:GL, :].rearrange("p t g c -> p t (g c)"))
            dve.nop().then_inc(xn_ready, 1)
            emit(dve, None, None, GL, GL + 1, 0, GL)
            bodies(dve, emit, *L1, steps, ATT_STEPS, peel=PEEL1)
            steps.sync()
            half, other = (scratch[:, T * i:T * i + T].rearrange("p (t c) -> p t c", c=C) for i in range(2))
            dve.wait_ge(done["yTb"], NCH)
            for n in range(NCH):
                rows = slice(4 * n, 4 * n + 4)
                dve.wait_ge(done["projb"], n + 1)
                dve.tensor_tensor(xn[:, rows, Mz:C], xn[:, rows, Mz:C],
                                  banks[n].rearrange("p (t c) -> p t c", t=4)[:, :, Mz:C], ALU.add)\
                    .then_inc(freed["projb"], 1)
                dve.wait_ge(freed["projb"], n + 1)
                steps(dve.tensor_tensor(other[:, rows, :], xn[:, rows, :], xn[:, rows, :], ALU.mult))
                steps.sync()
                steps(dve.tensor_reduce(mv[:, rows, 1], other[:, rows, :], AX.X, ALU.add))
            steps.sync()
            steps(dve.tensor_scalar(mv[:, :, 1], mv[:, :, 1], 1.0 / C, 1.1920929e-07, ALU.mult, ALU.add))
            steps.sync()
            dve.nop().then_inc(var_ready, 1)
            dve.wait_ge(sd_ready, 4)
            steps(dve.reciprocal(rstd[:, :], rstd[:, :]))
            steps.sync()
            for n in range(NCH):
                rows = slice(4 * n, 4 * n + 4)
                steps(dve.tensor_tensor(other[:, rows, :], xn[:, rows, :], bc(rstd[:, rows], [P, 4, C], 2), ALU.mult))
                steps.sync()
                dve.tensor_tensor(half[:, rows, :], other[:, rows, :], bc(cnorm[:, 1, :], [P, 4, C], 1), ALU.mult)\
                    .then_inc(xn_ready, 1)
            dve.wait_ge(freed["proja"], NCH)
            steps(dve.tensor_tensor(x[:, :, :], x[:, :, :], xn[:, :, :], ALU.add))

            def times_units(c):
                for u, (b, ko, ki, src, dst, f) in enumerate(MOE_UNITS):
                    if f != "times":
                        continue
                    n = NU * c + u
                    dve.wait_ge(moe_done, n + 1)
                    need(dve, moe_read, n)
                    silu = hidden[6 * (c % 2) + 1][:, ko, :]
                    dve.tensor_tensor(silu, silu, banks[n % 4], ALU.mult)\
                        .then_inc(moe_read, 1)
            times_units(0)
            dve.wait_ge(done["gate"], 1)
            sh = [P, NT, E1]
            r4 = lambda i: rt[:, i, 0:NT * E1].rearrange("p (t e) -> p t e", e=E1)
            g4 = oacc[:, 0:NT * E1].rearrange("p (t e) -> p t e", e=E1)
            io = con["iota"][:, 0:E1].unsqueeze(1).to_broadcast(sh)
            big_f = 3.4028235e38
            steps(dve.tensor_scalar(r4(5), g4, -big_f, big_f, ALU.max, ALU.min))
            steps.sync()
            steps(dve.tensor_reduce(small[:, 0, :], r4(5), AX.X, ALU.max))
            steps.sync()
            dve.tensor_tensor(r4(0), r4(5), bc(small[:, 0, :], sh, 2), ALU.subtract).then_inc(gate_dif, 1)
            dve.wait_ge(gate_exp, 1)
            steps(dve.tensor_reduce(small[:, 1, :], r4(1), AX.X, ALU.add))
            steps.sync()
            steps(dve.reciprocal(small[:, 2, :], small[:, 1, :]))
            steps.sync()
            steps(dve.tensor_tensor(r4(0), r4(1), bc(small[:, 2, :], sh, 2), ALU.mult))
            steps.sync()

            def top(src, dst):
                steps(dve.tensor_reduce(small[:, 0, :], src, AX.X, ALU.max))
                steps.sync()
                steps(dve.tensor_tensor(r4(2), src, bc(small[:, 0, :], sh, 2), ALU.is_lt))
                steps.sync()
                steps(dve.scalar_tensor_tensor(out=r4(3), in0=r4(2), scalar=64.0, in1=io, op0=ALU.mult, op1=ALU.add))
                steps.sync()
                steps(dve.tensor_reduce(small[:, 3, :], r4(3), AX.X, ALU.min))
                steps.sync()
                steps(dve.tensor_tensor(dst, io, bc(small[:, 3, :], sh, 2), ALU.is_equal))
                steps.sync()

            top(r4(0), r4(4))
            steps(dve.tensor_copy(small[:, 1, :], small[:, 0, :]))
            steps(dve.scalar_tensor_tensor(out=r4(5), in0=r4(4), scalar=-2.0, in1=r4(0), op0=ALU.mult, op1=ALU.add))
            steps.sync()
            top(r4(5), r4(1))
            steps(dve.tensor_tensor(r4(2), r4(1), r4(4), ALU.add))
            steps(dve.tensor_tensor(small[:, 2, :], small[:, 0, :], small[:, 1, :], ALU.add))
            steps.sync()
            steps(dve.tensor_scalar(small[:, 2, :], small[:, 2, :], 1e-08, None, ALU.add))
            steps.sync()
            steps(dve.reciprocal(small[:, 3, :], small[:, 2, :]))
            steps(dve.tensor_tensor(r4(3), r4(2), r4(0), ALU.mult))
            steps.sync()
            steps(dve.tensor_tensor(r4(4), r4(3), bc(small[:, 3, :], sh, 2), ALU.mult))
            steps.sync()
            wts = r4(4)
            for c in range(NCH):
                if c + 1 < NCH:
                    times_units(c + 1)
                for t in range(4):
                    n = 4 * c + t
                    dve.wait_ge(mix_done, n + 1)
                    for e in range(E1):
                        i = dve.scalar_tensor_tensor(out=x[:, n, Mz:C], in0=sq[n % 2][:, P * e + Mz:P * e + C],
                                                     scalar=wts[:, n, e:e + 1], in1=x[:, n, Mz:C],
                                                     op0=ALU.mult, op1=ALU.add)
                        if e == E1 - 1:
                            i.then_inc(mix_read, 1)
                        else:
                            steps(i)
                            steps.sync()


def constants():
    at, n = const_at()
    c = np.zeros((P, n), np.float32)
    r = np.arange(P)
    put = lambda k, v: c.__setitem__((slice(None), slice(*at[k])), v)
    put("ident", np.eye(P))
    put("mask_kq", np.where(r[:, None] > r[None, :], MASKED, 0.0))
    put("mask_qk", np.where(r[None, :] > r[:, None], MASKED, 0.0))
    put("before", (r[:, None] < r[None, :]))
    put("ones", 1.0)
    inv = (np.float32(1.0) / np.float32(10000.0) ** (np.arange(0, D, 2, dtype=np.float32) / np.float32(D)))
    freq = np.arange(T, dtype=np.float32)[:, None] * inv.astype(np.float32)[None, :]
    freq = np.concatenate([freq, freq], 1).astype(np.float64)
    sign = np.where(np.arange(D) < D // 2, -1.0, 1.0)
    tiled = lambda v: v.reshape(NT, P, D).transpose(1, 0, 2).reshape(P, NT * D)
    put("cos", tiled(np.cos(freq)))
    put("sin", tiled(np.sin(freq) * sign))
    e = np.arange(E0)
    put("upto", np.broadcast_to((e[None, :] <= e[:, None]).reshape(1, -1), (P, E0 * E0)))
    put("iota", np.broadcast_to(e, (P, E0)))
    put("tiles", np.broadcast_to(np.arange(NS), (P, NS)))
    return c


def lay_out(i):
    T_ = lambda w: np.ascontiguousarray(np.asarray(w).T)

    def blocks(w):
        w = T_(w)
        return [w[P * k:P * k + P, P * o:P * o + P] for k in range(w.shape[0] // P) for o in range(w.shape[1] // P)]

    f = {k: np.asarray(v) for k, v in i.items()}
    row = lambda n: f[n].reshape(1, -1)
    moe = []
    for n in ("e0_up", "e0_down", "e1_w1", "e1_w2", "e1_down", "e2_l1", "e2_l2", "e2_l3", "e2_l4",
              "e3_down", "e3_up", "e3_out"):
        moe += blocks(f["L1_ffn_" + n])
    return {
        "x": np.ascontiguousarray(f["L0_attn_x"].reshape(NT, P, C).transpose(1, 0, 2)),
        "consts": constants(),
        "w_kqv": T_(f["L0_attn_W_kqv"]), "w_proj": T_(f["L0_attn_W_proj"]),
        "w_mqa": np.ascontiguousarray(f["L1_attn_w_attn"]), "w_mproj": np.ascontiguousarray(f["L1_attn_w_proj"]),
        "w_qkv1": np.concatenate([T_(f["L1_ffn_wk"]), T_(f["L1_ffn_wq"]), T_(f["L1_ffn_wv"])], 1),
        "w_o": T_(f["L1_ffn_wo"]), "w_gate": T_(f["L1_ffn_gate_w"]),
        "routers": np.ascontiguousarray(f["L0_ffn_routers"].transpose(1, 0, 2).reshape(C, LAYERS * E0)),
        "hq0": row("L0_attn_q_norm_w"), "hk0": row("L0_attn_k_norm_w"),
        "hq1": row("L1_ffn_qn_w"), "hk1": row("L1_ffn_kn_w"),
        "n1": row("L1_ffn_n1_w"), "n2": row("L1_ffn_n2_w"),
        "w1": np.ascontiguousarray(f["L0_ffn_W1"].transpose(1, 0, 2).reshape(C, E0 * FF)),
        "w2": np.ascontiguousarray(f["L0_ffn_W2"].reshape(E0, KF, P, C).transpose(2, 0, 1, 3).reshape(P, E0 * FF)),
        "moe_w": np.ascontiguousarray(np.concatenate(moe, 1)),
    }


def kernel(**inputs):
    import concourse.bacc as bacc
    from concourse.bass_utils import run_bass_kernel_spmd

    arrays = lay_out(inputs)
    nc = bacc.Bacc("TRN2", target_bir_lowering=False, num_devices=1)
    args = {n: nc.dram_tensor(f"in_{n}", v.shape, mybir.dt.from_np(v.dtype), kind="ExternalInput").ap()
            for n, v in arrays.items()}
    out = nc.dram_tensor("out_0", (P, NT, C), F32, kind="ExternalOutput").ap()
    build(nc, args, out)
    r = run_bass_kernel_spmd(nc, [{f"in_{n}": v for n, v in arrays.items()}], core_ids=[0])
    got = np.asarray(r.results[0]["out_0"])
    return np.ascontiguousarray(got.transpose(1, 0, 2)).reshape(1, T, C)
```
